# Optimizing a Trainium2 kernel written in Bass

```python
import numpy as np
import jax
import jax.numpy as jnp

def _softmax(x, axis=-1):
    return jax.nn.softmax(x, axis=axis)

def _gelu(x):
    return jax.nn.gelu(x, approximate=True)

def _silu(x):
    return jax.nn.silu(x)

def _sigmoid(x):
    return jax.nn.sigmoid(x)

def _layernorm(x, axis=-1, eps=1e-05):
    m = jnp.mean(x, axis=axis, keepdims=True)
    v = jnp.var(x, axis=axis, keepdims=True)
    return (x - m) / jnp.sqrt(v + eps)

def _scatter_add(tgt, idx, src, axis=0):
    return tgt.at[idx].add(src)

def _segment_sum(src, seg, n):
    return jax.ops.segment_sum(src, seg, n)
kernel_name = 'mk_gnn_resnorm_d4_gnn_r32_8dcec6'

def setup_inputs(seed: int=0):
    np.random.seed(seed)
    _w = jnp.asarray

    def _rec_inputs():
        import jax
        import jax.numpy as jnp
        _gk = jax.random.key(seed)
        x = -0.000202 + 1 * jax.random.normal(jax.random.fold_in(_gk, 1), (3125, 64), jnp.float32)
        _s = jax.random.randint(jax.random.fold_in(_gk, 2), (50000,), 0, 3125, jnp.int32)
        _d = jax.random.randint(jax.random.fold_in(_gk, 3), (50000,), 0, 3125, jnp.int32)
        _loop = jnp.arange(3125, dtype=jnp.int32)
        src = jnp.concatenate([_s, _d, _loop])
        dst = jnp.concatenate([_d, _s, _loop])
        _o = jnp.argsort(dst, stable=True)
        src = src[_o]
        dst = dst[_o]
        return (x, src, dst)
    x, src, dst = _rec_inputs()

    def _L0_gnn_setup():
        import jax, jax.numpy as jnp
        import numpy as np
        N_NODES = 3125
        N_EDGES = 50000
        D = 64
        K = 10
        ALPHA = 0.1
        key = jax.random.key(seed)
        kx, kw, kb, ks, kd = jax.random.split(key, 5)
        x = jax.random.normal(kx, (N_NODES, D), dtype=jnp.float32)
        lim = 1.0 / np.sqrt(D)
        W = jax.random.uniform(kw, (D, D), minval=-lim, maxval=lim, dtype=jnp.float32)
        b = jax.random.uniform(kb, (D,), minval=-lim, maxval=lim, dtype=jnp.float32)
        src = jax.random.randint(ks, (N_EDGES,), 0, N_NODES, dtype=jnp.int32)
        dst = jax.random.randint(kd, (N_EDGES,), 0, N_NODES, dtype=jnp.int32)
        return {'x': x, 'W': W, 'b': b, 'src': src, 'dst': dst}
    _L0_gnn_all = _L0_gnn_setup()
    _L0_gnn_in = {k: v for k, v in _L0_gnn_all.items() if k in ('W', 'b')}
    del _L0_gnn_all

    def _L1_gnn_setup():
        import jax, jax.numpy as jnp
        import numpy as np
        NUM_NODES = 50000
        EMBED_DIM = 64
        NUM_EDGES = 1250000
        NUM_LAYERS = 3
        key = jax.random.key(seed)
        k1, k2 = jax.random.split(key)
        edge_index = jax.random.randint(k1, (2, NUM_EDGES), 0, NUM_NODES, dtype=jnp.int64) if jax.config.read('jax_enable_x64') else jax.random.randint(k1, (2, NUM_EDGES), 0, NUM_NODES, dtype=jnp.int32)
        embedding_weight = jax.random.normal(k2, (NUM_NODES, EMBED_DIM), dtype=jnp.float32)
        return {'edge_index': edge_index, 'embedding_weight': embedding_weight}
    _L1_gnn_all = _L1_gnn_setup()
    _L1_gnn_in = {k: v for k, v in _L1_gnn_all.items() if k in ()}
    del _L1_gnn_all

    def _L2_gnn_setup():
        import jax, jax.numpy as jnp
        import numpy as np
        N_NODES = 3125
        N_EDGES = 31250
        H = 64
        N_LAYERS = 5
        EPS = 1e-05

        def layer_norm(x, g, b):
            m = jnp.mean(x, axis=-1, keepdims=True)
            v = jnp.var(x, axis=-1, keepdims=True)
            return (x - m) * jax.lax.rsqrt(v + EPS) * g + b

        def sage_conv(x, src, dst, n_nodes, wl, bl, wr):
            xj = x[src]
            deg = jax.ops.segment_sum(jnp.ones((src.shape[0], 1), x.dtype), dst, num_segments=n_nodes)
            amax = jax.ops.segment_max(xj, dst, num_segments=n_nodes)
            amax = jnp.where(deg > 0, amax, jnp.zeros_like(amax))
            amean = jax.ops.segment_sum(xj, dst, num_segments=n_nodes) / jnp.maximum(deg, 1.0)
            agg = jnp.concatenate([amax, amean], axis=-1)
            return agg @ wl.T + bl + x @ wr.T
        key = jax.random.key(seed)
        ks = jax.random.split(key, 8)
        x = jax.random.normal(ks[0], (N_NODES, H), dtype=jnp.float32)
        edge_index = jax.random.randint(ks[1], (2, N_EDGES), 0, N_NODES, dtype=jnp.int64)
        s = 0.05
        return {'x': x, 'edge_index': edge_index, 'conv_wl': jax.random.normal(ks[2], (N_LAYERS, H, 2 * H), jnp.float32) * s, 'conv_bl': jnp.zeros((N_LAYERS, H), jnp.float32), 'conv_wr': jax.random.normal(ks[3], (N_LAYERS, H, H), jnp.float32) * s, 'ln_g': jnp.ones((N_LAYERS, H), jnp.float32), 'ln_b': jnp.zeros((N_LAYERS, H), jnp.float32), 'adapter_w': jax.random.normal(ks[4], (H, H), jnp.float32) * s, 'adapter_b': jnp.zeros((H,), jnp.float32), 'mlp_w1': jax.random.normal(ks[5], (4 * H, H), jnp.float32) * s, 'mlp_b1': jnp.zeros((4 * H,), jnp.float32), 'mlp_ln_g': jnp.ones((4 * H,), jnp.float32), 'mlp_ln_b': jnp.zeros((4 * H,), jnp.float32), 'mlp_w2': jax.random.normal(ks[6], (H, 4 * H), jnp.float32) * s, 'mlp_b2': jnp.zeros((H,), jnp.float32)}
    _L2_gnn_all = _L2_gnn_setup()
    _L2_gnn_in = {k: v for k, v in _L2_gnn_all.items() if k in ('conv_wl', 'conv_bl', 'conv_wr', 'ln_g', 'ln_b', 'adapter_w', 'adapter_b', 'mlp_w1', 'mlp_b1', 'mlp_ln_g', 'mlp_ln_b', 'mlp_w2', 'mlp_b2')}
    del _L2_gnn_all

    def _L3_gnn_setup():
        import jax, jax.numpy as jnp
        import numpy as np
        D = 4
        H = 16
        N = 50000
        E = 25000
        TI, TJ = np.tril_indices(D, -1)

        def _householder(params):
            A = jnp.zeros(params.shape[:-1] + (D, D), params.dtype)
            A = A.at[..., TI, TJ].set(params) + jnp.eye(D, dtype=params.dtype)
            Q, R = jnp.linalg.qr(A)
            s = jnp.sign(jnp.diagonal(R, axis1=-2, axis2=-1))
            s = jnp.where(s == 0, jnp.ones_like(s), s)
            return Q * s[..., None, :]

        def _mlp(z, w1, b1, w2, b2):
            h = jax.nn.relu(z @ w1.T + b1)
            return h @ w2.T + b2

        def _forward(x, edge_index, W1, W2, epsilons, mlp1_w, mlp1_b, mlp2_w, mlp2_b):
            n = x.shape[0]
            xr = x.reshape(n, D, H)
            xt = jnp.einsum('ndf,dk->nkf', xr, W1)
            xt = jnp.einsum('ndf,fg->ndg', xt, W2)
            loops = jnp.arange(n)
            row = jnp.concatenate([edge_index[0], loops])
            col = jnp.concatenate([edge_index[1], loops])
            deg = jax.ops.segment_sum(jnp.ones_like(row, x.dtype), row, num_segments=n)
            dis = jnp.where(deg > 0, deg ** (-0.5), jnp.zeros_like(deg))
            xf = xt.reshape(n, D * H)
            xi = xf[col]
            xj = xf[row]
            cat_ve = jnp.concatenate([xi, xj], axis=-1)
            cat_ue = jnp.concatenate([xj, xi], axis=-1)
            Fve = _householder(_mlp(cat_ve, mlp1_w, mlp1_b, mlp2_w, mlp2_b))
            Fue = _householder(_mlp(cat_ue, mlp1_w, mlp1_b, mlp2_w, mlp2_b))
            xjr = xj.reshape(-1, D, H)
            msg = jnp.einsum('eka,ekb,ebh->eah', Fve, Fue, xjr)
            msg = msg * (dis[col] * dis[row])[:, None, None]
            agg = jax.ops.segment_sum(msg.reshape(-1, D * H), col, num_segments=n)
            lap = jax.nn.elu(agg.reshape(n, D, H))
            coeff = (1.0 + jnp.tanh(epsilons))[None, :, None]
            return (coeff * xr - lap).reshape(n, D * H)
        key = jax.random.key(seed)
        ks = jax.random.split(key, 9)
        dh = D * H
        x = jax.random.normal(ks[0], (N, dh), jnp.float32)
        edge_index = jax.random.randint(ks[1], (2, E), 0, N, dtype=jnp.int64)
        W1 = jax.random.normal(ks[2], (D, D), jnp.float32) / np.sqrt(D)
        W2 = jax.random.normal(ks[3], (H, H), jnp.float32) / np.sqrt(H)
        epsilons = jnp.zeros((D,), jnp.float32)
        mlp1_w = jax.random.normal(ks[4], (H, 2 * dh), jnp.float32) / np.sqrt(2 * dh)
        mlp1_b = jnp.zeros((H,), jnp.float32)
        n_params = D * (D - 1) // 2
        mlp2_w = jax.random.normal(ks[5], (n_params, H), jnp.float32) / np.sqrt(H)
        mlp2_b = jnp.zeros((n_params,), jnp.float32)
        return {'x': x, 'edge_index': edge_index, 'W1': W1, 'W2': W2, 'epsilons': epsilons, 'mlp1_w': mlp1_w, 'mlp1_b': mlp1_b, 'mlp2_w': mlp2_w, 'mlp2_b': mlp2_b}
    _L3_gnn_all = _L3_gnn_setup()
    _L3_gnn_in = {k: v for k, v in _L3_gnn_all.items() if k in ('W1', 'W2', 'epsilons', 'mlp1_w', 'mlp1_b', 'mlp2_w', 'mlp2_b')}
    del _L3_gnn_all
    return {'x': x, 'src': src, 'dst': dst, 'L0_gnn_W': _L0_gnn_in['W'], 'L0_gnn_b': _L0_gnn_in['b'], 'L2_gnn_conv_wl': _L2_gnn_in['conv_wl'], 'L2_gnn_conv_bl': _L2_gnn_in['conv_bl'], 'L2_gnn_conv_wr': _L2_gnn_in['conv_wr'], 'L2_gnn_ln_g': _L2_gnn_in['ln_g'], 'L2_gnn_ln_b': _L2_gnn_in['ln_b'], 'L2_gnn_adapter_w': _L2_gnn_in['adapter_w'], 'L2_gnn_adapter_b': _L2_gnn_in['adapter_b'], 'L2_gnn_mlp_w1': _L2_gnn_in['mlp_w1'], 'L2_gnn_mlp_b1': _L2_gnn_in['mlp_b1'], 'L2_gnn_mlp_ln_g': _L2_gnn_in['mlp_ln_g'], 'L2_gnn_mlp_ln_b': _L2_gnn_in['mlp_ln_b'], 'L2_gnn_mlp_w2': _L2_gnn_in['mlp_w2'], 'L2_gnn_mlp_b2': _L2_gnn_in['mlp_b2'], 'L3_gnn_W1': _L3_gnn_in['W1'], 'L3_gnn_W2': _L3_gnn_in['W2'], 'L3_gnn_epsilons': _L3_gnn_in['epsilons'], 'L3_gnn_mlp1_w': _L3_gnn_in['mlp1_w'], 'L3_gnn_mlp1_b': _L3_gnn_in['mlp1_b'], 'L3_gnn_mlp2_w': _L3_gnn_in['mlp2_w'], 'L3_gnn_mlp2_b': _L3_gnn_in['mlp2_b']}

def reference(x, src, dst, L0_gnn_W, L0_gnn_b, L2_gnn_conv_wl, L2_gnn_conv_bl, L2_gnn_conv_wr, L2_gnn_ln_g, L2_gnn_ln_b, L2_gnn_adapter_w, L2_gnn_adapter_b, L2_gnn_mlp_w1, L2_gnn_mlp_b1, L2_gnn_mlp_ln_g, L2_gnn_mlp_ln_b, L2_gnn_mlp_w2, L2_gnn_mlp_b2, L3_gnn_W1, L3_gnn_W2, L3_gnn_epsilons, L3_gnn_mlp1_w, L3_gnn_mlp1_b, L3_gnn_mlp2_w, L3_gnn_mlp2_b):
    import jax
    import jax.numpy as jnp

    def _L0_gnn_ref(x, W, b, src, dst):
        import jax, jax.numpy as jnp
        import numpy as np
        N_NODES = 3125
        N_EDGES = 50000
        D = 64
        K = 10
        ALPHA = 0.1
        h0 = x @ W + b
        ones = jnp.ones((src.shape[0],), dtype=x.dtype)
        deg_out = jax.ops.segment_sum(ones, src, num_segments=N_NODES)
        deg_in = jax.ops.segment_sum(ones, dst, num_segments=N_NODES)
        norm_src = jnp.where(deg_out > 0, jax.lax.rsqrt(jnp.maximum(deg_out, 1.0)), 0.0)[:, None]
        norm_dst = jnp.where(deg_in > 0, jax.lax.rsqrt(jnp.maximum(deg_in, 1.0)), 0.0)[:, None]
        h = h0
        for _ in range(K):
            msg = (h * norm_src)[src]
            agg = jax.ops.segment_sum(msg, dst, num_segments=N_NODES)
            h = (1.0 - ALPHA) * (agg * norm_dst) + ALPHA * h0
        return h

    def _L1_gnn_ref(edge_index, embedding_weight):
        import jax, jax.numpy as jnp
        import numpy as np
        NUM_NODES = 50000
        EMBED_DIM = 64
        NUM_EDGES = 1250000
        NUM_LAYERS = 3
        row, col = (edge_index[0], edge_index[1])
        n = embedding_weight.shape[0]
        deg = jax.ops.segment_sum(jnp.ones_like(row, dtype=embedding_weight.dtype), row, num_segments=n)
        deg_inv_sqrt = jnp.where(deg > 0, jax.lax.rsqrt(jnp.maximum(deg, 1.0)) * jnp.where(deg > 0, 1.0, 0.0) + jax.lax.rsqrt(jnp.maximum(deg, 1.0)) * 0.0, 0.0)
        deg_inv_sqrt = jnp.where(deg > 0, jax.lax.rsqrt(jnp.maximum(deg, 1.0)), 0.0)
        x = embedding_weight
        acc = x
        for _ in range(NUM_LAYERS):
            m = deg_inv_sqrt[row][:, None] * x[col]
            x = jax.ops.segment_sum(m, row, num_segments=n) * deg_inv_sqrt[:, None]
            acc = acc + x
        return acc / (NUM_LAYERS + 1)

    def _L2_gnn_ref(x, edge_index, conv_wl, conv_bl, conv_wr, ln_g, ln_b, adapter_w, adapter_b, mlp_w1, mlp_b1, mlp_ln_g, mlp_ln_b, mlp_w2, mlp_b2):
        import jax, jax.numpy as jnp
        import numpy as np
        N_NODES = 3125
        N_EDGES = 31250
        H = 64
        N_LAYERS = 5
        EPS = 1e-05

        def layer_norm(x, g, b):
            m = jnp.mean(x, axis=-1, keepdims=True)
            v = jnp.var(x, axis=-1, keepdims=True)
            return (x - m) * jax.lax.rsqrt(v + EPS) * g + b

        def sage_conv(x, src, dst, n_nodes, wl, bl, wr):
            xj = x[src]
            deg = jax.ops.segment_sum(jnp.ones((src.shape[0], 1), x.dtype), dst, num_segments=n_nodes)
            amax = jax.ops.segment_max(xj, dst, num_segments=n_nodes)
            amax = jnp.where(deg > 0, amax, jnp.zeros_like(amax))
            amean = jax.ops.segment_sum(xj, dst, num_segments=n_nodes) / jnp.maximum(deg, 1.0)
            agg = jnp.concatenate([amax, amean], axis=-1)
            return agg @ wl.T + bl + x @ wr.T
        src, dst = (edge_index[0], edge_index[1])
        n = x.shape[0]
        x_res = x @ adapter_w.T + adapter_b
        h = sage_conv(x, src, dst, n, conv_wl[0], conv_bl[0], conv_wr[0])
        h = jax.nn.silu(layer_norm(h, ln_g[0], ln_b[0]) + x_res)
        for i in range(1, N_LAYERS):
            h_res = h
            h = sage_conv(h, src, dst, n, conv_wl[i], conv_bl[i], conv_wr[i])
            h = jax.nn.silu(layer_norm(h, ln_g[i], ln_b[i]) + h_res)
        h = jax.nn.silu(h @ mlp_w1.T + mlp_b1)
        h = layer_norm(h, mlp_ln_g, mlp_ln_b)
        return h @ mlp_w2.T + mlp_b2

    def _L3_gnn_ref(x, edge_index, W1, W2, epsilons, mlp1_w, mlp1_b, mlp2_w, mlp2_b):
        import jax, jax.numpy as jnp
        import numpy as np
        D = 4
        H = 16
        N = 50000
        E = 25000
        TI, TJ = np.tril_indices(D, -1)

        def _householder(params):
            A = jnp.zeros(params.shape[:-1] + (D, D), params.dtype)
            A = A.at[..., TI, TJ].set(params) + jnp.eye(D, dtype=params.dtype)
            Q, R = jnp.linalg.qr(A)
            s = jnp.sign(jnp.diagonal(R, axis1=-2, axis2=-1))
            s = jnp.where(s == 0, jnp.ones_like(s), s)
            return Q * s[..., None, :]

        def _mlp(z, w1, b1, w2, b2):
            h = jax.nn.relu(z @ w1.T + b1)
            return h @ w2.T + b2

        def _forward(x, edge_index, W1, W2, epsilons, mlp1_w, mlp1_b, mlp2_w, mlp2_b):
            n = x.shape[0]
            xr = x.reshape(n, D, H)
            xt = jnp.einsum('ndf,dk->nkf', xr, W1)
            xt = jnp.einsum('ndf,fg->ndg', xt, W2)
            loops = jnp.arange(n)
            row = jnp.concatenate([edge_index[0], loops])
            col = jnp.concatenate([edge_index[1], loops])
            deg = jax.ops.segment_sum(jnp.ones_like(row, x.dtype), row, num_segments=n)
            dis = jnp.where(deg > 0, deg ** (-0.5), jnp.zeros_like(deg))
            xf = xt.reshape(n, D * H)
            xi = xf[col]
            xj = xf[row]
            cat_ve = jnp.concatenate([xi, xj], axis=-1)
            cat_ue = jnp.concatenate([xj, xi], axis=-1)
            Fve = _householder(_mlp(cat_ve, mlp1_w, mlp1_b, mlp2_w, mlp2_b))
            Fue = _householder(_mlp(cat_ue, mlp1_w, mlp1_b, mlp2_w, mlp2_b))
            xjr = xj.reshape(-1, D, H)
            msg = jnp.einsum('eka,ekb,ebh->eah', Fve, Fue, xjr)
            msg = msg * (dis[col] * dis[row])[:, None, None]
            agg = jax.ops.segment_sum(msg.reshape(-1, D * H), col, num_segments=n)
            lap = jax.nn.elu(agg.reshape(n, D, H))
            coeff = (1.0 + jnp.tanh(epsilons))[None, :, None]
            return (coeff * xr - lap).reshape(n, D * H)
        return _forward(x, edge_index, W1, W2, epsilons, mlp1_w, mlp1_b, mlp2_w, mlp2_b)
    edge_index = jnp.stack([src, dst])
    x = _layernorm(x + _L0_gnn_ref(x, L0_gnn_W, L0_gnn_b, src, dst), axis=-1)
    x = _layernorm(x + _L1_gnn_ref(edge_index, x), axis=-1)
    x = _layernorm(x + _L2_gnn_ref(x, edge_index, L2_gnn_conv_wl, L2_gnn_conv_bl, L2_gnn_conv_wr, L2_gnn_ln_g, L2_gnn_ln_b, L2_gnn_adapter_w, L2_gnn_adapter_b, L2_gnn_mlp_w1, L2_gnn_mlp_b1, L2_gnn_mlp_ln_g, L2_gnn_mlp_ln_b, L2_gnn_mlp_w2, L2_gnn_mlp_b2), axis=-1)
    x = _layernorm(x + _L3_gnn_ref(x, edge_index, L3_gnn_W1, L3_gnn_W2, L3_gnn_epsilons, L3_gnn_mlp1_w, L3_gnn_mlp1_b, L3_gnn_mlp2_w, L3_gnn_mlp2_b), axis=-1)
    return x

_drawn_inputs = setup_inputs


def setup_inputs(seed=0):
    import zlib

    import numpy as np

    out = dict(_drawn_inputs(seed))
    spreads = {'L2_gnn_conv_bl': (0.0, 0.1),
     'L2_gnn_ln_g': (1.0, 0.2),
     'L2_gnn_ln_b': (0.0, 0.1),
     'L2_gnn_adapter_b': (0.0, 0.1),
     'L2_gnn_mlp_b1': (0.0, 0.1),
     'L2_gnn_mlp_ln_g': (1.0, 0.2),
     'L2_gnn_mlp_ln_b': (0.0, 0.1),
     'L2_gnn_mlp_b2': (0.0, 0.1),
     'L3_gnn_epsilons': (0.0, 0.1),
     'L3_gnn_mlp1_b': (0.0, 0.8),
     'L3_gnn_mlp2_b': (0.0, 0.8)}
    factors = {}
    for name, (base, spread) in spreads.items():
        noise = np.random.default_rng([zlib.crc32(name.encode()), seed]).standard_normal(out[name].shape)
        drawn = base * np.exp(spread * noise) if base else spread * noise
        out[name] = jnp.asarray(drawn.astype(out[name].dtype))
    for name, factor in factors.items():
        out[name] = (out[name] * factor).astype(out[name].dtype)
    return out
```

```python
from contextlib import ExitStack

import numpy as np

import concourse.bass as bass
from concourse import mybir

F32 = mybir.dt.float32
F16 = mybir.dt.float16
I32 = mybir.dt.int32
ALU = mybir.AluOpType
ACT = mybir.ActivationFunctionType
AX = mybir.AxisListType.X

P = 128
N = 3125
E = 103125
D = 64
T = -(-N // P)
NP = T * P
TAIL = N - (T - 1) * P
EC = -(-E // P)
DUMMY = NP - 1
NOHI = 63
HC = 13
HSTEPS = EC // HC
W = 64
S = 8
HS = S // 2
CAP = 4000
KEY = 4096
MINBLK = 2
WB = W // S
BLOCKS = WB * (E // W + 1 + sum(E // (P * t) // W + 1 for t in range(1, T)))
CHUNK = 4
CHUNKS = [(c, min(CHUNK, T - c)) for c in range(0, T, CHUNK)]
NC = len(CHUNKS)
LOSCALE = 2048.0
ROUNDS = 10
ALPHA = 0.1
HOPS = 3
LAYERS = 5
HID = 4 * D
EPS = 1e-5
BIG = 3.0e38
DD, HH = 4, 16
NPAR = DD * (DD - 1) // 2
TW = D + 2 * HH + 1
assert EC == HC * HSTEPS and W % S == 0 and DD * HH == D


def bc(ap, axis, n):
    x = ap.unsqueeze(axis)
    shape = list(x.shape)
    shape[axis] = n
    return x.broadcast_to(shape)


HELD = []


class Program:

    def __init__(self, nc, ctx, ins, out):
        self.nc, self.ctx, self.ins, self.out = nc, ctx, ins, out

        def dram(name, shape, dt):
            return nc.dram_tensor(name, shape, dt, kind="Internal").ap()

        HELD[:] = [self.sem("held")]
        self.src_pad = dram("src_pad", [E + P], I32)
        self.key_row = dram("key_row", [NP], F32)
        self.perm_tab = dram("perm_tab", [NP, 4], I32)
        self.ids_dram = dram("ids_blocks", [BLOCKS * P * S], I32)
        self.x2_dram = dram("x2_rows", [NP, D + 1], F32)
        self.h_tab = dram("h_tab", [NP, D], F32)
        self.t_tab = dram("t_tab", [NP, TW], F32)

        sb = self.sb
        self.ident = sb("ident", [P, P], F32)
        self.identh = sb("identh", [P, P], F16)
        self.comb = sb("comb", [P, D], F32)
        self.iota = sb("iota", [P, P], I32)
        self.slot = sb("slot", [P, W], F32)
        self.deg = sb("deg", [P, T], F32)
        self.start = sb("start", [P, T], F32)
        self.sorted = sb("sorted_tab", [P, T, 4], I32)
        self.sdeg = sb("sdeg", [P, T], F32)
        self.nblk = sb("nblk", [1, T], I32)
        self.nwin = sb("nwin", [1, T], I32)
        self.nwall = sb("nwall", [1, 1], I32)
        self.dego = sb("dego", [P, T], F32)

    def sb(self, name, shape, dt, ctx=None):
        return (ctx or self.ctx).enter_context(self.nc.sbuf_tensor(name, shape, dt))

    def ps(self, name, shape, dt, ctx):
        return ctx.enter_context(self.nc.psum_tensor(name, shape, dt))

    def sem(self, name):
        return self.ctx.enter_context(self.nc.semaphore(name))


def hold(eng, sem, value):
    eng.wait_ge(sem, value)
    eng.sem_inc(HELD[0], 1)


def one_hots(v, lo_out, hi_out, iota, lo, hi, n):
    v.tensor_tensor(lo_out, bc(iota[:, 0:P], 1, n), bc(lo, 2, P), ALU.is_equal)
    return v.tensor_tensor(hi_out, bc(iota[:, 0:T], 1, n), bc(hi, 2, T), ALU.is_equal)


def stage_graph(g):
    nc = g.nc
    src, dst = g.ins["src"], g.ins["dst"]
    with ExitStack() as c:
        dst_sb = g.sb("dst_sb", [P, EC], I32, c)
        lo = g.sb("dst_lo", [P, EC], I32, c)
        hi = g.sb("dst_hi", [P, EC], I32, c)
        oh_lo = g.sb("oh_lo", [P, 2, HC, P], F16, c)
        oh_hi = g.sb("oh_hi", [P, 2, HC, T], F16, c)
        zh = g.sb("zh", [P, P], F16, c)
        tri = g.sb("tri", [P, P], F32, c)
        ones = g.sb("ones", [P, P], F32, c)
        zt = g.sb("zt", [P, T], F32, c)
        incl = g.sb("incl", [P, T], F32, c)
        excl = g.sb("excl", [P, T], F32, c)
        nid = g.sb("nid", [P, T], F32, c)
        nkey = g.sb("nkey", [P, T], F32, c)
        key = g.sb("key", [P, T], F32, c)
        keys = g.sb("keys", [P, NP], F32, c)
        gt = g.sb("gt", [P, 2, NP], F16, c)
        rank = g.sb("rank", [P, T], F32, c)
        ranki = g.sb("ranki", [P, T], I32, c)
        tab = g.sb("tab", [P, T, 4], I32, c)
        zsrc = g.sb("zsrc", [1, P], I32, c)
        tmax = g.sb("tmax", [T, 1], F32, c)
        allmax = g.sb("allmax", [1, T], F32, c)
        maxi = g.sb("maxi", [1, T], I32, c)
        one = g.sb("one", [1, 1], F32, c)
        onei = g.sb("onei", [1, 1], I32, c)
        hist = g.ps("hist", [P, 512], F32, c)
        pre = g.ps("pre", [P, 512], F32, c)
        mt = g.ps("mt", [P, 512], F32, c)
        mt2 = g.ps("mt2", [P, 512], F32, c)
        dst_pad = g.sem("dst_padded")
        loaded = g.sem("dst_loaded")
        const = g.sem("graph_constants")
        zeros = g.sem("zeros_set")
        coded = g.sem("dst_coded")
        counted = g.sem("dst_counted")
        hist_done = g.sem("histogram_done")
        deg_done = g.sem("degrees_copied")
        pre_done = g.sem("prefix_done")
        key_done = g.sem("keys_computed")
        key_out = g.sem("keys_stored")
        key_in = g.sem("keys_loaded")
        ranked = g.sem("nodes_ranked")
        scattered = g.sem("rows_scattered")
        tab_in = g.sem("sorted_loaded")
        sdeg_done = g.sem("sorted_degrees")
        max_t = g.sem("degrees_transposed")
        max_d = g.sem("tile_maxima")
        max_r = g.sem("maxima_row")
        pad_out = g.sem("src_pad_stored")
        counts = g.sem("block_counts")

        with nc.Block() as block:

            @block.sync
            def _(sp):
                full = (P - 1) * EC
                sp.wait_ge(dst_pad, 1)
                sp.dma_start(dst_sb[0:P - 1, :], dst[0:full].rearrange("(p j) -> p j", j=EC)).then_inc(loaded, 16)
                sp.dma_start(dst_sb[P - 1:P, 0:E - full], dst[full:E].rearrange("(p j) -> p j", p=1)).then_inc(loaded, 16)
                sp.dma_start(g.src_pad[0:E].rearrange("(a b) -> a b", a=125), src.rearrange("(a b) -> a b", a=125)).then_inc(pad_out, 16)
                sp.wait_ge(zeros, 1)
                sp.dma_start(g.src_pad[E:E + P].rearrange("(a b) -> a b", a=1), zsrc[:]).then_inc(pad_out, 16)
                hold(sp, key_done, 1)
                with nc.allow_non_contiguous_dma(reason="keys in order of nodes, once"):
                    sp.dma_start(g.key_row.rearrange("(t p) -> p t", p=P), key[:]).then_inc(key_out, 16)
                sp.wait_ge(key_out, 16)
                sp.dma_start(keys[:], g.key_row.rearrange("(a n) -> a n", a=1).broadcast_to([P, NP])).then_inc(key_in, 16)
                sp.wait_ge(scattered, 16 * T)
                sp.dma_start(g.sorted[:], g.perm_tab.rearrange("(t p) c -> p t c", p=P)).then_inc(tab_in, 16)
                sp.wait_ge(pad_out, 32)

            @block.gpsimd
            def _(pool):
                nc.gpsimd.memset(dst_sb[:], NOHI * P).then_inc(dst_pad, 1)
                nc.gpsimd.memset(zsrc[:], 0).then_inc(zeros, 1)
                nc.gpsimd.iota(g.iota[:], [[1, P]], channel_multiplier=0)
                nc.gpsimd.iota(g.slot[:], [[1, W]], channel_multiplier=0, allow_small_or_imprecise_dtypes=True)
                nc.gpsimd.iota(nid[:], [[P, T]], channel_multiplier=1, allow_small_or_imprecise_dtypes=True)
                nc.gpsimd.memset(tab[:], 0)
                nc.gpsimd.memset(g.ident[:], 0.0)
                nc.gpsimd.memset(g.comb[:], 0.0)
                nc.gpsimd.memset(tri[:], 1.0)
                pool.drain()
                nc.gpsimd.affine_select(out=g.ident[:], in_=g.ident[:], compare_op=ALU.not_equal, fill=1.0, base=0,
                                        pattern=[[-1, P]], channel_multiplier=1)
                nc.gpsimd.affine_select(out=tri[:], in_=tri[:], compare_op=ALU.is_gt, fill=0.0, base=0,
                                        pattern=[[1, P]], channel_multiplier=-1)
                nc.gpsimd.affine_select(out=g.comb[:], in_=g.comb[:], compare_op=ALU.not_equal, fill=1.0, base=0,
                                        pattern=[[-1, D]], channel_multiplier=1)
                pool.drain()
                nc.gpsimd.affine_select(out=g.comb[:], in_=g.comb[:], compare_op=ALU.not_equal, fill=1.0 / LOSCALE,
                                        base=-D, pattern=[[-1, D]], channel_multiplier=1)
                nc.gpsimd.tensor_copy(g.identh[:], g.ident[:]).then_inc(const, 1)
                pool.wait_ge(ranked, 1)
                for t in range(T):
                    nc.gpsimd.indirect_dma_start(
                        out=g.perm_tab, out_offset=bass.IndirectOffsetOnAxis(ap=ranki[:, t:t + 1], axis=0),
                        in_=tab[:, t, :], in_offset=None).then_inc(scattered, 16)
                pool.wait_ge(scattered, 16 * T)

            @block.vector
            def _(v):
                v.memset(zh[:], 0.0)
                v.memset(ones[:], 1.0)
                v.memset(one[:], 1.0)
                v.memset(zt[:], 0.0)
                v.wait_ge(const, 1)
                v.wait_ge(loaded, 32)
                v.tensor_scalar(lo[:], dst_sb[:], P - 1, None, ALU.bitwise_and)
                v.tensor_scalar(hi[:], dst_sb[:], 7, None, ALU.logical_shift_right)
                v.drain()
                with v.Fori(0, HSTEPS // 2) as i:
                    for b in range(2):
                        v.wait_ge(counted, 2 * i + b)
                        at = bass.ds((2 * i + b) * HC, HC)
                        one_hots(v, oh_lo[:, b], oh_hi[:, b], g.iota, lo[:, at], hi[:, at], HC).then_inc(coded, 1)
                v.wait_ge(hist_done, 1)
                v.tensor_copy(g.deg[:], hist[:, 0:T])
                v.drain()
                v.tensor_tensor_scan(incl[:], g.deg[:], zt[:], 0.0, ALU.add, ALU.add)
                v.drain()
                v.tensor_tensor(excl[:], incl[:], g.deg[:], ALU.subtract).then_inc(deg_done, 1)
                v.tensor_scalar(nkey[:], nid[:], -1.0, KEY - 1.0, ALU.mult, ALU.add)
                v.tensor_scalar(key[:], g.deg[:], float(CAP), float(KEY), ALU.min, ALU.mult)
                v.drain()
                v.tensor_tensor(key[:], key[:], nkey[:], ALU.add).then_inc(key_done, 1)
                v.wait_ge(pre_done, 1)
                v.tensor_copy(g.start[:], pre[:, 0:T])
                v.drain()
                v.tensor_copy(tab[:, :, 0], g.start[:])
                v.tensor_copy(tab[:, :, 1], g.deg[:])
                v.tensor_copy(tab[:, :, 2], nid[:])
                v.wait_ge(key_in, 16)
                for t in range(T):
                    v.tensor_scalar(gt[:, t % 2, :], keys[:], key[:, t:t + 1], 0.0, ALU.is_gt, ALU.add,
                                    accum_out=rank[:, t:t + 1])
                    if t % 2:
                        v.drain()
                v.drain()
                v.tensor_copy(ranki[:], rank[:]).then_inc(ranked, 1)
                v.wait_ge(tab_in, 16)
                v.tensor_copy(g.sdeg[:], g.sorted[:, :, 1]).then_inc(sdeg_done, 1)
                v.wait_ge(max_t, 1)
                v.tensor_reduce(tmax[:], mt[0:T, 0:P], AX, ALU.max).then_inc(max_d, 1)
                v.wait_ge(max_r, 1)
                v.tensor_copy(allmax[:], mt2[0:1, 0:T])
                v.drain()
                v.tensor_reduce(one[:], allmax[:], AX, ALU.max)
                v.tensor_copy(maxi[:], allmax[:])
                v.drain()
                v.tensor_copy(onei[:], one[:])
                v.tensor_scalar(g.nblk[:], maxi[:], float(S - 1), None, ALU.add)
                v.drain()
                v.tensor_scalar(g.nblk[:], g.nblk[:], 3, None, ALU.logical_shift_right)
                v.drain()
                v.tensor_scalar(g.nblk[:], g.nblk[:], float(MINBLK), None, ALU.max)
                v.tensor_scalar(onei[:], onei[:], float(W - 1), None, ALU.add)
                v.drain()
                v.tensor_scalar(g.nwin[:], g.nblk[:], float(WB - 1), None, ALU.add)
                v.tensor_scalar(g.nwall[:], onei[:], 6, None, ALU.logical_shift_right)
                v.drain()
                v.tensor_scalar(g.nwin[:], g.nwin[:], 3, None, ALU.logical_shift_right)
                v.tensor_scalar(g.nwall[:], g.nwall[:], 1.0, None, ALU.max).then_inc(counts, 1)

            @block.tensor
            def _(pe):
                pe.wait_ge(coded, 1)
                nc.tensor.matmul(hist[:, 0:T], zh[:], oh_hi[:, 0, 0, :], start=True, stop=False,
                                 skip_group_check=True).then_inc(counted, 1)
                with pe.Fori(0, HSTEPS // 2) as i:
                    for b in range(2):
                        pe.wait_ge(coded, 2 * i + b + 1)
                        for j in range(HC):
                            mm = nc.tensor.matmul(hist[:, 0:T], oh_lo[:, b, j, :], oh_hi[:, b, j, :],
                                                  start=False, stop=False, skip_group_check=True)
                        mm.then_inc(counted, 1)
                nc.tensor.matmul(hist[:, 0:T], zh[:], oh_hi[:, 0, 0, :], start=False, stop=True,
                                 skip_group_check=True).then_inc(hist_done, 1)
                pe.wait_ge(deg_done, 1)
                nc.tensor.matmul(pre[:, 0:T], tri[:], g.deg[:], start=True, stop=False)
                nc.tensor.matmul(pre[:, 0:T], ones[:], excl[:], start=False, stop=True).then_inc(pre_done, 1)
                pe.wait_ge(sdeg_done, 1)
                nc.tensor.transpose(mt[0:T, 0:P], g.sdeg[:], g.ident[:]).then_inc(max_t, 1)
                pe.wait_ge(max_d, 1)
                nc.tensor.transpose(mt2[0:1, 0:T], tmax[:], g.ident[0:T, 0:T]).then_inc(max_r, 1)


def stage_lists(g):
    nc = g.nc
    with ExitStack() as c:
        first = g.sb("win_start", [P, T], I32, c)
        win = g.sb("win_ids", [P, T, W], I32, c)
        winf = g.sb("win_masked", [P, T, W], F32, c)
        mask = g.sb("win_mask", [P, T, W], F32, c)
        cur = g.sb("cur_start", [P, 1], F32, c)
        rem = g.sb("cur_left", [P, 1], F32, c)
        curi = g.sb("cur_start_i", [P, 1], I32, c)
        xwin = g.sb("xwin", [P, W], I32, c)
        xmask = g.sb("xmask", [P, W], F32, c)
        starts = g.sem("list_starts")
        landed = g.sem("list_windows")
        masked = g.sem("list_masked")
        stored = g.sem("list_stored")
        x_idx = g.sem("overflow_start")
        x_landed = g.sem("overflow_window")
        x_masked = g.sem("overflow_masked")
        x_stored = g.sem("overflow_stored")
        src_rows = g.src_pad.rearrange("(a e) -> a e", a=1)

        def blocks_at(block0):
            return g.ids_dram[bass.ds(block0 * (P * S), W * P)].rearrange("(b p s) -> p b s", p=P, s=S)

        with nc.Block() as block:

            @block.vector
            def _(v):
                v.tensor_scalar(first[:], g.sorted[:, :, 0], float(E), None, ALU.min).then_inc(starts, 1)
                v.tensor_tensor(mask[:], bc(g.slot[:], 1, T), bc(g.sdeg[:], 2, W), ALU.is_lt)
                v.wait_ge(landed, 16 * T)
                v.tensor_scalar(winf[:], win[:], float(-DUMMY), None, ALU.add)
                v.drain()
                v.tensor_tensor(winf[:], winf[:], mask[:], ALU.mult)
                v.drain()
                v.tensor_scalar(win[:], winf[:], float(DUMMY), None, ALU.add).then_inc(masked, 1)
                k = v.alloc_register("v_over")
                v.reg_mov(k, 0)
                with v.Fori(0, T) as t:
                    n = v.value_load(g.nwin[0:1, bass.ds(t, 1)], min_val=1, max_val=BLOCKS)
                    with v.If(n > 1):
                        v.tensor_copy(cur[:], g.sorted[:, bass.ds(t, 1), 0])
                        v.tensor_copy(rem[:], g.sdeg[:, bass.ds(t, 1)])
                        v.drain()
                        with v.Fori(1, n) as _w:
                            done = v.snap(k)
                            v.tensor_scalar(cur[:], cur[:], float(W), float(E), ALU.add, ALU.min)
                            v.tensor_scalar(rem[:], rem[:], float(-W), None, ALU.add)
                            v.drain()
                            v.tensor_copy(curi[:], cur[:]).then_inc(x_idx, 1)
                            v.tensor_scalar(xmask[:], g.slot[:], rem[:, 0:1], None, ALU.is_lt)
                            v.wait_ge(x_landed, (done + 1) * 16)
                            v.tensor_scalar(winf[:, 0, :], xwin[:], float(-DUMMY), None, ALU.add)
                            v.drain()
                            v.tensor_tensor(winf[:, 0, :], winf[:, 0, :], xmask[:], ALU.mult)
                            v.drain()
                            v.tensor_scalar(xwin[:], winf[:, 0, :], float(DUMMY), None, ALU.add).then_inc(x_masked, 1)
                            v.wait_ge(x_stored, (done + 1) * 16)
                            v.reg_add(k, k, 1)

            @block.gpsimd
            def _(pool):
                pool.wait_ge(starts, 1)
                for t in range(T):
                    nc.gpsimd.indirect_dma_start(
                        out=win[:, t, :], out_offset=None, in_=src_rows,
                        in_offset=bass.IndirectOffsetOnAxis(ap=first[:, t:t + 1], axis=1)).then_inc(landed, 16)
                k = pool.alloc_register("p_over")
                pool.reg_mov(k, 0)
                with pool.Fori(0, T) as t:
                    n = pool.value_load(g.nwin[0:1, bass.ds(t, 1)], min_val=1, max_val=BLOCKS)
                    with pool.If(n > 1):
                        with pool.Fori(1, n) as _w:
                            done = pool.snap(k)
                            hold(pool, x_idx, done + 1)
                            nc.gpsimd.indirect_dma_start(
                                out=xwin[:], out_offset=None, in_=src_rows,
                                in_offset=bass.IndirectOffsetOnAxis(ap=curi[:], axis=1)).then_inc(x_landed, 16)
                            hold(pool, x_landed, (done + 1) * 16)
                            pool.reg_add(k, k, 1)

            @block.sync
            def _(sp):
                k = sp.alloc_register("s_over")
                at = sp.alloc_register("s_block")
                sp.reg_mov(k, 0)
                sp.reg_mov(at, 0)
                sp.wait_ge(masked, 1)
                with sp.Fori(0, T) as t:
                    n = sp.value_load(g.nwin[0:1, bass.ds(t, 1)], min_val=1, max_val=BLOCKS)
                    base = sp.snap(at, min_val=0, max_val=BLOCKS - WB)
                    sp.dma_start(blocks_at(base), win[:, bass.ds(t, 1), :].rearrange("p a (b s) -> p (a b) s", s=S)
                                 ).then_inc(stored, 16)
                    with sp.If(n > 1):
                        with sp.Fori(1, n) as _w:
                            done = sp.snap(k)
                            sp.reg_add(at, at, WB)
                            here = sp.snap(at, min_val=WB, max_val=BLOCKS - WB)
                            hold(sp, x_masked, done + 1)
                            sp.dma_start(blocks_at(here), xwin[:].rearrange("p (b s) -> p b s", s=S)
                                         ).then_inc(x_stored, 16)
                            sp.reg_add(k, k, 1)
                    sp.reg_add(at, at, WB)
                sp.wait_ge(stored, 16 * T)
                hold(sp, x_stored, sp.snap(k) * 16)



TT = T + T % 2
PAIRS = TT // 2
GN = 16
GSTEPS = P // GN
STEPS = PAIRS * GSTEPS


def stage_adjacency(g, A, c):
    nc = g.nc
    none = float(NOHI * P)
    with ExitStack() as c:
        cur = g.sb("a_start", [P, TT], F32, c)
        rem = g.sb("a_left", [P, TT], F32, c)
        first = g.sb("a_start_i", [P, TT], I32, c)
        win = g.sb("a_win", [P, TT, W], I32, c)
        winf = g.sb("a_winf", [P, TT, W], F32, c)
        hi = g.sb("a_hi", [P, PAIRS * P], I32, c)
        lo = g.sb("a_lo", [P, PAIRS * P], I32, c)[:]
        oh_lo = g.sb("a_oh_lo", [P, 2, GN, P], F16, c)
        oh_hi = g.sb("a_oh_hi", [P, 2, GN, T], F16, c)
        turned = [g.ps(f"a_turned{b}", [P, 512], F32, c) for b in range(2)]
        cols = [[g.ps(f"a_cols{b}{h}", [P, 512], F32, c) for h in range(2)] for b in range(2)]
        starts = g.sem("adj_starts")
        landed = g.sem("adj_windows")
        masked = g.sem("adj_masked")
        turn_done = g.sem("adj_turned")
        turn_read = g.sem("adj_turned_read")
        coded = g.sem("adj_coded")
        used = g.sem("adj_multiplied")
        moved = g.sem("adj_moved")
        src_rows = g.src_pad.rearrange("(a e) -> a e", a=1)

        def columns(b, h, u, gi):
            frm = cols[b][h][:, 0:GN * T].rearrange("q (p h) -> q h p", h=T)
            return A[:, :, bass.ds(u * (2 * P) + h * P + gi * GN, GN)], frm

        def steps(eng, w, do):
            with eng.Fori(0, PAIRS - 1) as u:
                for gi in range(GSTEPS):
                    do(w * STEPS + u * GSTEPS + gi, u, gi, 2)
            for gi in range(GSTEPS):
                do(w * STEPS + (PAIRS - 1) * GSTEPS + gi, PAIRS - 1, gi, 2 if TT == T else 1)

        def overflow(eng, body):
            n = eng.value_load(g.nwall[0:1, 0:1], min_val=1, max_val=E // W + 1)
            with eng.If(n > 1):
                with eng.Fori(1, n) as w:
                    body(w)

        with nc.Block() as block:

            @block.vector
            def _(v):
                def windows(w, first_pass):
                    if first_pass:
                        v.memset(cur[:], 0.0)
                        v.memset(rem[:], 0.0)
                        v.memset(win[:, T:TT, :], 0)
                        v.drain()
                        v.tensor_copy(cur[:, 0:T], g.start[:])
                        v.tensor_copy(rem[:, 0:T], g.deg[:])
                        v.drain()
                        v.tensor_scalar(first[:], cur[:], float(E), None, ALU.min).then_inc(starts, 1)
                    else:
                        v.tensor_scalar(cur[:], cur[:], float(W), float(E), ALU.add, ALU.min)
                        v.tensor_scalar(rem[:], rem[:], float(-W), None, ALU.add)
                        v.drain()
                        v.tensor_copy(first[:], cur[:]).then_inc(starts, 1)
                    v.wait_ge(turn_read, w * PAIRS)
                    v.wait_ge(landed, (w + 1) * (16 * T))
                    v.tensor_scalar(winf[:], win[:], -none, None, ALU.add)
                    v.drain()
                    v.tensor_tensor(win[:], bc(g.slot[:], 1, TT), bc(rem[:], 2, W), ALU.is_lt)
                    v.drain()
                    v.tensor_tensor(winf[:], winf[:], win[:], ALU.mult)
                    v.drain()
                    v.tensor_scalar(winf[:], winf[:], none, None, ALU.add).then_inc(masked, 1)
                    for u in range(PAIRS):
                        v.wait_ge(turn_done, w * PAIRS + u + 1)
                        v.tensor_copy(lo[:, u * P:(u + 1) * P], turned[u % 2][:, 0:P]).then_inc(turn_read, 1)
                    v.drain()
                    v.tensor_scalar(hi[:], lo, 7, None, ALU.logical_shift_right)
                    v.drain()
                    v.tensor_scalar(lo, lo, P - 1, None, ALU.bitwise_and)
                    v.drain()

                def code(k, u, gi, halves):
                    v.wait_ge(used, k)
                    at = bass.ds(u * P + gi * GN, GN)
                    one_hots(v, oh_lo[:, gi % 2], oh_hi[:, gi % 2], g.iota, lo[:, at], hi[:, at], GN).then_inc(coded, 1)

                def add(k, u, gi, halves):
                    code(k, u, gi, halves)
                    v.wait_ge(used, k + 2)
                    for h in range(halves):
                        to, frm = columns(gi % 2, h, u, gi)
                        last = v.tensor_tensor(to, to, frm, ALU.add)
                    last.then_inc(moved, 1)

                windows(0, True)
                steps(v, 0, code)
                v.wait_ge(moved, STEPS + 1)

                def more(w):
                    windows(w, False)
                    steps(v, w, add)

                overflow(v, more)
                v.drain()
                v.tensor_reduce(g.dego[:], A[:], AX, ALU.add)
                v.drain()

            @block.gpsimd
            def _(pool):
                def gather(w):
                    hold(pool, starts, w + 1)
                    hold(pool, landed, w * (16 * T))
                    for t in range(T):
                        nc.gpsimd.indirect_dma_start(
                            out=win[:, t, :], out_offset=None, in_=src_rows,
                            in_offset=bass.IndirectOffsetOnAxis(ap=first[:, t:t + 1], axis=1)).then_inc(landed, 16)

                gather(0)
                overflow(pool, gather)

            @block.scalar
            def _(act):
                act.nop().then_inc(moved, 1)

                def move(k, u, gi, halves):
                    act.wait_ge(used, k + 2)
                    for h in range(halves):
                        to, frm = columns(gi % 2, h, u, gi)
                        last = nc.scalar.activation(to, frm, ACT.Copy)
                    last.then_inc(moved, 1)

                steps(act, 0, move)

            @block.tensor
            def _(pe):
                def passes(w, first_pass):
                    pe.wait_ge(masked, w + 1)
                    for u in range(PAIRS):
                        if not first_pass or u >= 2:
                            pe.wait_ge(turn_read, w * PAIRS + u - 1)
                        tr = nc.tensor.transpose(turned[u % 2][:, 0:P],
                                                 winf[:, 2 * u:2 * u + 2, :].rearrange("p a b -> p (a b)"), g.ident[:])
                        tr.then_inc(turn_done, 1)
                    if first_pass:
                        pe.nop().then_inc(used, 1)

                    def multiply(k, u, gi, halves):
                        pe.wait_ge(coded, k + 1)
                        pe.wait_ge(moved, k)
                        b = gi % 2
                        for h in range(halves):
                            at = slice(h * W, (h + 1) * W)
                            for p in range(GN):
                                mm = nc.tensor.matmul(cols[b][h][:, p * T:(p + 1) * T], oh_lo[at, b, p, :],
                                                      oh_hi[at, b, p, :], start=True, stop=True)
                        mm.then_inc(used, 1)

                    steps(pe, w, multiply)

                passes(0, True)
                overflow(pe, lambda w: passes(w, False))



def layernorm(v, x, sq, m, var, out_var, add, total):
    v.tensor_reduce(m, x, AX, ALU.add)
    v.drain()
    v.tensor_scalar(m, m, -1.0 / D, None, ALU.mult)
    v.drain()
    v.tensor_tensor(x, x, bc(m, 2, D), ALU.add)
    v.drain()
    v.tensor_tensor(sq, x, x, ALU.mult)
    v.drain()
    v.tensor_reduce(var, sq, AX, ALU.add)
    v.drain()
    v.tensor_scalar(var, var, 1.0 / D, EPS, ALU.mult, ALU.add).then_inc(out_var, add)


def root_inverse(act, x, inc):
    act.activation(x, x, ACT.Ln)
    act.drain()
    act.activation(x, x, ACT.Exp, scale=-0.5).then_inc(inc, 1)


class Spread:

    def __init__(self, g, name, c, A, x):
        self.g, self.A, self.x = g, A, x
        self.split = [g.sb(f"{name}_split{b}", [P, T, 2 * D], F16, c) for b in range(2)]
        self.copy = [g.sb(f"{name}_copy{b}", [P, CHUNK * P], F32, c) for b in range(2)]
        self.new = [g.sb(f"{name}_new{b}", [P, CHUNK, D], F32, c) for b in range(2)]
        self.rest = [g.sb(f"{name}_rest{b}", [P, CHUNK, D], F32, c) for b in range(2)]
        self.wide = [g.ps(f"{name}_wide{b}", [P, CHUNK * P], F32, c) for b in range(2)]
        self.turned = [g.ps(f"{name}_nodes{b}", [P, CHUNK * P], F32, c) for b in range(2)]
        self.product = g.sem(f"{name}_product")
        self.copied = g.sem(f"{name}_copied")
        self.nodes = g.sem(f"{name}_nodes_ready")
        self.made = g.sem(f"{name}_made")
        self.high = g.sem(f"{name}_high")
        self.low = g.sem(f"{name}_rest_ready")
        self.ready = g.sem(f"{name}_split_ready")

    def pe_turn(self, pe, r, c):
        t0, n = CHUNKS[c]
        k = r * NC + c
        pe.wait_ge(self.copied, k + 1)
        pe.wait_ge(self.made, NC + (k if c == 0 else k - 1))
        for j in range(n):
            mm = self.g.nc.tensor.matmul(self.turned[c % 2][:, j * D:(j + 1) * D],
                                         self.copy[c % 2][:, j * P:(j + 1) * P], self.g.comb[:],
                                         start=True, stop=True)
        mm.then_inc(self.nodes, 1)

    def pe_round(self, pe, r, b):
        for c, (t0, n) in enumerate(CHUNKS):
            k = r * NC + c
            pe.wait_ge(self.copied, k if c == 0 else k - 1)
            for s in range(T):
                if c == 0 and s % CHUNK == 0:
                    pe.wait_ge(self.ready, k + s // CHUNK + 1)
                if c > 0 and s == T // 2:
                    self.pe_turn(pe, r, c - 1)
                mm = self.g.nc.tensor.matmul(self.wide[c % 2][:, 0:n * P], self.split[b][:, s, :],
                                             self.A[:, s, t0 * P:(t0 + n) * P], start=(s == 0), stop=(s == T - 1))
            mm.then_inc(self.product, 1)
        self.pe_turn(pe, r, NC - 1)

    def act_split(self, act, j, c, b):
        t0, n = CHUNKS[c]
        act.wait_ge(self.made, j + 1)
        act.activation(self.split[b][:, t0:t0 + n, 0:D], self.new[c % 2][:, 0:n, :], ACT.Copy).then_inc(self.high, 1)
        act.wait_ge(self.low, j + 1)
        act.activation(self.split[b][:, t0:t0 + n, D:2 * D], self.rest[c % 2][:, 0:n, :], ACT.Copy,
                       scale=LOSCALE).then_inc(self.ready, 1)

    def act_round(self, act, r, b, last=False):
        for c, (t0, n) in enumerate(CHUNKS):
            k = r * NC + c
            act.wait_ge(self.product, k + 1)
            act.wait_ge(self.nodes, k if c == 0 else k - 1)
            act.activation(self.copy[c % 2][:, 0:n * P], self.wide[c % 2][:, 0:n * P], ACT.Copy).then_inc(self.copied, 1)
            if not last:
                self.act_split(act, NC + k, c, 1 - b)

    def v_split(self, v, j, c, b):
        t0, n = CHUNKS[c]
        v.wait_ge(self.high, j + 1)
        v.tensor_tensor(self.rest[c % 2][:, 0:n, :], self.new[c % 2][:, 0:n, :], self.split[b][:, t0:t0 + n, 0:D],
                        ALU.subtract).then_inc(self.low, 1)

    def v_round(self, v, r, b, make, last=False):
        for c, (t0, n) in enumerate(CHUNKS):
            k = r * NC + c
            v.wait_ge(self.nodes, k + 1)
            if not last:
                v.wait_ge(self.ready, NC + (k if c == 0 else k - 1))
            frm = self.turned[c % 2][:, 0:n * D].rearrange("p (t f) -> p t f", f=D)
            make(t0, n, frm, self.new[c % 2][:, 0:n, :])
            if not last:
                self.v_split(v, NC + k, c, 1 - b)


def stage_appnp(g, A, X, c):
    nc = g.nc
    with ExitStack() as c:
        sp_ = Spread(g, "appnp", c, A, X)
        H0 = g.sb("h0", [P, T, D], F32, c)
        wb = g.sb("w_b", [D + 1, D], F32, c)
        xt = [g.sb(f"x_turned{b}", [D + 1, CHUNK * P], F32, c) for b in range(2)]
        dl = g.sb("norm_in", [P, 2, T], F32, c)
        on = g.sb("norm_on", [P, 2, T], F32, c)
        c1 = g.sb("c_agg", [P, T], F32, c)
        cl = g.sb("c_agg_last", [P, T], F32, c)
        c2 = g.sb("c_h0", [P, T], F32, c)
        mean = g.sb("ln_mean", [P, T], F32, c)
        var = g.sb("ln_var", [P, T], F32, c)
        loaded = g.sem("appnp_loaded")
        padded = g.sem("appnp_padded")
        degs = g.sem("appnp_degrees")
        roots = g.sem("appnp_norms")
        x_turned = g.sem("appnp_x_turned")
        x_copied = g.sem("appnp_x_copied")
        h0_done = g.sem("appnp_h0")
        h0_read = g.sem("appnp_h0_read")
        var_done = g.sem("appnp_var")
        root_done = g.sem("appnp_root")
        full = (T - 1) * P

        with nc.Block() as block:

            @block.sync
            def _(sp):
                x = g.ins["x"]
                sp.dma_start(X[:, 0:T - 1, :], x[0:full].rearrange("(t p) f -> p t f", p=P)).then_inc(loaded, 16)
                sp.dma_start(wb[0:D, :], g.ins["L0_gnn_W"]).then_inc(loaded, 16)
                sp.dma_start(wb[D:D + 1, :], g.ins["L0_gnn_b"].rearrange("(a b) -> a b", a=1)).then_inc(loaded, 16)
                sp.wait_ge(padded, 1)
                sp.dma_start(X[0:TAIL, T - 1, :], x[full:N]).then_inc(loaded, 16)

            @block.gpsimd
            def _(pool):
                nc.gpsimd.memset(X[:, T - 1, :], 0.0).then_inc(padded, 1)

            @block.tensor
            def _(pe):
                pe.wait_ge(loaded, 64)
                pe.wait_ge(degs, 1)
                for ch, (t0, n) in enumerate(CHUNKS):
                    b = ch % 2
                    if ch >= 2:
                        pe.wait_ge(x_copied, ch - 1)
                    for j in range(n):
                        tr = nc.tensor.transpose(sp_.wide[b][0:D, j * P:(j + 1) * P], X[:, t0 + j, :], g.ident[:])
                    tr.then_inc(x_turned, 1)
                    pe.wait_ge(x_copied, ch + 1)
                    if ch >= 2:
                        pe.wait_ge(h0_read, ch - 1)
                    for j in range(n):
                        mm = nc.tensor.matmul(sp_.turned[b][:, j * D:(j + 1) * D], xt[b][:, j * P:(j + 1) * P], wb[:],
                                              start=True, stop=True)
                    mm.then_inc(h0_done, 1)
                with pe.Fori(0, ROUNDS // 2) as i:
                    sp_.pe_round(pe, i * 2, 0)
                    sp_.pe_round(pe, i * 2 + 1, 1)

            @block.scalar
            def _(act):
                act.wait_ge(degs, 1)
                root_inverse(act, dl[:], roots)
                for ch, (t0, n) in enumerate(CHUNKS):
                    b = ch % 2
                    act.wait_ge(x_turned, ch + 1)
                    if ch >= 2:
                        act.wait_ge(h0_done, ch - 1)
                    act.activation(xt[b][0:D, 0:n * P], sp_.wide[b][0:D, 0:n * P], ACT.Copy).then_inc(x_copied, 1)
                for ch in range(NC):
                    sp_.act_split(act, ch, ch, 0)
                with act.Fori(0, ROUNDS // 2 - 1) as i:
                    sp_.act_round(act, i * 2, 0)
                    sp_.act_round(act, i * 2 + 1, 1)
                sp_.act_round(act, ROUNDS - 2, 0)
                sp_.act_round(act, ROUNDS - 1, 1, last=True)
                act.wait_ge(var_done, 1)
                root_inverse(act, var[:], root_done)

            @block.vector
            def _(v):
                v.memset(xt[0][D:D + 1, :], 1.0)
                v.memset(xt[1][D:D + 1, :], 1.0)
                v.tensor_scalar(dl[:, 0, :], g.dego[:], 1.0, None, ALU.max)
                v.tensor_scalar(dl[:, 1, :], g.deg[:], 1.0, None, ALU.max).then_inc(degs, 1)
                v.tensor_scalar(on[:, 0, :], g.dego[:], 0.0, None, ALU.is_gt)
                v.tensor_scalar(on[:, 1, :], g.deg[:], 0.0, None, ALU.is_gt)
                v.drain()
                v.wait_ge(roots, 1)
                v.tensor_tensor(dl[:], dl[:], on[:], ALU.mult)
                v.drain()
                ns, nd = dl[:, 0, :], dl[:, 1, :]
                v.tensor_scalar(cl[:], nd, 1.0 - ALPHA, None, ALU.mult)
                v.tensor_scalar(c2[:], ns, ALPHA, None, ALU.mult)
                v.drain()
                v.tensor_tensor(c1[:], cl[:], ns, ALU.mult)
                for ch, (t0, n) in enumerate(CHUNKS):
                    v.wait_ge(h0_done, ch + 1)
                    v.tensor_copy(H0[:, t0:t0 + n, :],
                                  sp_.turned[ch % 2][:, 0:n * D].rearrange("p (t f) -> p t f", f=D)).then_inc(h0_read, 1)
                v.drain()
                for ch, (t0, n) in enumerate(CHUNKS):
                    if ch >= 2:
                        v.wait_ge(sp_.ready, ch - 1)
                    v.tensor_tensor(sp_.new[ch % 2][:, 0:n, :], H0[:, t0:t0 + n, :], bc(ns[:, t0:t0 + n], 2, D),
                                    ALU.mult).then_inc(sp_.made, 1)
                    sp_.v_split(v, ch, ch, 0)

                def make(t0, n, frm, to):
                    rest = sp_.rest[(t0 // CHUNK) % 2][:, 0:n, :]
                    v.tensor_tensor(to, frm, bc(c1[:, t0:t0 + n], 2, D), ALU.mult)
                    v.tensor_tensor(rest, H0[:, t0:t0 + n, :], bc(c2[:, t0:t0 + n], 2, D), ALU.mult)
                    v.drain()
                    v.tensor_tensor(to, to, rest, ALU.add).then_inc(sp_.made, 1)

                def make_last(t0, n, frm, to):
                    x = X[:, t0:t0 + n, :]
                    v.tensor_tensor(to, frm, bc(cl[:, t0:t0 + n], 2, D), ALU.mult)
                    v.scalar_tensor_tensor(x, H0[:, t0:t0 + n, :], ALPHA, x, ALU.mult, ALU.add)
                    v.drain()
                    v.tensor_tensor(x, x, to, ALU.add).then_inc(sp_.made, 1)

                with v.Fori(0, ROUNDS // 2 - 1) as i:
                    sp_.v_round(v, i * 2, 0, make)
                    sp_.v_round(v, i * 2 + 1, 1, make)
                sp_.v_round(v, ROUNDS - 2, 0, make)
                v.wait_ge(sp_.ready, NC * ROUNDS)
                sp_.v_round(v, ROUNDS - 1, 1, make_last, last=True)
                v.drain()
                layernorm(v, X[:], H0[:], mean[:], var[:], var_done, 1, 1)
                v.wait_ge(root_done, 1)
                v.tensor_tensor(X[:], X[:], bc(var[:], 2, D), ALU.mult)


def stage_turn(g, A):
    nc = g.nc
    BANK = 8
    groups = [(s, t0, min(BANK, T - t0)) for s in range(T) for t0 in range(s + 1, T, BANK)]
    with ExitStack() as c:
        up = [g.ps(f"turn_up{b}", [P, BANK, P], F16, c) for b in range(2)]
        down = [g.ps(f"turn_down{b}", [P, BANK, P], F16, c) for b in range(2)]
        done = g.sem("turn_done")
        up_moved = g.sem("turn_up_moved")
        down_moved = g.sem("turn_down_moved")
        diagonal = [(t0, min(BANK, T - t0)) for t0 in range(0, T, BANK)]

        with nc.Block() as block:

            @block.tensor
            def _(pe):
                for k, (s, t0, n) in enumerate(groups):
                    if k >= 2:
                        pe.wait_ge(up_moved, k - 1)
                        pe.wait_ge(down_moved, k - 1)
                    for j in range(n):
                        t = t0 + j
                        nc.tensor.transpose(up[k % 2][:, j, :], A[:, s, t * P:(t + 1) * P], g.identh[:])
                        tr = nc.tensor.transpose(down[k % 2][:, j, :], A[:, t, s * P:(s + 1) * P], g.identh[:])
                    tr.then_inc(done, 1)
                for i, (t0, n) in enumerate(diagonal):
                    k = len(groups) + i
                    pe.wait_ge(up_moved, k - 1)
                    for j in range(n):
                        t = t0 + j
                        tr = nc.tensor.transpose(up[k % 2][:, j, :], A[:, t, t * P:(t + 1) * P], g.identh[:])
                    tr.then_inc(done, 1)

            @block.scalar
            def _(act):
                for k, (s, t0, n) in enumerate(groups):
                    act.wait_ge(done, k + 1)
                    act.activation(A[:, t0:t0 + n, s * P:(s + 1) * P], up[k % 2][:, 0:n, :], ACT.Copy).then_inc(up_moved, 1)
                for i, (t0, n) in enumerate(diagonal):
                    k = len(groups) + i
                    act.wait_ge(done, k + 1)
                    for j in range(n):
                        t = t0 + j
                        last = act.activation(A[:, t, t * P:(t + 1) * P], up[k % 2][:, j, :], ACT.Copy)
                    last.then_inc(up_moved, 1)

            @block.vector
            def _(v):
                for k, (s, t0, n) in enumerate(groups):
                    v.wait_ge(done, k + 1)
                    v.tensor_copy(A[:, s, t0 * P:(t0 + n) * P].rearrange("p (t q) -> p t q", q=P),
                                  down[k % 2][:, 0:n, :]).then_inc(down_moved, 1)


def stage_lightgcn(g, A, X):
    nc = g.nc
    with ExitStack() as c:
        sp_ = Spread(g, "light", c, A, X)
        acc = g.sb("light_sum", [P, T, D], F32, c)
        dl = g.sb("light_norm", [P, T], F32, c)
        on = g.sb("light_on", [P, T], F32, c)
        mean = g.sb("light_mean", [P, T], F32, c)
        var = g.sb("light_var", [P, T], F32, c)
        degs = g.sem("light_degrees")
        roots = g.sem("light_norms")
        var_done = g.sem("light_var_done")
        root_done = g.sem("light_root")
        x_done = g.sem("light_x")
        x_out = g.sem("light_x_stored")

        with nc.Block() as block:

            @block.tensor
            def _(pe):
                with pe.Fori(0, (HOPS - 1) // 2) as i:
                    sp_.pe_round(pe, i * 2, 0)
                    sp_.pe_round(pe, i * 2 + 1, 1)
                sp_.pe_round(pe, HOPS - 1, 0)

            @block.scalar
            def _(act):
                act.wait_ge(degs, 1)
                root_inverse(act, dl[:], roots)
                for ch in range(NC):
                    sp_.act_split(act, ch, ch, 0)
                with act.Fori(0, (HOPS - 1) // 2) as i:
                    sp_.act_round(act, i * 2, 0)
                    sp_.act_round(act, i * 2 + 1, 1)
                sp_.act_round(act, HOPS - 1, 0, last=True)
                act.wait_ge(var_done, 1)
                root_inverse(act, var[:], root_done)

            @block.vector
            def _(v):
                v.tensor_scalar(dl[:], g.dego[:], 1.0, None, ALU.max).then_inc(degs, 1)
                v.tensor_scalar(on[:], g.dego[:], 0.0, None, ALU.is_gt)
                v.tensor_copy(acc[:], X[:])
                v.drain()
                v.wait_ge(roots, 1)
                v.tensor_tensor(dl[:], dl[:], dl[:], ALU.mult)
                v.drain()
                v.tensor_tensor(dl[:], dl[:], on[:], ALU.mult)
                v.drain()
                for ch, (t0, n) in enumerate(CHUNKS):
                    if ch >= 2:
                        v.wait_ge(sp_.ready, ch - 1)
                    v.tensor_copy(sp_.new[ch % 2][:, 0:n, :], X[:, t0:t0 + n, :]).then_inc(sp_.made, 1)
                    sp_.v_split(v, ch, ch, 0)

                def make(t0, n, frm, to):
                    a = acc[:, t0:t0 + n, :]
                    v.tensor_tensor(to, frm, bc(dl[:, t0:t0 + n], 2, D), ALU.mult).then_inc(sp_.made, 1)
                    v.drain()
                    v.tensor_tensor(a, a, to, ALU.add)

                with v.Fori(0, (HOPS - 1) // 2) as i:
                    sp_.v_round(v, i * 2, 0, make)
                    sp_.v_round(v, i * 2 + 1, 1, make)
                v.wait_ge(sp_.ready, NC * HOPS)
                sp_.v_round(v, HOPS - 1, 0, make, last=True)
                v.drain()
                v.scalar_tensor_tensor(X[:], acc[:], 1.0 / (HOPS + 1), X[:], ALU.mult, ALU.add)
                v.drain()
                layernorm(v, X[:], acc[:], mean[:], var[:], var_done, 1, 1)
                v.wait_ge(root_done, 1)
                v.tensor_tensor(X[:], X[:], bc(var[:], 2, D), ALU.mult).then_inc(x_done, 1)

            @block.sync
            def _(sp):
                rows = g.x2_dram.rearrange("(t p) f -> p t f", p=P)
                with nc.allow_non_contiguous_dma(reason="one degree beside each row, once"):
                    sp.dma_start(rows[:, :, D:D + 1], g.dego[:].unsqueeze(2)).then_inc(x_out, 16)
                hold(sp, x_done, 1)
                sp.dma_start(rows[:, :, 0:D], X[:]).then_inc(x_out, 16)
                sp.wait_ge(x_out, 32)



IDS = 4


class Lists:

    def __init__(self, g, name, c, table, width):
        self.g, self.table, self.width = g, table, width
        self.ring = g.sb(f"{name}_ids", [P, IDS, S], I32, c)
        self.ids = [g.sb(f"{name}_ids{h}", [P, HS], I32, c) for h in range(2)]
        self.rows = g.sb(f"{name}_rows", [P, S, width], F32, c)
        self.landed = g.sem(f"{name}_ids_landed")
        self.taken = g.sem(f"{name}_ids_taken")
        self.half = [g.sem(f"{name}_rows{h}") for h in range(2)]
        self.free = [g.sem(f"{name}_free{h}") for h in range(2)]

    def counter(self, eng, name):
        k = eng.alloc_register(f"{name}_blocks")
        eng.reg_mov(k, 0)
        return k

    def count(self, eng, t):
        return eng.value_load(self.g.nblk[0:1, bass.ds(t, 1)], min_val=MINBLK, max_val=BLOCKS)

    def sp_walk(self, sp, k):
        g = self.g
        at = sp.alloc_register(f"sp_at_{self.ring.name}")
        sp.reg_mov(at, 0)
        with sp.Fori(0, T) as t:
            n = self.count(sp, t)
            wins = sp.value_load(g.nwin[0:1, bass.ds(t, 1)], min_val=1, max_val=BLOCKS)
            base = sp.snap(at)
            with sp.Fori(0, n) as j:
                kk = sp.snap(k)
                block = sp.snap(base + j, min_val=0, max_val=BLOCKS - 1)
                slot = sp.snap(kk % IDS, min_val=0, max_val=IDS - 1)
                hold(sp, self.taken, kk + 1)
                hold(sp, self.landed, kk * 16)
                sp.dma_start(self.ring[:, bass.ds(slot, 1), :].rearrange("p a s -> p (a s)"),
                             g.ids_dram[bass.ds(block * (P * S), P * S)].rearrange("(p s) -> p s", s=S)
                             ).then_inc(self.landed, 16)
                sp.reg_add(k, k, 1)
            sp.reg_add(at, at, wins * WB)
        sp.free_register(at)

    def pool_begin(self, pool):
        pool.nop().then_inc(self.taken, IDS)

    def pool_walk(self, pool, k):
        g = self.g
        with pool.Fori(0, T) as t:
            n = self.count(pool, t)
            with pool.Fori(0, n) as _j:
                kk = pool.snap(k)
                slot = pool.snap(kk % IDS, min_val=0, max_val=IDS - 1)
                hold(pool, self.landed, (kk + 1) * 16)
                for h in range(2):
                    hold(pool, self.half[h], kk * (16 * HS))
                    copy = g.nc.gpsimd.tensor_copy(
                        self.ids[h][:], self.ring[:, bass.ds(slot, 1), h * HS:(h + 1) * HS].rearrange("p a s -> p (a s)"))
                    if h == 1:
                        copy.then_inc(self.taken, 1)
                    pool.drain()
                    hold(pool, self.free[h], kk)
                    for s in range(HS):
                        g.nc.gpsimd.indirect_dma_start(
                            out=self.rows[:, h * HS + s, :], out_offset=None, in_=self.table,
                            in_offset=bass.IndirectOffsetOnAxis(ap=self.ids[h][:, s:s + 1], axis=0)
                        ).then_inc(self.half[h], 16)
                pool.reg_add(k, k, 1)


def stage_sage(g, XS, sdego):
    nc = g.nc
    I = g.ins
    with ExitStack() as c:
        H = g.sb("h", [P, T, D], F32, c)
        x2 = g.sb("x2_sorted", [P, T, D + 1], F32, c)
        lists = Lists(g, "sage", c, g.h_tab, D)
        wl_n = g.sb("wl_rows", [D, LAYERS, 2 * D], F32, c)
        wr_n = g.sb("wr_rows", [D, LAYERS, D], F32, c)
        ad_n = g.sb("adapter_rows", [D, D], F32, c)
        w1_n = g.sb("w1_rows", [P, HID // P, D], F32, c)
        w2_n = g.sb("w2_rows", [D, HID], F32, c)
        WL = g.sb("wl", [2 * D, LAYERS, D], F32, c)
        WR = g.sb("wr", [D + 1, LAYERS, 2 * D], F32, c)
        adb = g.sb("adapter_b", [D + 1, D], F32, c)
        lng = g.sb("ln_g", [P, LAYERS, D], F32, c)
        wl = g.sb("wl_now", [2 * D, D], F32, c)
        wr = g.sb("wr_now", [D + 1, 2 * D], F32, c)
        gain = g.sb("gain_now", [P, D], F32, c)
        W1 = g.sb("w1", [D + 1, HID], F32, c)
        W2 = g.sb("w2", [P, HID // P, D], F32, c)
        b2 = g.sb("b2", [1, D], F32, c)
        ones = g.sb("sage_ones", [1, P], F32, c)
        g2 = g.sb("mlp_g", [P, HID], F32, c)
        be2 = g.sb("mlp_be", [P, HID], F32, c)
        neg = g.sb("neg_big", [NP - N, D], F32, c)
        valid = g.sb("valid", [P, T], F32, c)
        rdeg = g.sb("rdeg", [P, T], F32, c)
        rem = g.sb("left", [P, 1], F32, c)
        mask = g.sb("row_mask", [P, S], F32, c)
        masked = g.sb("masked_rows", [P, S, D], F32, c)
        top = [g.sb(f"half_max{h}", [P, D], F32, c) for h in range(2)]
        part = g.sb("block_sum", [P, D], F32, c)
        acc_max = g.sb("acc_max", [P, D], F32, c)
        acc_sum = g.sb("acc_sum", [P, D], F32, c)
        cat = g.sb("cat", [P, 3 * D], F32, c)
        catT = g.sb("cat_turned", [P, P], F32, c)
        hT = g.sb("h_turned", [D + 1, P], F32, c)
        stats = g.sb("bn_stats", [P, 6], F32, c)
        mv = g.sb("mean_var", [P, 2], F32, c)
        root = g.sb("root", [P, 1], F32, c)
        y = g.sb("y", [P, D], F32, c)
        z = g.sb("z", [P, D], F32, c)
        e = g.sb("e", [P, D], F32, c)
        hc = g.sb("h_tile", [P, D], F32, c)
        em = g.sb("mlp_e", [P, HID], F32, c)
        zm = g.sb("mlp_z", [P, HID], F32, c)
        zT = g.sb("mlp_z_turned", [P, HID], F32, c)
        mean = g.sb("sage_mean", [P, T], F32, c)
        var = g.sb("sage_var", [P, T], F32, c)
        ps_t = g.ps("sage_turned", [P, 512], F32, c)
        ps_o = g.ps("sage_out", [P, 512], F32, c)
        ps_w = [g.ps(f"sage_w{b}", [P, 512], F32, c) for b in range(2)]
        loaded = g.sem("sage_weights")
        neg_set = g.sem("sage_neg_set")
        neg_out = g.sem("sage_neg_out")
        x_in = g.sem("sage_x_gathered")
        w_turned = g.sem("sage_w_turned")
        w_moved = g.sem("sage_w_moved")
        prepared = g.sem("sage_prepared")
        scattered = g.sem("sage_scattered")
        cat_ready = g.sem("sage_cat")
        turned = g.sem("sage_cat_turned")
        copied = g.sem("sage_cat_copied")
        out_ready = g.sem("sage_conv")
        var_ready = g.sem("sage_var_ready")
        root_ready = g.sem("sage_root")
        z_ready = g.sem("sage_z")
        e_ready = g.sem("sage_e")
        h_ready = g.sem("sage_h")
        m_h = g.sem("mlp_h")
        m_t = g.sem("mlp_h_turned")
        m_c = g.sem("mlp_h_copied")
        m_1 = g.sem("mlp_hidden")
        m_e = g.sem("mlp_exp")
        m_v = g.sem("mlp_var")
        m_r = g.sem("mlp_root")
        m_z = g.sem("mlp_normed")
        m_zt = g.sem("mlp_z_turned_ready")
        m_zc = g.sem("mlp_z_copied")
        m_o = g.sem("mlp_out")
        f_var = g.sem("sage_final_var")
        f_root = g.sem("sage_final_root")
        LOADS = 15
        turns = [(wl_n[:, l, :], WL[:, l, :], D, 2 * D) for l in range(LAYERS)]
        turns += [(wr_n[:, l, :], WR[0:D, l, 0:D], D, D) for l in range(LAYERS)]
        turns += [(ad_n[:], WR[0:D, 0, D:2 * D], D, D)]
        turns += [(w1_n[:, i, :], W1[0:D, i * P:(i + 1) * P], P, D) for i in range(HID // P)]
        turns += [(w2_n[:, i * P:(i + 1) * P], W2[:, i, :], D, P) for i in range(HID // P)]

        with nc.Block() as block:

            @block.sync
            def _(sp):
                def load(to, frm):
                    sp.dma_start(to, frm).then_inc(loaded, 16)

                def row(ap):
                    return ap.rearrange("(a b) -> a b", a=1)

                load(wl_n[:], I["L2_gnn_conv_wl"].rearrange("l o i -> o l i"))
                load(wr_n[:], I["L2_gnn_conv_wr"].rearrange("l o i -> o l i"))
                load(ad_n[:], I["L2_gnn_adapter_w"])
                load(w1_n[:], I["L2_gnn_mlp_w1"].rearrange("(a p) i -> p a i", p=P))
                load(w2_n[:], I["L2_gnn_mlp_w2"])
                load(W1[D:D + 1, :], row(I["L2_gnn_mlp_b1"]))
                load(b2[:], row(I["L2_gnn_mlp_b2"]))
                load(g2[:], row(I["L2_gnn_mlp_ln_g"]).broadcast_to([P, HID]))
                load(be2[:], row(I["L2_gnn_mlp_ln_b"]).broadcast_to([P, HID]))
                load(adb[D:D + 1, :], row(I["L2_gnn_adapter_b"]))
                load(lng[:], I["L2_gnn_ln_g"].unsqueeze(0).broadcast_to([P, LAYERS, D]))
                load(WR[D:D + 1, :, 0:D], I["L2_gnn_conv_bl"].unsqueeze(0))
                load(WR[D:D + 1, :, D:2 * D], I["L2_gnn_ln_b"].unsqueeze(0))
                sp.wait_ge(neg_set, 1)
                sp.dma_start(g.h_tab[N:NP, :], neg[:]).then_inc(neg_out, 16)
                k = lists.counter(sp, "sage_sp")
                with sp.Fori(0, LAYERS) as _l:
                    lists.sp_walk(sp, k)

            @block.gpsimd
            def _(pool):
                for t in range(T):
                    nc.gpsimd.indirect_dma_start(
                        out=x2[:, t, :], out_offset=None, in_=g.x2_dram,
                        in_offset=bass.IndirectOffsetOnAxis(ap=g.sorted[:, t, 2:3], axis=0)).then_inc(x_in, 16)
                lists.pool_begin(pool)
                k = lists.counter(pool, "sage_pool")
                pool.wait_ge(neg_out, 16)
                with pool.Fori(0, LAYERS) as l:
                    pool.wait_ge(prepared, 1)
                    hold(pool, h_ready, l * T)
                    for h in range(2):
                        hold(pool, lists.half[h], pool.snap(k) * (16 * HS))
                    for t in range(T):
                        nc.gpsimd.indirect_dma_start(
                            out=g.h_tab, out_offset=bass.IndirectOffsetOnAxis(ap=g.sorted[:, t, 2:3], axis=0),
                            in_=H[:, t, :], in_offset=None, bounds_check=N - 1, oob_is_err=False
                        ).then_inc(scattered, 16)
                    hold(pool, scattered, (l + 1) * (16 * T))
                    lists.pool_walk(pool, k)

            @block.tensor
            def _(pe):
                pe.wait_ge(loaded, 16 * 13)
                for i, (frm, _to, rows, cols) in enumerate(turns):
                    if i >= 2:
                        pe.wait_ge(w_moved, i - 1)
                    nc.tensor.transpose(ps_w[i % 2][0:cols, 0:rows], frm, g.ident[0:rows, 0:rows]).then_inc(w_turned, 1)
                with pe.Fori(0, LAYERS) as l:
                    with pe.Fori(0, T) as t:
                        q = pe.snap(l * T + t)
                        pe.wait_ge(cat_ready, q + 1)
                        nc.tensor.transpose(ps_t[:, 0:P], cat[:, 0:2 * D], g.ident[:])
                        nc.tensor.transpose(ps_t[0:D, P:2 * P], cat[:, 2 * D:3 * D], g.ident[:]).then_inc(turned, 1)
                        pe.wait_ge(copied, q + 1)
                        pe.wait_ge(z_ready, q)
                        nc.tensor.matmul(ps_o[:, 0:2 * D], hT[:], wr[:], start=True, stop=False, skip_group_check=True)
                        nc.tensor.matmul(ps_o[:, 0:D], catT[:], wl[:], start=False, stop=True,
                                         skip_group_check=True).then_inc(out_ready, 1)
                with pe.Fori(0, T) as t:
                    hold(pe, m_h, t + 1)
                    nc.tensor.transpose(ps_t[0:D, 0:P], hc[:], g.ident[:]).then_inc(m_t, 1)
                    pe.wait_ge(m_c, t + 1)
                    nc.tensor.matmul(ps_w[0][:, 0:HID], hT[:], W1[:], start=True, stop=True).then_inc(m_1, 1)
                    pe.wait_ge(m_z, t + 1)
                    for i in range(HID // P):
                        tr = nc.tensor.transpose(ps_w[1][:, i * P:(i + 1) * P], zm[:, i * P:(i + 1) * P], g.ident[:])
                    tr.then_inc(m_zt, 1)
                    pe.wait_ge(m_zc, t + 1)
                    for i in range(HID // P):
                        nc.tensor.matmul(ps_o[:, 0:D], zT[:, i * P:(i + 1) * P], W2[:, i, :], start=(i == 0), stop=False)
                    nc.tensor.matmul(ps_o[:, 0:D], ones[:], b2[:], start=False, stop=True).then_inc(m_o, 1)

            @block.scalar
            def _(act):
                for i, (_frm, to, rows, cols) in enumerate(turns):
                    act.wait_ge(w_turned, i + 1)
                    act.activation(to, ps_w[i % 2][0:cols, 0:rows], ACT.Copy).then_inc(w_moved, 1)

                def conv(q):
                    act.wait_ge(turned, q + 1)
                    act.activation(catT[:], ps_t[:, 0:P], ACT.Copy)
                    act.activation(hT[0:D, :], ps_t[0:D, P:2 * P], ACT.Copy).then_inc(copied, 1)

                def post(q):
                    act.wait_ge(var_ready, q + 1)
                    act.activation(root[:], mv[:, 1:2], ACT.Ln)
                    act.drain()
                    act.activation(root[:], root[:], ACT.Exp, scale=-0.5).then_inc(root_ready, 1)
                    act.wait_ge(z_ready, q + 1)
                    act.activation(e[:], z[:], ACT.Exp, scale=-1.0).then_inc(e_ready, 1)

                with act.Fori(0, LAYERS) as l:
                    with act.Fori(0, T) as t:
                        q = act.snap(l * T + t)
                        conv(q)
                        post(q)
                with act.Fori(0, T) as t:
                    act.wait_ge(m_t, t + 1)
                    act.activation(hT[0:D, :], ps_t[0:D, 0:P], ACT.Copy).then_inc(m_c, 1)
                    act.wait_ge(m_1, t + 1)
                    act.activation(em[:], ps_w[0][:, 0:HID], ACT.Exp, scale=-1.0).then_inc(m_e, 1)
                    act.wait_ge(m_v, t + 1)
                    act.activation(root[:], mv[:, 1:2], ACT.Ln)
                    act.drain()
                    act.activation(root[:], root[:], ACT.Exp, scale=-0.5).then_inc(m_r, 1)
                    act.wait_ge(m_zt, t + 1)
                    act.activation(zT[:], ps_w[1][:, 0:HID], ACT.Copy).then_inc(m_zc, 1)
                act.wait_ge(f_var, 1)
                root_inverse(act, var[:], f_root)

            @block.vector
            def _(v):
                v.memset(neg[:], -BIG).then_inc(neg_set, 1)
                v.memset(ones[:], 1.0)
                v.memset(hT[D:D + 1, :], 1.0)
                v.tensor_scalar(valid[:], g.sdeg[:], 0.0, None, ALU.is_gt)
                v.tensor_scalar(rdeg[:], g.sdeg[:], 1.0, None, ALU.max)
                v.drain()
                v.reciprocal(rdeg[:], rdeg[:])
                v.wait_ge(loaded, 16 * 13)
                for l in range(1, LAYERS):
                    v.tensor_copy(WR[0:D, l, D:2 * D], g.ident[0:D, 0:D])
                v.tensor_tensor(WR[D:D + 1, 0, D:2 * D], WR[D:D + 1, 0, D:2 * D], adb[D:D + 1, :], ALU.add)
                v.wait_ge(w_moved, len(turns))
                v.wait_ge(x_in, 16 * T)
                v.tensor_copy(XS[:], x2[:, :, 0:D])
                v.tensor_copy(sdego[:], x2[:, :, D])
                v.tensor_copy(H[:], x2[:, :, 0:D]).then_inc(prepared, 1)
                k = lists.counter(v, "sage_v")

                def take(kk, h):
                    v.wait_ge(lists.half[h], (kk + 1) * (16 * HS))
                    rows = lists.rows[:, h * HS:(h + 1) * HS, :]
                    v.tensor_reduce(top[h][:], rows.rearrange("p s f -> p f s"), AX, ALU.max)
                    v.tensor_tensor(masked[:, h * HS:(h + 1) * HS, :], rows, bc(mask[:, h * HS:(h + 1) * HS], 2, D),
                                    ALU.mult).then_inc(lists.free[h], 1)

                def post_stats(q):
                    v.wait_ge(out_ready, q)
                    v.bn_stats(stats[:], ps_o[:, 0:D])
                    v.drain()
                    v.bn_aggr(mv[:], stats[:])
                    v.drain()
                    v.tensor_scalar(mv[:, 1:2], mv[:, 1:2], EPS, None, ALU.add).then_inc(var_ready, 1)

                def post_norm(q):
                    v.wait_ge(root_ready, q)
                    v.tensor_scalar(y[:], ps_o[:, 0:D], mv[:, 0:1], root[:, 0:1], ALU.subtract, ALU.mult)
                    v.drain()
                    v.tensor_tensor(y[:], y[:], gain[:], ALU.mult)
                    v.drain()
                    v.tensor_tensor(z[:], y[:], ps_o[:, D:2 * D], ALU.add).then_inc(z_ready, 1)

                def post_silu(q, t):
                    v.wait_ge(e_ready, q)
                    v.tensor_scalar(e[:], e[:], 1.0, None, ALU.add)
                    v.drain()
                    v.reciprocal(e[:], e[:])
                    v.drain()
                    v.tensor_tensor(H[:, bass.ds(t, 1), :].rearrange("p a f -> p (a f)"), z[:], e[:],
                                    ALU.mult).then_inc(h_ready, 1)

                def tile_walk(l, t, first):
                    q = v.snap(l * T + t)
                    n = lists.count(v, t)
                    v.tensor_copy(rem[:], g.sdeg[:, bass.ds(t, 1)])
                    v.drain()
                    v.tensor_scalar(mask[:], g.slot[:, 0:S], rem[:, 0:1], None, ALU.is_lt)
                    v.drain()
                    kk = v.snap(k)
                    take(kk, 0)
                    if not first:
                        post_stats(q)
                    take(kk, 1)
                    if not first:
                        post_norm(q)
                    v.drain()
                    v.tensor_tensor(acc_max[:], top[0][:], top[1][:], ALU.max)
                    v.tensor_reduce(acc_sum[:], masked[:].rearrange("p s f -> p f s"), AX, ALU.add)
                    v.reg_add(k, k, 1)
                    with v.Fori(1, n) as _j:
                        kk = v.snap(k)
                        v.tensor_scalar(rem[:], rem[:], float(-S), None, ALU.add)
                        v.drain()
                        v.tensor_scalar(mask[:], g.slot[:, 0:S], rem[:, 0:1], None, ALU.is_lt)
                        v.drain()
                        take(kk, 0)
                        take(kk, 1)
                        v.drain()
                        v.tensor_reduce(part[:], masked[:].rearrange("p s f -> p f s"), AX, ALU.add)
                        v.tensor_tensor(acc_max[:], acc_max[:], top[0][:], ALU.max)
                        v.drain()
                        v.tensor_tensor(acc_max[:], acc_max[:], top[1][:], ALU.max)
                        v.tensor_tensor(acc_sum[:], acc_sum[:], part[:], ALU.add)
                        v.reg_add(k, k, 1)
                    if not first:
                        post_silu(q, t - 1)
                    v.drain()
                    v.wait_ge(turned, q)
                    v.tensor_scalar(cat[:, 0:D], acc_max[:], valid[:, bass.ds(t, 1)], None, ALU.mult)
                    v.tensor_scalar(cat[:, D:2 * D], acc_sum[:], rdeg[:, bass.ds(t, 1)], None, ALU.mult)
                    v.tensor_copy(cat[:, 2 * D:3 * D], H[:, bass.ds(t, 1), :].rearrange("p a f -> p (a f)")
                                  ).then_inc(cat_ready, 1)

                with v.Fori(0, LAYERS) as l:
                    v.drain()
                    at = bass.ds(l, 1)
                    v.tensor_copy(wl[:], WL[:, at, :].rearrange("p a f -> p (a f)"))
                    v.tensor_copy(wr[:], WR[:, at, :].rearrange("p a f -> p (a f)"))
                    v.tensor_copy(gain[:], lng[:, at, :].rearrange("p a f -> p (a f)"))
                    tile_walk(l, 0, True)
                    with v.Fori(1, T) as t:
                        tile_walk(l, t, False)
                    q = v.snap((l + 1) * T)
                    post_stats(q)
                    post_norm(q)
                    post_silu(q, T - 1)
                v.drain()
                with v.Fori(0, T) as t:
                    v.tensor_copy(hc[:], H[:, bass.ds(t, 1), :].rearrange("p a f -> p (a f)")).then_inc(m_h, 1)
                    v.wait_ge(m_e, t + 1)
                    v.tensor_scalar(em[:], em[:], 1.0, None, ALU.add)
                    v.drain()
                    v.reciprocal(em[:], em[:])
                    v.drain()
                    v.tensor_tensor(zm[:], em[:], ps_w[0][:, 0:HID], ALU.mult)
                    v.drain()
                    v.bn_stats(stats[:], zm[:])
                    v.drain()
                    v.bn_aggr(mv[:], stats[:])
                    v.drain()
                    v.tensor_scalar(mv[:, 1:2], mv[:, 1:2], EPS, None, ALU.add).then_inc(m_v, 1)
                    v.wait_ge(m_r, t + 1)
                    v.tensor_scalar(zm[:], zm[:], mv[:, 0:1], root[:, 0:1], ALU.subtract, ALU.mult)
                    v.drain()
                    v.tensor_tensor(zm[:], zm[:], g2[:], ALU.mult)
                    v.drain()
                    v.tensor_tensor(zm[:], zm[:], be2[:], ALU.add).then_inc(m_z, 1)
                    v.wait_ge(m_o, t + 1)
                    x = XS[:, bass.ds(t, 1), :].rearrange("p a f -> p (a f)")
                    v.tensor_tensor(x, x, ps_o[:, 0:D], ALU.add)
                    v.drain()
                layernorm(v, XS[:], H[:], mean[:], var[:], f_var, 1, 1)
                v.wait_ge(f_root, 1)
                v.tensor_tensor(XS[:], XS[:], bc(var[:], 2, D), ALU.mult)



def flat(ap):
    return ap.rearrange("p a f -> p (a f)")


def stage_sheaf(g, XS, sdego):
    nc = g.nc
    I = g.ins
    M = 2 * S
    GROUPS = -(-T // S)
    OT = GROUPS * S
    with ExitStack() as c:
        lists = Lists(g, "sheaf", c, g.t_tab, TW)
        own = g.sb("own_rows", [P, OT, TW], F32, c)
        agg = g.sb("agg", [P, OT, D], F32, c)
        w1r = g.sb("sheaf_w1", [D, DD], F32, c)
        w2r = g.sb("sheaf_w2", [D, HH], F32, c)
        K = g.sb("sheaf_k", [D, D], F32, c)
        m1 = g.sb("mlp1_rows", [HH, 2 * D], F32, c)
        PQ = g.sb("pq", [D + 1, 2 * HH], F32, c)
        m2 = g.sb("mlp2", [P, NPAR, HH], F32, c)
        mb2 = g.sb("mlp2_b", [P, NPAR], F32, c)
        eps = g.sb("epsilons", [P, DD], F32, c)
        coef = g.sb("coefficients", [P, DD], F32, c)
        xt = [g.sb(f"x3_turned{b}", [D, CHUNK * P], F32, c) for b in range(2)]
        xft = [g.sb(f"xf_turned{b}", [D + 1, CHUNK * P], F32, c) for b in range(2)]
        zrow = g.sb("zero_rows", [NP - N, TW], F32, c)
        pq = g.sb("block_pq", [P, S, 2 * HH + 1], F32, c)
        xj = g.sb("block_x", [P, HH, S, DD], F32, c)
        hid = g.sb("hidden", [P, M, HH], F32, c)
        prod = g.sb("hidden_products", [P, M * NPAR, HH], F32, c)
        par = g.sb("params", [P, M, NPAR], F32, c)
        V = g.sb("lower", [P, M, DD, DD], F32, c)
        U = g.sb("orthogonal", [P, M, DD, DD], F32, c)
        tmp = g.sb("column_products", [P, M, DD, DD], F32, c)
        dots = g.sb("dots", [P, M, DD], F32, c)
        inv = g.sb("inverse_norm", [P, M], F32, c)
        nn = g.sb("norms", [P, M, DD], F32, c)
        mm4 = g.sb("map_products", [P, DD * S * DD, DD], F32, c)
        maps = g.sb("maps", [P, DD, S, DD], F32, c)
        wts = g.sb("edge_weights", [P, S], F32, c)
        rw = g.sb("weighted_norms", [P, S, DD], F32, c)
        pm = g.sb("message_products", [P, D, S * DD], F32, c)
        part = g.sb("message_sum", [P, D], F32, c)
        rem = g.sb("sheaf_left", [P, 1], F32, c)
        mask = g.sb("sheaf_mask", [P, S], F32, c)
        dis = g.sb("dis", [P, T], F32, c)
        mean = g.sb("sheaf_mean", [P, T], F32, c)
        var = g.sb("sheaf_var", [P, T], F32, c)
        el = g.sb("elu", [P, T, D], F32, c)
        ps_a = [g.ps(f"sheaf_a{b}", [P, 512], F32, c) for b in range(2)]
        ps_b = [g.ps(f"sheaf_b{b}", [P, 512], F32, c) for b in range(2)]
        loaded = g.sem("sheaf_weights")
        z_set = g.sem("sheaf_zero_set")
        z_out = g.sem("sheaf_zero_out")
        deg_ready = g.sem("sheaf_degrees")
        dis_ready = g.sem("sheaf_dis")
        k_ready = g.sem("sheaf_k_ready")
        w_turned = g.sem("sheaf_w_turned")
        w_moved = g.sem("sheaf_w_moved")
        x_turned = g.sem("sheaf_x_turned")
        x_copied = g.sem("sheaf_x_copied")
        f_done = g.sem("sheaf_xf_turned")
        f_copied = g.sem("sheaf_xf_copied")
        rows_done = g.sem("sheaf_rows")
        rows_read = g.sem("sheaf_rows_read")
        table_ready = g.sem("sheaf_own_ready")
        scattered = g.sem("sheaf_table_out")
        edges_done = g.sem("sheaf_edges_done")
        nn_ready = g.sem("sheaf_norms")
        rs_ready = g.sem("sheaf_roots")
        e_in = g.sem("sheaf_exp_in")
        e_out = g.sem("sheaf_exp_out")
        f_var = g.sem("final_var")
        f_root = g.sem("final_root")
        final = g.sem("final_ready")
        stored = g.sem("final_stored")
        LOADS = 2 * DD + 6

        with nc.Block() as block:

            @block.sync
            def _(sp):
                def load(to, frm):
                    sp.dma_start(to, frm).then_inc(loaded, 16)

                def row(ap):
                    return ap.rearrange("(a b) -> a b", a=1)

                for d in range(DD):
                    load(w1r[d * HH:(d + 1) * HH, :], I["L3_gnn_W1"][d:d + 1, :].broadcast_to([HH, DD]))
                    load(w2r[d * HH:(d + 1) * HH, :], I["L3_gnn_W2"])
                load(m1[:], I["L3_gnn_mlp1_w"])
                load(PQ[D:D + 1, 0:HH], row(I["L3_gnn_mlp1_b"]))
                load(m2[:], I["L3_gnn_mlp2_w"].unsqueeze(0).broadcast_to([P, NPAR, HH]))
                load(mb2[:], row(I["L3_gnn_mlp2_b"]).broadcast_to([P, NPAR]))
                load(eps[:], row(I["L3_gnn_epsilons"]).broadcast_to([P, DD]))
                sp.wait_ge(z_set, 1)
                load(PQ[D:D + 1, HH:2 * HH], zrow[0:1, 0:HH])
                sp.dma_start(g.t_tab[N:NP, :], zrow[:]).then_inc(z_out, 16)
                k = lists.counter(sp, "sheaf_sp")
                lists.sp_walk(sp, k)

            @block.gpsimd
            def _(pool):
                lists.pool_begin(pool)
                k = lists.counter(pool, "sheaf_pool")
                pool.wait_ge(z_out, 16)
                pool.wait_ge(table_ready, 1)
                for t in range(T):
                    nc.gpsimd.indirect_dma_start(
                        out=g.t_tab, out_offset=bass.IndirectOffsetOnAxis(ap=g.sorted[:, t, 2:3], axis=0),
                        in_=own[:, t, :], in_offset=None, bounds_check=N - 1, oob_is_err=False
                    ).then_inc(scattered, 16)
                pool.wait_ge(scattered, 16 * T)
                lists.pool_walk(pool, k)
                pool.wait_ge(final, 1)
                for t in range(T):
                    nc.gpsimd.indirect_dma_start(
                        out=g.out, out_offset=bass.IndirectOffsetOnAxis(ap=g.sorted[:, t, 2:3], axis=0),
                        in_=XS[:, t, :], in_offset=None, bounds_check=N - 1, oob_is_err=False
                    ).then_inc(stored, 16)
                pool.wait_ge(stored, 16 * T)

            @block.tensor
            def _(pe):
                pe.wait_ge(loaded, 16 * LOADS)
                for i in range(2):
                    nc.tensor.transpose(ps_a[i][0:D, 0:HH], m1[:, i * D:(i + 1) * D], g.ident[0:HH, 0:HH]).then_inc(w_turned, 1)
                pe.wait_ge(w_moved, 2)
                pe.wait_ge(k_ready, 1)
                for ch, (t0, n) in enumerate(CHUNKS):
                    b = ch % 2
                    for j in range(n):
                        tr = nc.tensor.transpose(ps_a[b][0:D, j * P:(j + 1) * P], XS[:, t0 + j, :], g.ident[:])
                    tr.then_inc(x_turned, 1)
                    pe.wait_ge(x_copied, ch + 1)
                    nc.tensor.matmul(ps_a[b][0:D, 0:n * P], K[:], xt[b][:, 0:n * P], start=True, stop=True).then_inc(f_done, 1)
                    pe.wait_ge(f_copied, ch + 1)
                    if ch >= 2:
                        pe.wait_ge(rows_read, ch - 1)
                    for j in range(n):
                        at = slice(j * P, (j + 1) * P)
                        nc.tensor.matmul(ps_b[b][:, j * P:j * P + D], xt[b][:, at], K[:], start=True, stop=True)
                        mm = nc.tensor.matmul(ps_b[b][:, j * P + D:j * P + D + 2 * HH], xft[b][:, at], PQ[:],
                                              start=True, stop=True)
                    mm.then_inc(rows_done, 1)

            @block.scalar
            def _(act):
                for i in range(2):
                    act.wait_ge(w_turned, i + 1)
                    act.activation(PQ[0:D, i * HH:(i + 1) * HH], ps_a[i][0:D, 0:HH], ACT.Copy).then_inc(w_moved, 1)
                act.wait_ge(deg_ready, 1)
                root_inverse(act, dis[:], dis_ready)
                act.activation(coef[:], eps[:], ACT.Exp, scale=2.0).then_inc(dis_ready, 1)
                for ch, (t0, n) in enumerate(CHUNKS):
                    b = ch % 2
                    act.wait_ge(x_turned, ch + 1)
                    if ch >= 2:
                        act.wait_ge(rows_done, ch - 1)
                    act.activation(xt[b][:, 0:n * P], ps_a[b][0:D, 0:n * P], ACT.Copy).then_inc(x_copied, 1)
                    act.wait_ge(f_done, ch + 1)
                    act.activation(xft[b][0:D, 0:n * P], ps_a[b][0:D, 0:n * P], ACT.Copy).then_inc(f_copied, 1)

                def roots(count):
                    act.wait_ge(nn_ready, count + 1)
                    act.activation(nn[:], nn[:], ACT.Ln)
                    act.drain()
                    act.activation(nn[:], nn[:], ACT.Exp, scale=-0.5).then_inc(rs_ready, 1)

                for i in range(GROUPS):
                    roots(i)
                k = lists.counter(act, "sheaf_act")
                with act.Fori(0, T) as t:
                    n = lists.count(act, t)
                    with act.Fori(0, n) as _j:
                        kk = act.snap(k)
                        act.wait_ge(edges_done, kk + GROUPS)
                        for h in range(2):
                            act.wait_ge(lists.half[h], (kk + 1) * (16 * HS))
                            at = slice(h * HS, (h + 1) * HS)
                            rows = lists.rows[:, at, :]
                            act.activation(xj[:, :, at, :].rearrange("p h s b -> p s b h"),
                                           rows[:, :, 0:D].rearrange("p s (b h) -> p s b h", b=DD), ACT.Copy)
                            act.activation(pq[:, at, :], rows[:, :, D:TW], ACT.Copy).then_inc(lists.free[h], 1)
                        roots(kk + GROUPS)
                        act.reg_add(k, k, 1)
                act.wait_ge(e_in, 1)
                act.activation(el[:], el[:], ACT.Exp).then_inc(e_out, 1)
                act.wait_ge(f_var, 1)
                root_inverse(act, var[:], f_root)

            @block.vector
            def _(v):
                def tt(to, a, b, op):
                    return v.tensor_tensor(to, a, b, op)

                v.memset(zrow[:], 0.0).then_inc(z_set, 1)
                v.memset(xft[0][D:D + 1, :], 1.0)
                v.memset(xft[1][D:D + 1, :], 1.0)
                v.memset(own[:, T:OT, :], 0.0)
                v.memset(V[:], 0.0)
                v.drain()
                for i in range(DD):
                    v.memset(V[:, :, i, i], 1.0)
                v.tensor_scalar(dis[:], sdego[:], 1.0, None, ALU.add).then_inc(deg_ready, 1)
                v.wait_ge(loaded, 16 * LOADS)
                tt(K[:].rearrange("p (k f) -> p k f", k=DD), bc(w1r[:], 2, HH), bc(w2r[:], 1, DD), ALU.mult).then_inc(k_ready, 1)
                v.wait_ge(dis_ready, 2)
                v.tensor_scalar(coef[:], coef[:], 1.0, None, ALU.add)
                v.drain()
                v.reciprocal(coef[:], coef[:])
                v.drain()
                v.tensor_scalar(coef[:], coef[:], -2.0, 3.0, ALU.mult, ALU.add)
                for ch, (t0, n) in enumerate(CHUNKS):
                    v.wait_ge(rows_done, ch + 1)
                    frm = ps_b[ch % 2][:, 0:n * P].rearrange("p (t f) -> p t f", f=P)
                    v.tensor_copy(own[:, t0:t0 + n, 0:TW - 1], frm[:, :, 0:TW - 1]).then_inc(rows_read, 1)
                v.tensor_copy(own[:, 0:T, TW - 1], dis[:])
                v.drain()
                v.nop().then_inc(table_ready, 1)

                def orthogonal(count):
                    v.tensor_copy(U[:, :, 0, :], V[:, :, 0, :])
                    for i in range(DD):
                        frm = V if i == 0 else U
                        w = DD - i
                        tt(tmp[:, :, 0:w, :], frm[:, :, i:DD, :], bc(frm[:, :, i, :], 2, w), ALU.mult)
                        v.drain()
                        v.tensor_reduce(dots[:, :, 0:w], tmp[:, :, 0:w, :], AX, ALU.add)
                        v.drain()
                        last = v.tensor_copy(nn[:, :, i], dots[:, :, 0])
                        if i == DD - 1:
                            last.then_inc(nn_ready, 1)
                            break
                        v.reciprocal(inv[:], dots[:, :, 0])
                        v.drain()
                        tt(dots[:, :, 1:w], dots[:, :, 1:w], bc(inv[:], 2, w - 1), ALU.mult)
                        v.drain()
                        tt(tmp[:, :, 1:w, :], bc(dots[:, :, 1:w], 3, DD), bc(frm[:, :, i, :], 2, w - 1), ALU.mult)
                        v.drain()
                        tt(U[:, :, i + 1:DD, :], frm[:, :, i + 1:DD, :], tmp[:, :, 1:w, :], ALU.subtract)
                        v.drain()

                def edge_maps(count, hidden):
                    hidden()
                    v.drain()
                    v.tensor_scalar(hid[:], hid[:], 0.0, None, ALU.max)
                    v.drain()
                    tt(prod[:].rearrange("p (m n) h -> p m n h", n=NPAR), bc(hid[:], 2, NPAR), bc(m2[:], 1, M), ALU.mult)
                    v.drain()
                    v.tensor_reduce(par[:].rearrange("p m n -> p (m n)"), prod[:], AX, ALU.add)
                    v.drain()
                    tt(V[:, :, 0, 1:3], par[:, :, 0:2], bc(mb2[:, 0:2], 1, M), ALU.add)
                    tt(V[:, :, 0, 3], par[:, :, 3], mb2[:, 3:4].broadcast_to([P, M]), ALU.add)
                    tt(V[:, :, 1, 2:4], par[:, :, 2:5:2], bc(mb2[:, 2:5:2], 1, M), ALU.add)
                    tt(V[:, :, 2, 3], par[:, :, 5], mb2[:, 5:6].broadcast_to([P, M]), ALU.add)
                    v.drain()
                    orthogonal(count)
                    prod4 = mm4[:].rearrange("p (a s b) k -> p a s b k", a=DD, s=S)
                    for a in range(DD):
                        tt(prod4[:, a], bc(U[:, 0:S, a, :], 2, DD), U[:, S:M, :, :], ALU.mult)
                    v.drain()
                    v.tensor_reduce(maps[:].rearrange("p a s b -> p (a s b)"), mm4[:], AX, ALU.add)
                    v.wait_ge(rs_ready, count + 1)
                    tt(rw[:], nn[:, 0:S, :], bc(wts[:], 2, DD), ALU.mult)
                    v.drain()
                    tt(maps[:], maps[:], bc(rw[:].rearrange("p s a -> p a s"), 3, DD), ALU.mult)
                    v.drain()
                    for a in range(DD):
                        last = tt(maps[:, a], maps[:, a], nn[:, S:M, :], ALU.mult)
                    v.drain()

                for i in range(GROUPS):
                    rows = own[:, i * S:(i + 1) * S, :]

                    def hidden():
                        for m in (0, S):
                            tt(hid[:, m:m + S, :], rows[:, :, D:D + HH], rows[:, :, D + HH:D + 2 * HH], ALU.add)

                    v.tensor_copy(wts[:], rows[:, :, TW - 1])
                    edge_maps(i, hidden)
                    for s in range(S):
                        x = own[:, i * S + s, 0:D].rearrange("p (b h) -> p h b", b=DD)
                        tt(pm[:].rearrange("p d (s b) -> p s d b", b=DD)[:, s].rearrange("p (a h) b -> p a h b", a=DD),
                           bc(maps[:, :, s, :], 2, HH), bc(x, 1, DD), ALU.mult)
                    v.drain()
                    v.tensor_reduce(agg[:, i * S:(i + 1) * S, :].rearrange("p s d -> p d s"),
                                    pm[:].rearrange("p d (s b) -> p d s b", b=DD), AX, ALU.add).then_inc(edges_done, 1)
                    v.drain()

                k = lists.counter(v, "sheaf_v")
                with v.Fori(0, T) as t:
                    at = bass.ds(t, 1)
                    n = lists.count(v, t)
                    v.tensor_scalar(rem[:], g.sdeg[:, at], float(S), None, ALU.add)
                    v.drain()
                    with v.Fori(0, n) as _j:
                        kk = v.snap(k)
                        v.tensor_scalar(rem[:], rem[:], float(-S), None, ALU.add)
                        v.drain()
                        v.tensor_scalar(mask[:], g.slot[:, 0:S], rem[:, 0:1], None, ALU.is_lt)
                        v.drain()
                        for h in range(2):
                            v.wait_ge(lists.free[h], kk + 1)

                        def hidden():
                            tt(wts[:], pq[:, :, 2 * HH], mask[:], ALU.mult)
                            tt(hid[:, 0:S, :], pq[:, :, HH:2 * HH],
                               own[:, at, D:D + HH].broadcast_to([P, S, HH]), ALU.add)
                            tt(hid[:, S:M, :], pq[:, :, 0:HH],
                               own[:, at, D + HH:D + 2 * HH].broadcast_to([P, S, HH]), ALU.add)

                        edge_maps(kk + GROUPS, hidden)
                        tt(pm[:].rearrange("p (a h) e -> p a h e", a=DD),
                           bc(maps[:].rearrange("p a s b -> p a (s b)"), 2, HH),
                           bc(xj[:].rearrange("p h s b -> p h (s b)"), 1, DD), ALU.mult).then_inc(edges_done, 1)
                        v.drain()
                        v.tensor_reduce(part[:], pm[:], AX, ALU.add)
                        v.drain()
                        tt(flat(agg[:, at, :]), flat(agg[:, at, :]), part[:], ALU.add)
                        v.reg_add(k, k, 1)
                v.drain()
                a = agg[:, 0:T, :]
                tt(a, a, bc(dis[:], 2, D), ALU.mult)
                v.drain()
                v.tensor_scalar(el[:], a, 0.0, None, ALU.min).then_inc(e_in, 1)
                for d in range(DD):
                    at = slice(d * HH, (d + 1) * HH)
                    v.tensor_scalar(XS[:, :, at], XS[:, :, at], coef[:, d:d + 1], None, ALU.mult)
                v.drain()
                v.tensor_scalar(a, a, 0.0, -1.0, ALU.max, ALU.add)
                v.drain()
                tt(XS[:], XS[:], a, ALU.subtract)
                v.wait_ge(e_out, 1)
                v.drain()
                tt(XS[:], XS[:], el[:], ALU.subtract)
                v.drain()
                layernorm(v, XS[:], el[:], mean[:], var[:], f_var, 1, 1)
                v.wait_ge(f_root, 1)
                tt(XS[:], XS[:], bc(var[:], 2, D), ALU.mult).then_inc(final, 1)


def build(nc, ins, out, upto=99):
    with ExitStack() as ctx:
        g = Program(nc, ctx, ins, out)
        stage_graph(g)
        if upto < 2:
            return g
        stage_lists(g)
        if upto < 3:
            return g
        with ExitStack() as c:
            A = g.sb("adjacency", [P, T, NP], F16, c)
            stage_adjacency(g, A, c)
            if upto < 4:
                return g
            X = g.sb("x", [P, T, D], F32, c)
            stage_appnp(g, A, X, c)
            if upto < 5:
                return g
            stage_turn(g, A)
            stage_lightgcn(g, A, X)
        if upto < 6:
            return g
        XS = g.sb("x_sorted", [P, T, D], F32)
        sdego = g.sb("dego_sorted", [P, T], F32)
        stage_sage(g, XS, sdego)
        if upto < 7:
            return g
        stage_sheaf(g, XS, sdego)
        return g


def kernel(**inputs):
    import concourse.bacc as bacc
    from concourse.bass_utils import run_bass_kernel_spmd

    nc = bacc.Bacc("TRN2", target_bir_lowering=False, num_devices=1)
    arrays, aps = {}, {}
    for name, value in inputs.items():
        a = np.ascontiguousarray(value)
        arrays["in_" + name] = a
        aps[name] = nc.dram_tensor("in_" + name, a.shape, mybir.dt.from_np(a.dtype), kind="ExternalInput").ap()
    out = nc.dram_tensor("out", [N, D], F32, kind="ExternalOutput").ap()
    build(nc, aps, out)
    result = run_bass_kernel_spmd(nc, [arrays], core_ids=[0])
    return result.results[0]["out"]
```

```python
from contextlib import ExitStack

import numpy as np

import concourse.bass as bass
from concourse import mybir

F32 = mybir.dt.float32
F16 = mybir.dt.float16
I32 = mybir.dt.int32
ALU = mybir.AluOpType
ACT = mybir.ActivationFunctionType
AX = mybir.AxisListType.X

P = 128
N = 3125
E = 103125
D = 64
T = -(-N // P)
NP = T * P
TAIL = N - (T - 1) * P
EC = -(-E // P)
DUMMY = NP - 1
NOHI = 63
HC = 13
HSTEPS = EC // HC
W = 64
S = 8
HS = S // 2
CAP = 4000
KEY = 4096
MINBLK = 2
WB = W // S
BLOCKS = WB * (E // W + 1 + sum(E // (P * t) // W + 1 for t in range(1, T)))
CHUNK = 4
CHUNKS = [(c, min(CHUNK, T - c)) for c in range(0, T, CHUNK)]
NC = len(CHUNKS)
LOSCALE = 2048.0
ROUNDS = 10
ALPHA = 0.1
HOPS = 3
LAYERS = 5
HID = 4 * D
EPS = 1e-5
BIG = 3.0e38
DD, HH = 4, 16
NPAR = DD * (DD - 1) // 2
TW = D + 2 * HH + 1
assert EC == HC * HSTEPS and W % S == 0 and DD * HH == D


def bc(ap, axis, n):
    x = ap.unsqueeze(axis)
    shape = list(x.shape)
    shape[axis] = n
    return x.broadcast_to(shape)


HELD = []


class Program:

    def __init__(self, nc, ctx, ins, out):
        self.nc, self.ctx, self.ins, self.out = nc, ctx, ins, out

        def dram(name, shape, dt):
            return nc.dram_tensor(name, shape, dt, kind="Internal").ap()

        HELD[:] = [self.sem("held")]
        self.src_pad = dram("src_pad", [E + P], I32)
        self.key_row = dram("key_row", [NP], F32)
        self.perm_tab = dram("perm_tab", [NP, 4], I32)
        self.ids_dram = dram("ids_blocks", [BLOCKS * P * S], I32)
        self.x2_dram = dram("x2_rows", [NP, D + 1], F32)
        self.h_tab = dram("h_tab", [NP, D], F32)
        self.t_tab = dram("t_tab", [NP, TW], F32)

        sb = self.sb
        self.ident = sb("ident", [P, P], F32)
        self.identh = sb("identh", [P, P], F16)
        self.comb = sb("comb", [P, D], F32)
        self.iota = sb("iota", [P, P], I32)
        self.slot = sb("slot", [P, W], F32)
        self.deg = sb("deg", [P, T], F32)
        self.start = sb("start", [P, T], F32)
        self.sorted = sb("sorted_tab", [P, T, 4], I32)
        self.sdeg = sb("sdeg", [P, T], F32)
        self.nblk = sb("nblk", [1, T], I32)
        self.nwin = sb("nwin", [1, T], I32)
        self.nwall = sb("nwall", [1, 1], I32)
        self.dego = sb("dego", [P, T], F32)

    def sb(self, name, shape, dt, ctx=None):
        return (ctx or self.ctx).enter_context(self.nc.sbuf_tensor(name, shape, dt))

    def ps(self, name, shape, dt, ctx):
        return ctx.enter_context(self.nc.psum_tensor(name, shape, dt))

    def sem(self, name):
        return self.ctx.enter_context(self.nc.semaphore(name))


def hold(eng, sem, value):
    eng.wait_ge(sem, value)
    eng.sem_inc(HELD[0], 1)


def one_hots(v, lo_out, hi_out, iota, lo, hi, n):
    v.tensor_tensor(lo_out, bc(iota[:, 0:P], 1, n), bc(lo, 2, P), ALU.is_equal)
    return v.tensor_tensor(hi_out, bc(iota[:, 0:T], 1, n), bc(hi, 2, T), ALU.is_equal)


def stage_graph(g):
    nc = g.nc
    src, dst = g.ins["src"], g.ins["dst"]
    with ExitStack() as c:
        dst_sb = g.sb("dst_sb", [P, EC], I32, c)
        lo = g.sb("dst_lo", [P, EC], I32, c)
        hi = g.sb("dst_hi", [P, EC], I32, c)
        oh_lo = g.sb("oh_lo", [P, 2, HC, P], F16, c)
        oh_hi = g.sb("oh_hi", [P, 2, HC, T], F16, c)
        zh = g.sb("zh", [P, P], F16, c)
        tri = g.sb("tri", [P, P], F32, c)
        ones = g.sb("ones", [P, P], F32, c)
        zt = g.sb("zt", [P, T], F32, c)
        incl = g.sb("incl", [P, T], F32, c)
        excl = g.sb("excl", [P, T], F32, c)
        nid = g.sb("nid", [P, T], F32, c)
        nkey = g.sb("nkey", [P, T], F32, c)
        key = g.sb("key", [P, T], F32, c)
        keys = g.sb("keys", [P, NP], F32, c)
        gt = g.sb("gt", [P, 2, NP], F16, c)
        rank = g.sb("rank", [P, T], F32, c)
        ranki = g.sb("ranki", [P, T], I32, c)
        tab = g.sb("tab", [P, T, 4], I32, c)
        zsrc = g.sb("zsrc", [1, P], I32, c)
        tmax = g.sb("tmax", [T, 1], F32, c)
        allmax = g.sb("allmax", [1, T], F32, c)
        maxi = g.sb("maxi", [1, T], I32, c)
        one = g.sb("one", [1, 1], F32, c)
        onei = g.sb("onei", [1, 1], I32, c)
        hist = g.ps("hist", [P, 512], F32, c)
        pre = g.ps("pre", [P, 512], F32, c)
        mt = g.ps("mt", [P, 512], F32, c)
        mt2 = g.ps("mt2", [P, 512], F32, c)
        dst_pad = g.sem("dst_padded")
        loaded = g.sem("dst_loaded")
        const = g.sem("graph_constants")
        zeros = g.sem("zeros_set")
        coded = g.sem("dst_coded")
        counted = g.sem("dst_counted")
        hist_done = g.sem("histogram_done")
        deg_done = g.sem("degrees_copied")
        pre_done = g.sem("prefix_done")
        key_done = g.sem("keys_computed")
        key_out = g.sem("keys_stored")
        key_in = g.sem("keys_loaded")
        ranked = g.sem("nodes_ranked")
        scattered = g.sem("rows_scattered")
        tab_in = g.sem("sorted_loaded")
        sdeg_done = g.sem("sorted_degrees")
        max_t = g.sem("degrees_transposed")
        max_d = g.sem("tile_maxima")
        max_r = g.sem("maxima_row")
        pad_out = g.sem("src_pad_stored")
        counts = g.sem("block_counts")

        with nc.Block() as block:

            @block.sync
            def _(sp):
                full = (P - 1) * EC
                sp.wait_ge(dst_pad, 1)
                sp.dma_start(dst_sb[0:P - 1, :], dst[0:full].rearrange("(p j) -> p j", j=EC)).then_inc(loaded, 16)
                sp.dma_start(dst_sb[P - 1:P, 0:E - full], dst[full:E].rearrange("(p j) -> p j", p=1)).then_inc(loaded, 16)
                sp.dma_start(g.src_pad[0:E].rearrange("(a b) -> a b", a=125), src.rearrange("(a b) -> a b", a=125)).then_inc(pad_out, 16)
                sp.wait_ge(zeros, 1)
                sp.dma_start(g.src_pad[E:E + P].rearrange("(a b) -> a b", a=1), zsrc[:]).then_inc(pad_out, 16)
                hold(sp, key_done, 1)
                with nc.allow_non_contiguous_dma(reason="keys in order of nodes, once"):
                    sp.dma_start(g.key_row.rearrange("(t p) -> p t", p=P), key[:]).then_inc(key_out, 16)
                sp.wait_ge(key_out, 16)
                sp.dma_start(keys[:], g.key_row.rearrange("(a n) -> a n", a=1).broadcast_to([P, NP])).then_inc(key_in, 16)
                sp.wait_ge(scattered, 16 * T)
                sp.dma_start(g.sorted[:], g.perm_tab.rearrange("(t p) c -> p t c", p=P)).then_inc(tab_in, 16)
                sp.wait_ge(pad_out, 32)

            @block.gpsimd
            def _(pool):
                nc.gpsimd.memset(dst_sb[:], NOHI * P).then_inc(dst_pad, 1)
                nc.gpsimd.memset(zsrc[:], 0).then_inc(zeros, 1)
                nc.gpsimd.iota(g.iota[:], [[1, P]], channel_multiplier=0)
                nc.gpsimd.iota(g.slot[:], [[1, W]], channel_multiplier=0, allow_small_or_imprecise_dtypes=True)
                nc.gpsimd.iota(nid[:], [[P, T]], channel_multiplier=1, allow_small_or_imprecise_dtypes=True)
                nc.gpsimd.memset(tab[:], 0)
                nc.gpsimd.memset(g.ident[:], 0.0)
                nc.gpsimd.memset(g.comb[:], 0.0)
                nc.gpsimd.memset(tri[:], 1.0)
                pool.drain()
                nc.gpsimd.affine_select(out=g.ident[:], in_=g.ident[:], compare_op=ALU.not_equal, fill=1.0, base=0,
                                        pattern=[[-1, P]], channel_multiplier=1)
                nc.gpsimd.affine_select(out=tri[:], in_=tri[:], compare_op=ALU.is_gt, fill=0.0, base=0,
                                        pattern=[[1, P]], channel_multiplier=-1)
                nc.gpsimd.affine_select(out=g.comb[:], in_=g.comb[:], compare_op=ALU.not_equal, fill=1.0, base=0,
                                        pattern=[[-1, D]], channel_multiplier=1)
                pool.drain()
                nc.gpsimd.affine_select(out=g.comb[:], in_=g.comb[:], compare_op=ALU.not_equal, fill=1.0 / LOSCALE,
                                        base=-D, pattern=[[-1, D]], channel_multiplier=1)
                nc.gpsimd.tensor_copy(g.identh[:], g.ident[:]).then_inc(const, 1)
                pool.wait_ge(ranked, 1)
                for t in range(T):
                    nc.gpsimd.indirect_dma_start(
                        out=g.perm_tab, out_offset=bass.IndirectOffsetOnAxis(ap=ranki[:, t:t + 1], axis=0),
                        in_=tab[:, t, :], in_offset=None).then_inc(scattered, 16)
                pool.wait_ge(scattered, 16 * T)

            @block.vector
            def _(v):
                v.memset(zh[:], 0.0)
                v.memset(ones[:], 1.0)
                v.memset(one[:], 1.0)
                v.memset(zt[:], 0.0)
                v.wait_ge(const, 1)
                v.wait_ge(loaded, 32)
                v.tensor_scalar(lo[:], dst_sb[:], P - 1, None, ALU.bitwise_and)
                v.tensor_scalar(hi[:], dst_sb[:], 7, None, ALU.logical_shift_right)
                v.drain()
                with v.Fori(0, HSTEPS // 2) as i:
                    for b in range(2):
                        v.wait_ge(counted, 2 * i + b)
                        at = bass.ds((2 * i + b) * HC, HC)
                        one_hots(v, oh_lo[:, b], oh_hi[:, b], g.iota, lo[:, at], hi[:, at], HC).then_inc(coded, 1)
                v.wait_ge(hist_done, 1)
                v.tensor_copy(g.deg[:], hist[:, 0:T])
                v.drain()
                v.tensor_tensor_scan(incl[:], g.deg[:], zt[:], 0.0, ALU.add, ALU.add)
                v.drain()
                v.tensor_tensor(excl[:], incl[:], g.deg[:], ALU.subtract).then_inc(deg_done, 1)
                v.tensor_scalar(nkey[:], nid[:], -1.0, KEY - 1.0, ALU.mult, ALU.add)
                v.tensor_scalar(key[:], g.deg[:], float(CAP), float(KEY), ALU.min, ALU.mult)
                v.drain()
                v.tensor_tensor(key[:], key[:], nkey[:], ALU.add).then_inc(key_done, 1)
                v.wait_ge(pre_done, 1)
                v.tensor_copy(g.start[:], pre[:, 0:T])
                v.drain()
                v.tensor_copy(tab[:, :, 0], g.start[:])
                v.tensor_copy(tab[:, :, 1], g.deg[:])
                v.tensor_copy(tab[:, :, 2], nid[:])
                v.wait_ge(key_in, 16)
                for t in range(T):
                    v.tensor_scalar(gt[:, t % 2, :], keys[:], key[:, t:t + 1], 0.0, ALU.is_gt, ALU.add,
                                    accum_out=rank[:, t:t + 1])
                    if t % 2:
                        v.drain()
                v.drain()
                v.tensor_copy(ranki[:], rank[:]).then_inc(ranked, 1)
                v.wait_ge(tab_in, 16)
                v.tensor_copy(g.sdeg[:], g.sorted[:, :, 1]).then_inc(sdeg_done, 1)
                v.wait_ge(max_t, 1)
                v.tensor_reduce(tmax[:], mt[0:T, 0:P], AX, ALU.max).then_inc(max_d, 1)
                v.wait_ge(max_r, 1)
                v.tensor_copy(allmax[:], mt2[0:1, 0:T])
                v.drain()
                v.tensor_reduce(one[:], allmax[:], AX, ALU.max)
                v.tensor_copy(maxi[:], allmax[:])
                v.drain()
                v.tensor_copy(onei[:], one[:])
                v.tensor_scalar(g.nblk[:], maxi[:], float(S - 1), None, ALU.add)
                v.drain()
                v.tensor_scalar(g.nblk[:], g.nblk[:], 3, None, ALU.logical_shift_right)
                v.drain()
                v.tensor_scalar(g.nblk[:], g.nblk[:], float(MINBLK), None, ALU.max)
                v.tensor_scalar(onei[:], onei[:], float(W - 1), None, ALU.add)
                v.drain()
                v.tensor_scalar(g.nwin[:], g.nblk[:], float(WB - 1), None, ALU.add)
                v.tensor_scalar(g.nwall[:], onei[:], 6, None, ALU.logical_shift_right)
                v.drain()
                v.tensor_scalar(g.nwin[:], g.nwin[:], 3, None, ALU.logical_shift_right)
                v.tensor_scalar(g.nwall[:], g.nwall[:], 1.0, None, ALU.max).then_inc(counts, 1)

            @block.tensor
            def _(pe):
                pe.wait_ge(coded, 1)
                nc.tensor.matmul(hist[:, 0:T], zh[:], oh_hi[:, 0, 0, :], start=True, stop=False,
                                 skip_group_check=True).then_inc(counted, 1)
                with pe.Fori(0, HSTEPS // 2) as i:
                    for b in range(2):
                        pe.wait_ge(coded, 2 * i + b + 1)
                        for j in range(HC):
                            mm = nc.tensor.matmul(hist[:, 0:T], oh_lo[:, b, j, :], oh_hi[:, b, j, :],
                                                  start=False, stop=False, skip_group_check=True)
                        mm.then_inc(counted, 1)
                nc.tensor.matmul(hist[:, 0:T], zh[:], oh_hi[:, 0, 0, :], start=False, stop=True,
                                 skip_group_check=True).then_inc(hist_done, 1)
                pe.wait_ge(deg_done, 1)
                nc.tensor.matmul(pre[:, 0:T], tri[:], g.deg[:], start=True, stop=False)
                nc.tensor.matmul(pre[:, 0:T], ones[:], excl[:], start=False, stop=True).then_inc(pre_done, 1)
                pe.wait_ge(sdeg_done, 1)
                nc.tensor.transpose(mt[0:T, 0:P], g.sdeg[:], g.ident[:]).then_inc(max_t, 1)
                pe.wait_ge(max_d, 1)
                nc.tensor.transpose(mt2[0:1, 0:T], tmax[:], g.ident[0:T, 0:T]).then_inc(max_r, 1)


def stage_lists(g):
    nc = g.nc
    with ExitStack() as c:
        first = g.sb("win_start", [P, T], I32, c)
        win = g.sb("win_ids", [P, T, W], I32, c)
        winf = g.sb("win_masked", [P, T, W], F32, c)
        mask = g.sb("win_mask", [P, T, W], F32, c)
        cur = g.sb("cur_start", [P, 1], F32, c)
        rem = g.sb("cur_left", [P, 1], F32, c)
        curi = g.sb("cur_start_i", [P, 1], I32, c)
        xwin = g.sb("xwin", [P, W], I32, c)
        xmask = g.sb("xmask", [P, W], F32, c)
        starts = g.sem("list_starts")
        landed = g.sem("list_windows")
        masked = g.sem("list_masked")
        stored = g.sem("list_stored")
        x_idx = g.sem("overflow_start")
        x_landed = g.sem("overflow_window")
        x_masked = g.sem("overflow_masked")
        x_stored = g.sem("overflow_stored")
        src_rows = g.src_pad.rearrange("(a e) -> a e", a=1)

        def blocks_at(block0):
            return g.ids_dram[bass.ds(block0 * (P * S), W * P)].rearrange("(b p s) -> p b s", p=P, s=S)

        with nc.Block() as block:

            @block.vector
            def _(v):
                v.tensor_scalar(first[:], g.sorted[:, :, 0], float(E), None, ALU.min).then_inc(starts, 1)
                v.tensor_tensor(mask[:], bc(g.slot[:], 1, T), bc(g.sdeg[:], 2, W), ALU.is_lt)
                v.wait_ge(landed, 16 * T)
                v.tensor_scalar(winf[:], win[:], float(-DUMMY), None, ALU.add)
                v.drain()
                v.tensor_tensor(winf[:], winf[:], mask[:], ALU.mult)
                v.drain()
                v.tensor_scalar(win[:], winf[:], float(DUMMY), None, ALU.add).then_inc(masked, 1)
                k = v.alloc_register("v_over")
                v.reg_mov(k, 0)
                with v.Fori(0, T) as t:
                    n = v.value_load(g.nwin[0:1, bass.ds(t, 1)], min_val=1, max_val=BLOCKS)
                    with v.If(n > 1):
                        v.tensor_copy(cur[:], g.sorted[:, bass.ds(t, 1), 0])
                        v.tensor_copy(rem[:], g.sdeg[:, bass.ds(t, 1)])
                        v.drain()
                        with v.Fori(1, n) as _w:
                            done = v.snap(k)
                            v.tensor_scalar(cur[:], cur[:], float(W), float(E), ALU.add, ALU.min)
                            v.tensor_scalar(rem[:], rem[:], float(-W), None, ALU.add)
                            v.drain()
                            v.tensor_copy(curi[:], cur[:]).then_inc(x_idx, 1)
                            v.tensor_scalar(xmask[:], g.slot[:], rem[:, 0:1], None, ALU.is_lt)
                            v.wait_ge(x_landed, (done + 1) * 16)
                            v.tensor_scalar(winf[:, 0, :], xwin[:], float(-DUMMY), None, ALU.add)
                            v.drain()
                            v.tensor_tensor(winf[:, 0, :], winf[:, 0, :], xmask[:], ALU.mult)
                            v.drain()
                            v.tensor_scalar(xwin[:], winf[:, 0, :], float(DUMMY), None, ALU.add).then_inc(x_masked, 1)
                            v.wait_ge(x_stored, (done + 1) * 16)
                            v.reg_add(k, k, 1)

            @block.gpsimd
            def _(pool):
                pool.wait_ge(starts, 1)
                for t in range(T):
                    nc.gpsimd.indirect_dma_start(
                        out=win[:, t, :], out_offset=None, in_=src_rows,
                        in_offset=bass.IndirectOffsetOnAxis(ap=first[:, t:t + 1], axis=1)).then_inc(landed, 16)
                k = pool.alloc_register("p_over")
                pool.reg_mov(k, 0)
                with pool.Fori(0, T) as t:
                    n = pool.value_load(g.nwin[0:1, bass.ds(t, 1)], min_val=1, max_val=BLOCKS)
                    with pool.If(n > 1):
                        with pool.Fori(1, n) as _w:
                            done = pool.snap(k)
                            hold(pool, x_idx, done + 1)
                            nc.gpsimd.indirect_dma_start(
                                out=xwin[:], out_offset=None, in_=src_rows,
                                in_offset=bass.IndirectOffsetOnAxis(ap=curi[:], axis=1)).then_inc(x_landed, 16)
                            hold(pool, x_landed, (done + 1) * 16)
                            pool.reg_add(k, k, 1)

            @block.sync
            def _(sp):
                k = sp.alloc_register("s_over")
                at = sp.alloc_register("s_block")
                sp.reg_mov(k, 0)
                sp.reg_mov(at, 0)
                sp.wait_ge(masked, 1)
                with sp.Fori(0, T) as t:
                    n = sp.value_load(g.nwin[0:1, bass.ds(t, 1)], min_val=1, max_val=BLOCKS)
                    base = sp.snap(at, min_val=0, max_val=BLOCKS - WB)
                    sp.dma_start(blocks_at(base), win[:, bass.ds(t, 1), :].rearrange("p a (b s) -> p (a b) s", s=S)
                                 ).then_inc(stored, 16)
                    with sp.If(n > 1):
                        with sp.Fori(1, n) as _w:
                            done = sp.snap(k)
                            sp.reg_add(at, at, WB)
                            here = sp.snap(at, min_val=WB, max_val=BLOCKS - WB)
                            hold(sp, x_masked, done + 1)
                            sp.dma_start(blocks_at(here), xwin[:].rearrange("p (b s) -> p b s", s=S)
                                         ).then_inc(x_stored, 16)
                            sp.reg_add(k, k, 1)
                    sp.reg_add(at, at, WB)
                sp.wait_ge(stored, 16 * T)
                hold(sp, x_stored, sp.snap(k) * 16)



TT = T + T % 2
PAIRS = TT // 2
GN = 16
GSTEPS = P // GN
STEPS = PAIRS * GSTEPS


def stage_adjacency(g, A, c):
    nc = g.nc
    none = float(NOHI * P)
    with ExitStack() as c:
        cur = g.sb("a_start", [P, TT], F32, c)
        rem = g.sb("a_left", [P, TT], F32, c)
        first = g.sb("a_start_i", [P, TT], I32, c)
        win = g.sb("a_win", [P, TT, W], I32, c)
        winf = g.sb("a_winf", [P, TT, W], F32, c)
        hi = g.sb("a_hi", [P, PAIRS * P], I32, c)
        lo = g.sb("a_lo", [P, PAIRS * P], I32, c)[:]
        oh_lo = g.sb("a_oh_lo", [P, 2, GN, P], F16, c)
        oh_hi = g.sb("a_oh_hi", [P, 2, GN, T], F16, c)
        turned = [g.ps(f"a_turned{b}", [P, 512], F32, c) for b in range(2)]
        cols = [[g.ps(f"a_cols{b}{h}", [P, 512], F32, c) for h in range(2)] for b in range(2)]
        starts = g.sem("adj_starts")
        landed = g.sem("adj_windows")
        masked = g.sem("adj_masked")
        turn_done = g.sem("adj_turned")
        turn_read = g.sem("adj_turned_read")
        coded = g.sem("adj_coded")
        used = g.sem("adj_multiplied")
        moved = g.sem("adj_moved")
        src_rows = g.src_pad.rearrange("(a e) -> a e", a=1)

        def columns(b, h, u, gi):
            frm = cols[b][h][:, 0:GN * T].rearrange("q (p h) -> q h p", h=T)
            return A[:, :, bass.ds(u * (2 * P) + h * P + gi * GN, GN)], frm

        def steps(eng, w, do):
            with eng.Fori(0, PAIRS - 1) as u:
                for gi in range(GSTEPS):
                    do(w * STEPS + u * GSTEPS + gi, u, gi, 2)
            for gi in range(GSTEPS):
                do(w * STEPS + (PAIRS - 1) * GSTEPS + gi, PAIRS - 1, gi, 2 if TT == T else 1)

        def overflow(eng, body):
            n = eng.value_load(g.nwall[0:1, 0:1], min_val=1, max_val=E // W + 1)
            with eng.If(n > 1):
                with eng.Fori(1, n) as w:
                    body(w)

        with nc.Block() as block:

            @block.vector
            def _(v):
                def windows(w, first_pass):
                    if first_pass:
                        v.memset(cur[:], 0.0)
                        v.memset(rem[:], 0.0)
                        v.memset(win[:, T:TT, :], 0)
                        v.drain()
                        v.tensor_copy(cur[:, 0:T], g.start[:])
                        v.tensor_copy(rem[:, 0:T], g.deg[:])
                        v.drain()
                        v.tensor_scalar(first[:], cur[:], float(E), None, ALU.min).then_inc(starts, 1)
                    else:
                        v.tensor_scalar(cur[:], cur[:], float(W), float(E), ALU.add, ALU.min)
                        v.tensor_scalar(rem[:], rem[:], float(-W), None, ALU.add)
                        v.drain()
                        v.tensor_copy(first[:], cur[:]).then_inc(starts, 1)
                    v.wait_ge(turn_read, w * PAIRS)
                    v.wait_ge(landed, (w + 1) * (16 * T))
                    v.tensor_scalar(winf[:], win[:], -none, None, ALU.add)
                    v.drain()
                    v.tensor_tensor(win[:], bc(g.slot[:], 1, TT), bc(rem[:], 2, W), ALU.is_lt)
                    v.drain()
                    v.tensor_tensor(winf[:], winf[:], win[:], ALU.mult)
                    v.drain()
                    v.tensor_scalar(winf[:], winf[:], none, None, ALU.add).then_inc(masked, 1)
                    for u in range(PAIRS):
                        v.wait_ge(turn_done, w * PAIRS + u + 1)
                        v.tensor_copy(lo[:, u * P:(u + 1) * P], turned[u % 2][:, 0:P]).then_inc(turn_read, 1)
                    v.drain()
                    v.tensor_scalar(hi[:], lo, 7, None, ALU.logical_shift_right)
                    v.drain()
                    v.tensor_scalar(lo, lo, P - 1, None, ALU.bitwise_and)
                    v.drain()

                def code(k, u, gi, halves):
                    v.wait_ge(used, k)
                    at = bass.ds(u * P + gi * GN, GN)
                    one_hots(v, oh_lo[:, gi % 2], oh_hi[:, gi % 2], g.iota, lo[:, at], hi[:, at], GN).then_inc(coded, 1)

                def add(k, u, gi, halves):
                    code(k, u, gi, halves)
                    v.wait_ge(used, k + 2)
                    for h in range(halves):
                        to, frm = columns(gi % 2, h, u, gi)
                        last = v.tensor_tensor(to, to, frm, ALU.add)
                    last.then_inc(moved, 1)

                windows(0, True)
                steps(v, 0, code)
                v.wait_ge(moved, STEPS + 1)

                def more(w):
                    windows(w, False)
                    steps(v, w, add)

                overflow(v, more)
                v.drain()
                v.tensor_reduce(g.dego[:], A[:], AX, ALU.add)
                v.drain()

            @block.gpsimd
            def _(pool):
                def gather(w):
                    hold(pool, starts, w + 1)
                    hold(pool, landed, w * (16 * T))
                    for t in range(T):
                        nc.gpsimd.indirect_dma_start(
                            out=win[:, t, :], out_offset=None, in_=src_rows,
                            in_offset=bass.IndirectOffsetOnAxis(ap=first[:, t:t + 1], axis=1)).then_inc(landed, 16)

                gather(0)
                overflow(pool, gather)

            @block.scalar
            def _(act):
                act.nop().then_inc(moved, 1)

                def move(k, u, gi, halves):
                    act.wait_ge(used, k + 2)
                    for h in range(halves):
                        to, frm = columns(gi % 2, h, u, gi)
                        last = nc.scalar.activation(to, frm, ACT.Copy)
                    last.then_inc(moved, 1)

                steps(act, 0, move)

            @block.tensor
            def _(pe):
                def passes(w, first_pass):
                    pe.wait_ge(masked, w + 1)
                    for u in range(PAIRS):
                        if not first_pass or u >= 2:
                            pe.wait_ge(turn_read, w * PAIRS + u - 1)
                        tr = nc.tensor.transpose(turned[u % 2][:, 0:P],
                                                 winf[:, 2 * u:2 * u + 2, :].rearrange("p a b -> p (a b)"), g.ident[:])
                        tr.then_inc(turn_done, 1)
                    if first_pass:
                        pe.nop().then_inc(used, 1)

                    def multiply(k, u, gi, halves):
                        pe.wait_ge(coded, k + 1)
                        pe.wait_ge(moved, k)
                        b = gi % 2
                        for h in range(halves):
                            at = slice(h * W, (h + 1) * W)
                            for p in range(GN):
                                mm = nc.tensor.matmul(cols[b][h][:, p * T:(p + 1) * T], oh_lo[at, b, p, :],
                                                      oh_hi[at, b, p, :], start=True, stop=True)
                        mm.then_inc(used, 1)

                    steps(pe, w, multiply)

                passes(0, True)
                overflow(pe, lambda w: passes(w, False))



def layernorm(v, x, sq, m, var, out_var, add, total):
    v.tensor_reduce(m, x, AX, ALU.add)
    v.drain()
    v.tensor_scalar(m, m, -1.0 / D, None, ALU.mult)
    v.drain()
    v.tensor_tensor(x, x, bc(m, 2, D), ALU.add)
    v.drain()
    v.tensor_tensor(sq, x, x, ALU.mult)
    v.drain()
    v.tensor_reduce(var, sq, AX, ALU.add)
    v.drain()
    v.tensor_scalar(var, var, 1.0 / D, EPS, ALU.mult, ALU.add).then_inc(out_var, add)


def root_inverse(act, x, inc):
    act.activation(x, x, ACT.Ln)
    act.drain()
    act.activation(x, x, ACT.Exp, scale=-0.5).then_inc(inc, 1)


class Spread:

    def __init__(self, g, name, c, A, x):
        self.g, self.A, self.x = g, A, x
        self.split = [g.sb(f"{name}_split{b}", [P, T, 2 * D], F16, c) for b in range(2)]
        self.copy = [g.sb(f"{name}_copy{b}", [P, CHUNK * P], F32, c) for b in range(2)]
        self.new = [g.sb(f"{name}_new{b}", [P, CHUNK, D], F32, c) for b in range(2)]
        self.rest = [g.sb(f"{name}_rest{b}", [P, CHUNK, D], F32, c) for b in range(2)]
        self.wide = [g.ps(f"{name}_wide{b}", [P, CHUNK * P], F32, c) for b in range(2)]
        self.turned = [g.ps(f"{name}_nodes{b}", [P, CHUNK * P], F32, c) for b in range(2)]
        self.product = g.sem(f"{name}_product")
        self.copied = g.sem(f"{name}_copied")
        self.nodes = g.sem(f"{name}_nodes_ready")
        self.made = g.sem(f"{name}_made")
        self.high = g.sem(f"{name}_high")
        self.low = g.sem(f"{name}_rest_ready")
        self.ready = g.sem(f"{name}_split_ready")

    def pe_turn(self, pe, r, c):
        t0, n = CHUNKS[c]
        k = r * NC + c
        pe.wait_ge(self.copied, k + 1)
        pe.wait_ge(self.made, NC + (k if c == 0 else k - 1))
        for j in range(n):
            mm = self.g.nc.tensor.matmul(self.turned[c % 2][:, j * D:(j + 1) * D],
                                         self.copy[c % 2][:, j * P:(j + 1) * P], self.g.comb[:],
                                         start=True, stop=True)
        mm.then_inc(self.nodes, 1)

    def pe_round(self, pe, r, b):
        for c, (t0, n) in enumerate(CHUNKS):
            k = r * NC + c
            pe.wait_ge(self.copied, k if c == 0 else k - 1)
            for s in range(T):
                if c == 0 and s % CHUNK == 0:
                    pe.wait_ge(self.ready, k + s // CHUNK + 1)
                if c > 0 and s == T // 2:
                    self.pe_turn(pe, r, c - 1)
                mm = self.g.nc.tensor.matmul(self.wide[c % 2][:, 0:n * P], self.split[b][:, s, :],
                                             self.A[:, s, t0 * P:(t0 + n) * P], start=(s == 0), stop=(s == T - 1))
            mm.then_inc(self.product, 1)
        self.pe_turn(pe, r, NC - 1)

    def act_split(self, act, j, c, b):
        t0, n = CHUNKS[c]
        act.wait_ge(self.made, j + 1)
        act.activation(self.split[b][:, t0:t0 + n, 0:D], self.new[c % 2][:, 0:n, :], ACT.Copy).then_inc(self.high, 1)
        act.wait_ge(self.low, j + 1)
        act.activation(self.split[b][:, t0:t0 + n, D:2 * D], self.rest[c % 2][:, 0:n, :], ACT.Copy,
                       scale=LOSCALE).then_inc(self.ready, 1)

    def act_round(self, act, r, b, last=False):
        for c, (t0, n) in enumerate(CHUNKS):
            k = r * NC + c
            act.wait_ge(self.product, k + 1)
            act.wait_ge(self.nodes, k if c == 0 else k - 1)
            act.activation(self.copy[c % 2][:, 0:n * P], self.wide[c % 2][:, 0:n * P], ACT.Copy).then_inc(self.copied, 1)
            if not last:
                self.act_split(act, NC + k, c, 1 - b)

    def v_split(self, v, j, c, b):
        t0, n = CHUNKS[c]
        v.wait_ge(self.high, j + 1)
        v.tensor_tensor(self.rest[c % 2][:, 0:n, :], self.new[c % 2][:, 0:n, :], self.split[b][:, t0:t0 + n, 0:D],
                        ALU.subtract).then_inc(self.low, 1)

    def v_round(self, v, r, b, make, last=False):
        for c, (t0, n) in enumerate(CHUNKS):
            k = r * NC + c
            v.wait_ge(self.nodes, k + 1)
            if not last:
                v.wait_ge(self.ready, NC + (k if c == 0 else k - 1))
            frm = self.turned[c % 2][:, 0:n * D].rearrange("p (t f) -> p t f", f=D)
            make(t0, n, frm, self.new[c % 2][:, 0:n, :])
            if not last:
                self.v_split(v, NC + k, c, 1 - b)


def stage_appnp(g, A, X, c):
    nc = g.nc
    with ExitStack() as c:
        sp_ = Spread(g, "appnp", c, A, X)
        H0 = g.sb("h0", [P, T, D], F32, c)
        wb = g.sb("w_b", [D + 1, D], F32, c)
        xt = [g.sb(f"x_turned{b}", [D + 1, CHUNK * P], F32, c) for b in range(2)]
        dl = g.sb("norm_in", [P, 2, T], F32, c)
        on = g.sb("norm_on", [P, 2, T], F32, c)
        c1 = g.sb("c_agg", [P, T], F32, c)
        cl = g.sb("c_agg_last", [P, T], F32, c)
        c2 = g.sb("c_h0", [P, T], F32, c)
        mean = g.sb("ln_mean", [P, T], F32, c)
        var = g.sb("ln_var", [P, T], F32, c)
        loaded = g.sem("appnp_loaded")
        padded = g.sem("appnp_padded")
        degs = g.sem("appnp_degrees")
        roots = g.sem("appnp_norms")
        x_turned = g.sem("appnp_x_turned")
        x_copied = g.sem("appnp_x_copied")
        h0_done = g.sem("appnp_h0")
        h0_read = g.sem("appnp_h0_read")
        var_done = g.sem("appnp_var")
        root_done = g.sem("appnp_root")
        full = (T - 1) * P

        with nc.Block() as block:

            @block.sync
            def _(sp):
                x = g.ins["x"]
                sp.dma_start(X[:, 0:T - 1, :], x[0:full].rearrange("(t p) f -> p t f", p=P)).then_inc(loaded, 16)
                sp.dma_start(wb[0:D, :], g.ins["L0_gnn_W"]).then_inc(loaded, 16)
                sp.dma_start(wb[D:D + 1, :], g.ins["L0_gnn_b"].rearrange("(a b) -> a b", a=1)).then_inc(loaded, 16)
                sp.wait_ge(padded, 1)
                sp.dma_start(X[0:TAIL, T - 1, :], x[full:N]).then_inc(loaded, 16)

            @block.gpsimd
            def _(pool):
                nc.gpsimd.memset(X[:, T - 1, :], 0.0).then_inc(padded, 1)

            @block.tensor
            def _(pe):
                pe.wait_ge(loaded, 64)
                pe.wait_ge(degs, 1)
                for ch, (t0, n) in enumerate(CHUNKS):
                    b = ch % 2
                    if ch >= 2:
                        pe.wait_ge(x_copied, ch - 1)
                    for j in range(n):
                        tr = nc.tensor.transpose(sp_.wide[b][0:D, j * P:(j + 1) * P], X[:, t0 + j, :], g.ident[:])
                    tr.then_inc(x_turned, 1)
                    pe.wait_ge(x_copied, ch + 1)
                    if ch >= 2:
                        pe.wait_ge(h0_read, ch - 1)
                    for j in range(n):
                        mm = nc.tensor.matmul(sp_.turned[b][:, j * D:(j + 1) * D], xt[b][:, j * P:(j + 1) * P], wb[:],
                                              start=True, stop=True)
                    mm.then_inc(h0_done, 1)
                with pe.Fori(0, ROUNDS // 2) as i:
                    sp_.pe_round(pe, i * 2, 0)
                    sp_.pe_round(pe, i * 2 + 1, 1)

            @block.scalar
            def _(act):
                act.wait_ge(degs, 1)
                root_inverse(act, dl[:], roots)
                for ch, (t0, n) in enumerate(CHUNKS):
                    b = ch % 2
                    act.wait_ge(x_turned, ch + 1)
                    if ch >= 2:
                        act.wait_ge(h0_done, ch - 1)
                    act.activation(xt[b][0:D, 0:n * P], sp_.wide[b][0:D, 0:n * P], ACT.Copy).then_inc(x_copied, 1)
                for ch in range(NC):
                    sp_.act_split(act, ch, ch, 0)
                with act.Fori(0, ROUNDS // 2 - 1) as i:
                    sp_.act_round(act, i * 2, 0)
                    sp_.act_round(act, i * 2 + 1, 1)
                sp_.act_round(act, ROUNDS - 2, 0)
                sp_.act_round(act, ROUNDS - 1, 1, last=True)
                act.wait_ge(var_done, 1)
                root_inverse(act, var[:], root_done)

            @block.vector
            def _(v):
                v.memset(xt[0][D:D + 1, :], 1.0)
                v.memset(xt[1][D:D + 1, :], 1.0)
                v.tensor_scalar(dl[:, 0, :], g.dego[:], 1.0, None, ALU.max)
                v.tensor_scalar(dl[:, 1, :], g.deg[:], 1.0, None, ALU.max).then_inc(degs, 1)
                v.tensor_scalar(on[:, 0, :], g.dego[:], 0.0, None, ALU.is_gt)
                v.tensor_scalar(on[:, 1, :], g.deg[:], 0.0, None, ALU.is_gt)
                v.drain()
                v.wait_ge(roots, 1)
                v.tensor_tensor(dl[:], dl[:], on[:], ALU.mult)
                v.drain()
                ns, nd = dl[:, 0, :], dl[:, 1, :]
                v.tensor_scalar(cl[:], nd, 1.0 - ALPHA, None, ALU.mult)
                v.tensor_scalar(c2[:], ns, ALPHA, None, ALU.mult)
                v.drain()
                v.tensor_tensor(c1[:], cl[:], ns, ALU.mult)
                for ch, (t0, n) in enumerate(CHUNKS):
                    v.wait_ge(h0_done, ch + 1)
                    v.tensor_copy(H0[:, t0:t0 + n, :],
                                  sp_.turned[ch % 2][:, 0:n * D].rearrange("p (t f) -> p t f", f=D)).then_inc(h0_read, 1)
                v.drain()
                for ch, (t0, n) in enumerate(CHUNKS):
                    if ch >= 2:
                        v.wait_ge(sp_.ready, ch - 1)
                    v.tensor_tensor(sp_.new[ch % 2][:, 0:n, :], H0[:, t0:t0 + n, :], bc(ns[:, t0:t0 + n], 2, D),
                                    ALU.mult).then_inc(sp_.made, 1)
                    sp_.v_split(v, ch, ch, 0)

                def make(t0, n, frm, to):
                    rest = sp_.rest[(t0 // CHUNK) % 2][:, 0:n, :]
                    v.tensor_tensor(to, frm, bc(c1[:, t0:t0 + n], 2, D), ALU.mult)
                    v.tensor_tensor(rest, H0[:, t0:t0 + n, :], bc(c2[:, t0:t0 + n], 2, D), ALU.mult)
                    v.drain()
                    v.tensor_tensor(to, to, rest, ALU.add).then_inc(sp_.made, 1)

                def make_last(t0, n, frm, to):
                    x = X[:, t0:t0 + n, :]
                    v.tensor_tensor(to, frm, bc(cl[:, t0:t0 + n], 2, D), ALU.mult)
                    v.scalar_tensor_tensor(x, H0[:, t0:t0 + n, :], ALPHA, x, ALU.mult, ALU.add)
                    v.drain()
                    v.tensor_tensor(x, x, to, ALU.add).then_inc(sp_.made, 1)

                with v.Fori(0, ROUNDS // 2 - 1) as i:
                    sp_.v_round(v, i * 2, 0, make)
                    sp_.v_round(v, i * 2 + 1, 1, make)
                sp_.v_round(v, ROUNDS - 2, 0, make)
                v.wait_ge(sp_.ready, NC * ROUNDS)
                sp_.v_round(v, ROUNDS - 1, 1, make_last, last=True)
                v.drain()
                layernorm(v, X[:], H0[:], mean[:], var[:], var_done, 1, 1)
                v.wait_ge(root_done, 1)
                v.tensor_tensor(X[:], X[:], bc(var[:], 2, D), ALU.mult)


def stage_turn(g, A):
    nc = g.nc
    BANK = 8
    groups = [(s, t0, min(BANK, T - t0)) for s in range(T) for t0 in range(s + 1, T, BANK)]
    with ExitStack() as c:
        up = [g.ps(f"turn_up{b}", [P, BANK, P], F16, c) for b in range(2)]
        down = [g.ps(f"turn_down{b}", [P, BANK, P], F16, c) for b in range(2)]
        done = g.sem("turn_done")
        up_moved = g.sem("turn_up_moved")
        down_moved = g.sem("turn_down_moved")
        diagonal = [(t0, min(BANK, T - t0)) for t0 in range(0, T, BANK)]

        with nc.Block() as block:

            @block.tensor
            def _(pe):
                for k, (s, t0, n) in enumerate(groups):
                    if k >= 2:
                        pe.wait_ge(up_moved, k - 1)
                        pe.wait_ge(down_moved, k - 1)
                    for j in range(n):
                        t = t0 + j
                        nc.tensor.transpose(up[k % 2][:, j, :], A[:, s, t * P:(t + 1) * P], g.identh[:])
                        tr = nc.tensor.transpose(down[k % 2][:, j, :], A[:, t, s * P:(s + 1) * P], g.identh[:])
                    tr.then_inc(done, 1)
                for i, (t0, n) in enumerate(diagonal):
                    k = len(groups) + i
                    pe.wait_ge(up_moved, k - 1)
                    for j in range(n):
                        t = t0 + j
                        tr = nc.tensor.transpose(up[k % 2][:, j, :], A[:, t, t * P:(t + 1) * P], g.identh[:])
                    tr.then_inc(done, 1)

            @block.scalar
            def _(act):
                for k, (s, t0, n) in enumerate(groups):
                    act.wait_ge(done, k + 1)
                    act.activation(A[:, t0:t0 + n, s * P:(s + 1) * P], up[k % 2][:, 0:n, :], ACT.Copy).then_inc(up_moved, 1)
                for i, (t0, n) in enumerate(diagonal):
                    k = len(groups) + i
                    act.wait_ge(done, k + 1)
                    for j in range(n):
                        t = t0 + j
                        last = act.activation(A[:, t, t * P:(t + 1) * P], up[k % 2][:, j, :], ACT.Copy)
                    last.then_inc(up_moved, 1)

            @block.vector
            def _(v):
                for k, (s, t0, n) in enumerate(groups):
                    v.wait_ge(done, k + 1)
                    v.tensor_copy(A[:, s, t0 * P:(t0 + n) * P].rearrange("p (t q) -> p t q", q=P),
                                  down[k % 2][:, 0:n, :]).then_inc(down_moved, 1)


def stage_lightgcn(g, A, X):
    nc = g.nc
    with ExitStack() as c:
        sp_ = Spread(g, "light", c, A, X)
        acc = g.sb("light_sum", [P, T, D], F32, c)
        dl = g.sb("light_norm", [P, T], F32, c)
        on = g.sb("light_on", [P, T], F32, c)
        mean = g.sb("light_mean", [P, T], F32, c)
        var = g.sb("light_var", [P, T], F32, c)
        degs = g.sem("light_degrees")
        roots = g.sem("light_norms")
        var_done = g.sem("light_var_done")
        root_done = g.sem("light_root")
        x_done = g.sem("light_x")
        x_out = g.sem("light_x_stored")

        with nc.Block() as block:

            @block.tensor
            def _(pe):
                with pe.Fori(0, (HOPS - 1) // 2) as i:
                    sp_.pe_round(pe, i * 2, 0)
                    sp_.pe_round(pe, i * 2 + 1, 1)
                sp_.pe_round(pe, HOPS - 1, 0)

            @block.scalar
            def _(act):
                act.wait_ge(degs, 1)
                root_inverse(act, dl[:], roots)
                for ch in range(NC):
                    sp_.act_split(act, ch, ch, 0)
                with act.Fori(0, (HOPS - 1) // 2) as i:
                    sp_.act_round(act, i * 2, 0)
                    sp_.act_round(act, i * 2 + 1, 1)
                sp_.act_round(act, HOPS - 1, 0, last=True)
                act.wait_ge(var_done, 1)
                root_inverse(act, var[:], root_done)

            @block.vector
            def _(v):
                v.tensor_scalar(dl[:], g.dego[:], 1.0, None, ALU.max).then_inc(degs, 1)
                v.tensor_scalar(on[:], g.dego[:], 0.0, None, ALU.is_gt)
                v.tensor_copy(acc[:], X[:])
                v.drain()
                v.wait_ge(roots, 1)
                v.tensor_tensor(dl[:], dl[:], dl[:], ALU.mult)
                v.drain()
                v.tensor_tensor(dl[:], dl[:], on[:], ALU.mult)
                v.drain()
                for ch, (t0, n) in enumerate(CHUNKS):
                    if ch >= 2:
                        v.wait_ge(sp_.ready, ch - 1)
                    v.tensor_copy(sp_.new[ch % 2][:, 0:n, :], X[:, t0:t0 + n, :]).then_inc(sp_.made, 1)
                    sp_.v_split(v, ch, ch, 0)

                def make(t0, n, frm, to):
                    a = acc[:, t0:t0 + n, :]
                    v.tensor_tensor(to, frm, bc(dl[:, t0:t0 + n], 2, D), ALU.mult).then_inc(sp_.made, 1)
                    v.drain()
                    v.tensor_tensor(a, a, to, ALU.add)

                with v.Fori(0, (HOPS - 1) // 2) as i:
                    sp_.v_round(v, i * 2, 0, make)
                    sp_.v_round(v, i * 2 + 1, 1, make)
                v.wait_ge(sp_.ready, NC * HOPS)
                sp_.v_round(v, HOPS - 1, 0, make, last=True)
                v.drain()
                v.scalar_tensor_tensor(X[:], acc[:], 1.0 / (HOPS + 1), X[:], ALU.mult, ALU.add)
                v.drain()
                layernorm(v, X[:], acc[:], mean[:], var[:], var_done, 1, 1)
                v.wait_ge(root_done, 1)
                v.tensor_tensor(X[:], X[:], bc(var[:], 2, D), ALU.mult).then_inc(x_done, 1)

            @block.sync
            def _(sp):
                rows = g.x2_dram.rearrange("(t p) f -> p t f", p=P)
                with nc.allow_non_contiguous_dma(reason="one degree beside each row, once"):
                    sp.dma_start(rows[:, :, D:D + 1], g.dego[:].unsqueeze(2)).then_inc(x_out, 16)
                hold(sp, x_done, 1)
                sp.dma_start(rows[:, :, 0:D], X[:]).then_inc(x_out, 16)
                sp.wait_ge(x_out, 32)



class Lists:

    def __init__(self, g, name, c, table, width):
        self.g, self.table, self.width = g, table, width
        self.ids = [g.sb(f"{name}_ids{h}", [P, HS], I32, c) for h in range(2)]
        self.rows = g.sb(f"{name}_rows", [P, S, width], F32, c)
        self.landed = [g.sem(f"{name}_ids_landed{h}") for h in range(2)]
        self.half = [g.sem(f"{name}_rows{h}") for h in range(2)]
        self.free = [g.sem(f"{name}_free{h}") for h in range(2)]

    def counter(self, eng, name):
        k = eng.alloc_register(f"{name}_blocks")
        eng.reg_mov(k, 0)
        return k

    def count(self, eng, t):
        return eng.value_load(self.g.nblk[0:1, bass.ds(t, 1)], min_val=MINBLK, max_val=BLOCKS)

    def sp_walk(self, sp, k):
        g = self.g
        at = sp.alloc_register(f"sp_at_{self.rows.name}")
        sp.reg_mov(at, 0)
        with sp.Fori(0, T) as t:
            n = self.count(sp, t)
            wins = sp.value_load(g.nwin[0:1, bass.ds(t, 1)], min_val=1, max_val=BLOCKS)
            base = sp.snap(at)
            with sp.Fori(0, n) as j:
                kk = sp.snap(k)
                block = sp.snap(base + j, min_val=0, max_val=BLOCKS - 1)
                ids = g.ids_dram[bass.ds(block * (P * S), P * S)].rearrange("(p s) -> p s", s=S)
                for h in range(2):
                    hold(sp, self.half[h], kk * (16 * HS))
                    sp.dma_start(self.ids[h][:], ids[:, h * HS:(h + 1) * HS]).then_inc(self.landed[h], 16)
                sp.reg_add(k, k, 1)
            sp.reg_add(at, at, wins * WB)
        sp.free_register(at)

    def pool_walk(self, pool, k):
        g = self.g
        with pool.Fori(0, T) as t:
            n = self.count(pool, t)
            with pool.Fori(0, n) as _j:
                kk = pool.snap(k)
                for h in range(2):
                    hold(pool, self.free[h], kk)
                    hold(pool, self.landed[h], (kk + 1) * 16)
                    for s in range(HS):
                        g.nc.gpsimd.indirect_dma_start(
                            out=self.rows[:, h * HS + s, :], out_offset=None, in_=self.table,
                            in_offset=bass.IndirectOffsetOnAxis(ap=self.ids[h][:, s:s + 1], axis=0)
                        ).then_inc(self.half[h], 16)
                pool.reg_add(k, k, 1)


def stage_sage(g, XS, sdego):
    nc = g.nc
    I = g.ins
    with ExitStack() as c:
        H = g.sb("h", [P, T, D], F32, c)
        x2 = g.sb("x2_sorted", [P, T, D + 1], F32, c)
        lists = Lists(g, "sage", c, g.h_tab, D)
        wl_n = g.sb("wl_rows", [D, LAYERS, 2 * D], F32, c)
        wr_n = g.sb("wr_rows", [D, LAYERS, D], F32, c)
        ad_n = g.sb("adapter_rows", [D, D], F32, c)
        w1_n = g.sb("w1_rows", [P, HID // P, D], F32, c)
        w2_n = g.sb("w2_rows", [D, HID], F32, c)
        WL = g.sb("wl", [2 * D, LAYERS, D], F32, c)
        WR = g.sb("wr", [D + 1, LAYERS, 2 * D], F32, c)
        adb = g.sb("adapter_b", [D + 1, D], F32, c)
        lng = g.sb("ln_g", [P, LAYERS, D], F32, c)
        wl = g.sb("wl_now", [2 * D, D], F32, c)
        wr = g.sb("wr_now", [D + 1, 2 * D], F32, c)
        gain = g.sb("gain_now", [P, D], F32, c)
        W1 = g.sb("w1", [D + 1, HID], F32, c)
        W2 = g.sb("w2", [P, HID // P, D], F32, c)
        b2 = g.sb("b2", [1, D], F32, c)
        ones = g.sb("sage_ones", [1, P], F32, c)
        g2 = g.sb("mlp_g", [P, HID], F32, c)
        be2 = g.sb("mlp_be", [P, HID], F32, c)
        neg = g.sb("neg_big", [NP - N, D], F32, c)
        valid = g.sb("valid", [P, T], F32, c)
        rdeg = g.sb("rdeg", [P, T], F32, c)
        rem = g.sb("left", [P, 1], F32, c)
        mask = g.sb("row_mask", [P, S], F32, c)
        masked = g.sb("masked_rows", [P, S, D], F32, c)
        top = [g.sb(f"half_max{h}", [P, D], F32, c) for h in range(2)]
        part = g.sb("block_sum", [P, D], F32, c)
        acc_max = g.sb("acc_max", [P, D], F32, c)
        acc_sum = g.sb("acc_sum", [P, D], F32, c)
        cat = g.sb("cat", [P, 3 * D], F32, c)
        catT = g.sb("cat_turned", [P, P], F32, c)
        hT = g.sb("h_turned", [D + 1, P], F32, c)
        stats = g.sb("bn_stats", [P, 6], F32, c)
        mv = g.sb("mean_var", [P, 2], F32, c)
        root = g.sb("root", [P, 1], F32, c)
        y = g.sb("y", [P, D], F32, c)
        z = g.sb("z", [P, D], F32, c)
        e = g.sb("e", [P, D], F32, c)
        hc = g.sb("h_tile", [P, D], F32, c)
        em = g.sb("mlp_e", [P, HID], F32, c)
        zm = g.sb("mlp_z", [P, HID], F32, c)
        zT = g.sb("mlp_z_turned", [P, HID], F32, c)
        mean = g.sb("sage_mean", [P, T], F32, c)
        var = g.sb("sage_var", [P, T], F32, c)
        ps_t = g.ps("sage_turned", [P, 512], F32, c)
        ps_o = g.ps("sage_out", [P, 512], F32, c)
        ps_w = [g.ps(f"sage_w{b}", [P, 512], F32, c) for b in range(2)]
        loaded = g.sem("sage_weights")
        neg_set = g.sem("sage_neg_set")
        neg_out = g.sem("sage_neg_out")
        x_in = g.sem("sage_x_gathered")
        w_turned = g.sem("sage_w_turned")
        w_moved = g.sem("sage_w_moved")
        prepared = g.sem("sage_prepared")
        scattered = g.sem("sage_scattered")
        cat_ready = g.sem("sage_cat")
        turned = g.sem("sage_cat_turned")
        copied = g.sem("sage_cat_copied")
        out_ready = g.sem("sage_conv")
        var_ready = g.sem("sage_var_ready")
        root_ready = g.sem("sage_root")
        z_ready = g.sem("sage_z")
        e_ready = g.sem("sage_e")
        h_ready = g.sem("sage_h")
        m_h = g.sem("mlp_h")
        m_t = g.sem("mlp_h_turned")
        m_c = g.sem("mlp_h_copied")
        m_1 = g.sem("mlp_hidden")
        m_e = g.sem("mlp_exp")
        m_v = g.sem("mlp_var")
        m_r = g.sem("mlp_root")
        m_z = g.sem("mlp_normed")
        m_zt = g.sem("mlp_z_turned_ready")
        m_zc = g.sem("mlp_z_copied")
        m_o = g.sem("mlp_out")
        f_var = g.sem("sage_final_var")
        f_root = g.sem("sage_final_root")
        LOADS = 15
        turns = [(wl_n[:, l, :], WL[:, l, :], D, 2 * D) for l in range(LAYERS)]
        turns += [(wr_n[:, l, :], WR[0:D, l, 0:D], D, D) for l in range(LAYERS)]
        turns += [(ad_n[:], WR[0:D, 0, D:2 * D], D, D)]
        turns += [(w1_n[:, i, :], W1[0:D, i * P:(i + 1) * P], P, D) for i in range(HID // P)]
        turns += [(w2_n[:, i * P:(i + 1) * P], W2[:, i, :], D, P) for i in range(HID // P)]

        with nc.Block() as block:

            @block.sync
            def _(sp):
                def load(to, frm):
                    sp.dma_start(to, frm).then_inc(loaded, 16)

                def row(ap):
                    return ap.rearrange("(a b) -> a b", a=1)

                load(wl_n[:], I["L2_gnn_conv_wl"].rearrange("l o i -> o l i"))
                load(wr_n[:], I["L2_gnn_conv_wr"].rearrange("l o i -> o l i"))
                load(ad_n[:], I["L2_gnn_adapter_w"])
                load(w1_n[:], I["L2_gnn_mlp_w1"].rearrange("(a p) i -> p a i", p=P))
                load(w2_n[:], I["L2_gnn_mlp_w2"])
                load(W1[D:D + 1, :], row(I["L2_gnn_mlp_b1"]))
                load(b2[:], row(I["L2_gnn_mlp_b2"]))
                load(g2[:], row(I["L2_gnn_mlp_ln_g"]).broadcast_to([P, HID]))
                load(be2[:], row(I["L2_gnn_mlp_ln_b"]).broadcast_to([P, HID]))
                load(adb[D:D + 1, :], row(I["L2_gnn_adapter_b"]))
                load(lng[:], I["L2_gnn_ln_g"].unsqueeze(0).broadcast_to([P, LAYERS, D]))
                load(WR[D:D + 1, :, 0:D], I["L2_gnn_conv_bl"].unsqueeze(0))
                load(WR[D:D + 1, :, D:2 * D], I["L2_gnn_ln_b"].unsqueeze(0))
                sp.wait_ge(neg_set, 1)
                sp.dma_start(g.h_tab[N:NP, :], neg[:]).then_inc(neg_out, 16)
                k = lists.counter(sp, "sage_sp")
                with sp.Fori(0, LAYERS) as _l:
                    lists.sp_walk(sp, k)

            @block.gpsimd
            def _(pool):
                for t in range(T):
                    nc.gpsimd.indirect_dma_start(
                        out=x2[:, t, :], out_offset=None, in_=g.x2_dram,
                        in_offset=bass.IndirectOffsetOnAxis(ap=g.sorted[:, t, 2:3], axis=0)).then_inc(x_in, 16)
                k = lists.counter(pool, "sage_pool")
                pool.wait_ge(neg_out, 16)
                with pool.Fori(0, LAYERS) as l:
                    pool.wait_ge(prepared, 1)
                    hold(pool, h_ready, l * T)
                    for h in range(2):
                        hold(pool, lists.half[h], pool.snap(k) * (16 * HS))
                    for t in range(T):
                        nc.gpsimd.indirect_dma_start(
                            out=g.h_tab, out_offset=bass.IndirectOffsetOnAxis(ap=g.sorted[:, t, 2:3], axis=0),
                            in_=H[:, t, :], in_offset=None, bounds_check=N - 1, oob_is_err=False
                        ).then_inc(scattered, 16)
                    hold(pool, scattered, (l + 1) * (16 * T))
                    lists.pool_walk(pool, k)

            @block.tensor
            def _(pe):
                pe.wait_ge(loaded, 16 * 13)
                for i, (frm, _to, rows, cols) in enumerate(turns):
                    if i >= 2:
                        pe.wait_ge(w_moved, i - 1)
                    nc.tensor.transpose(ps_w[i % 2][0:cols, 0:rows], frm, g.ident[0:rows, 0:rows]).then_inc(w_turned, 1)
                with pe.Fori(0, LAYERS) as l:
                    with pe.Fori(0, T) as t:
                        q = pe.snap(l * T + t)
                        pe.wait_ge(cat_ready, q + 1)
                        nc.tensor.transpose(ps_t[:, 0:P], cat[:, 0:2 * D], g.ident[:])
                        nc.tensor.transpose(ps_t[0:D, P:2 * P], cat[:, 2 * D:3 * D], g.ident[:]).then_inc(turned, 1)
                        pe.wait_ge(copied, q + 1)
                        pe.wait_ge(z_ready, q)
                        nc.tensor.matmul(ps_o[:, 0:2 * D], hT[:], wr[:], start=True, stop=False, skip_group_check=True)
                        nc.tensor.matmul(ps_o[:, 0:D], catT[:], wl[:], start=False, stop=True,
                                         skip_group_check=True).then_inc(out_ready, 1)
                with pe.Fori(0, T) as t:
                    hold(pe, m_h, t + 1)
                    nc.tensor.transpose(ps_t[0:D, 0:P], hc[:], g.ident[:]).then_inc(m_t, 1)
                    pe.wait_ge(m_c, t + 1)
                    nc.tensor.matmul(ps_w[0][:, 0:HID], hT[:], W1[:], start=True, stop=True).then_inc(m_1, 1)
                    pe.wait_ge(m_z, t + 1)
                    for i in range(HID // P):
                        tr = nc.tensor.transpose(ps_w[1][:, i * P:(i + 1) * P], zm[:, i * P:(i + 1) * P], g.ident[:])
                    tr.then_inc(m_zt, 1)
                    pe.wait_ge(m_zc, t + 1)
                    for i in range(HID // P):
                        nc.tensor.matmul(ps_o[:, 0:D], zT[:, i * P:(i + 1) * P], W2[:, i, :], start=(i == 0), stop=False)
                    nc.tensor.matmul(ps_o[:, 0:D], ones[:], b2[:], start=False, stop=True).then_inc(m_o, 1)

            @block.scalar
            def _(act):
                for i, (_frm, to, rows, cols) in enumerate(turns):
                    act.wait_ge(w_turned, i + 1)
                    act.activation(to, ps_w[i % 2][0:cols, 0:rows], ACT.Copy).then_inc(w_moved, 1)

                def conv(q):
                    act.wait_ge(turned, q + 1)
                    act.activation(catT[:], ps_t[:, 0:P], ACT.Copy)
                    act.activation(hT[0:D, :], ps_t[0:D, P:2 * P], ACT.Copy).then_inc(copied, 1)

                def post(q):
                    act.wait_ge(var_ready, q + 1)
                    act.activation(root[:], mv[:, 1:2], ACT.Ln)
                    act.drain()
                    act.activation(root[:], root[:], ACT.Exp, scale=-0.5).then_inc(root_ready, 1)
                    act.wait_ge(z_ready, q + 1)
                    act.activation(e[:], z[:], ACT.Exp, scale=-1.0).then_inc(e_ready, 1)

                with act.Fori(0, LAYERS) as l:
                    with act.Fori(0, T) as t:
                        q = act.snap(l * T + t)
                        conv(q)
                        post(q)
                with act.Fori(0, T) as t:
                    act.wait_ge(m_t, t + 1)
                    act.activation(hT[0:D, :], ps_t[0:D, 0:P], ACT.Copy).then_inc(m_c, 1)
                    act.wait_ge(m_1, t + 1)
                    act.activation(em[:], ps_w[0][:, 0:HID], ACT.Exp, scale=-1.0).then_inc(m_e, 1)
                    act.wait_ge(m_v, t + 1)
                    act.activation(root[:], mv[:, 1:2], ACT.Ln)
                    act.drain()
                    act.activation(root[:], root[:], ACT.Exp, scale=-0.5).then_inc(m_r, 1)
                    act.wait_ge(m_zt, t + 1)
                    act.activation(zT[:], ps_w[1][:, 0:HID], ACT.Copy).then_inc(m_zc, 1)
                act.wait_ge(f_var, 1)
                root_inverse(act, var[:], f_root)

            @block.vector
            def _(v):
                v.memset(neg[:], -BIG).then_inc(neg_set, 1)
                v.memset(ones[:], 1.0)
                v.memset(hT[D:D + 1, :], 1.0)
                v.tensor_scalar(valid[:], g.sdeg[:], 0.0, None, ALU.is_gt)
                v.tensor_scalar(rdeg[:], g.sdeg[:], 1.0, None, ALU.max)
                v.drain()
                v.reciprocal(rdeg[:], rdeg[:])
                v.wait_ge(loaded, 16 * 13)
                for l in range(1, LAYERS):
                    v.tensor_copy(WR[0:D, l, D:2 * D], g.ident[0:D, 0:D])
                v.tensor_tensor(WR[D:D + 1, 0, D:2 * D], WR[D:D + 1, 0, D:2 * D], adb[D:D + 1, :], ALU.add)
                v.wait_ge(w_moved, len(turns))
                v.wait_ge(x_in, 16 * T)
                v.tensor_copy(XS[:], x2[:, :, 0:D])
                v.tensor_copy(sdego[:], x2[:, :, D])
                v.tensor_copy(H[:], x2[:, :, 0:D]).then_inc(prepared, 1)
                k = lists.counter(v, "sage_v")

                def take(kk, h):
                    v.wait_ge(lists.half[h], (kk + 1) * (16 * HS))
                    rows = lists.rows[:, h * HS:(h + 1) * HS, :]
                    v.tensor_reduce(top[h][:], rows.rearrange("p s f -> p f s"), AX, ALU.max)
                    v.tensor_tensor(masked[:, h * HS:(h + 1) * HS, :], rows, bc(mask[:, h * HS:(h + 1) * HS], 2, D),
                                    ALU.mult).then_inc(lists.free[h], 1)

                def post_stats(q):
                    v.wait_ge(out_ready, q)
                    v.bn_stats(stats[:], ps_o[:, 0:D])
                    v.drain()
                    v.bn_aggr(mv[:], stats[:])
                    v.drain()
                    v.tensor_scalar(mv[:, 1:2], mv[:, 1:2], EPS, None, ALU.add).then_inc(var_ready, 1)

                def post_norm(q):
                    v.wait_ge(root_ready, q)
                    v.tensor_scalar(y[:], ps_o[:, 0:D], mv[:, 0:1], root[:, 0:1], ALU.subtract, ALU.mult)
                    v.drain()
                    v.tensor_tensor(y[:], y[:], gain[:], ALU.mult)
                    v.drain()
                    v.tensor_tensor(z[:], y[:], ps_o[:, D:2 * D], ALU.add).then_inc(z_ready, 1)

                def post_silu(q, t):
                    v.wait_ge(e_ready, q)
                    v.tensor_scalar(e[:], e[:], 1.0, None, ALU.add)
                    v.drain()
                    v.reciprocal(e[:], e[:])
                    v.drain()
                    v.tensor_tensor(H[:, bass.ds(t, 1), :].rearrange("p a f -> p (a f)"), z[:], e[:],
                                    ALU.mult).then_inc(h_ready, 1)

                def tile_walk(l, t, first):
                    q = v.snap(l * T + t)
                    n = lists.count(v, t)
                    v.tensor_copy(rem[:], g.sdeg[:, bass.ds(t, 1)])
                    v.drain()
                    v.tensor_scalar(mask[:], g.slot[:, 0:S], rem[:, 0:1], None, ALU.is_lt)
                    v.drain()
                    kk = v.snap(k)
                    take(kk, 0)
                    if not first:
                        post_stats(q)
                    take(kk, 1)
                    if not first:
                        post_norm(q)
                    v.drain()
                    v.tensor_tensor(acc_max[:], top[0][:], top[1][:], ALU.max)
                    v.tensor_reduce(acc_sum[:], masked[:].rearrange("p s f -> p f s"), AX, ALU.add)
                    v.reg_add(k, k, 1)
                    with v.Fori(1, n) as _j:
                        kk = v.snap(k)
                        v.tensor_scalar(rem[:], rem[:], float(-S), None, ALU.add)
                        v.drain()
                        v.tensor_scalar(mask[:], g.slot[:, 0:S], rem[:, 0:1], None, ALU.is_lt)
                        v.drain()
                        take(kk, 0)
                        take(kk, 1)
                        v.drain()
                        v.tensor_reduce(part[:], masked[:].rearrange("p s f -> p f s"), AX, ALU.add)
                        v.tensor_tensor(acc_max[:], acc_max[:], top[0][:], ALU.max)
                        v.drain()
                        v.tensor_tensor(acc_max[:], acc_max[:], top[1][:], ALU.max)
                        v.tensor_tensor(acc_sum[:], acc_sum[:], part[:], ALU.add)
                        v.reg_add(k, k, 1)
                    if not first:
                        post_silu(q, t - 1)
                    v.drain()
                    v.wait_ge(turned, q)
                    v.tensor_scalar(cat[:, 0:D], acc_max[:], valid[:, bass.ds(t, 1)], None, ALU.mult)
                    v.tensor_scalar(cat[:, D:2 * D], acc_sum[:], rdeg[:, bass.ds(t, 1)], None, ALU.mult)
                    v.tensor_copy(cat[:, 2 * D:3 * D], H[:, bass.ds(t, 1), :].rearrange("p a f -> p (a f)")
                                  ).then_inc(cat_ready, 1)

                with v.Fori(0, LAYERS) as l:
                    v.drain()
                    at = bass.ds(l, 1)
                    v.tensor_copy(wl[:], WL[:, at, :].rearrange("p a f -> p (a f)"))
                    v.tensor_copy(wr[:], WR[:, at, :].rearrange("p a f -> p (a f)"))
                    v.tensor_copy(gain[:], lng[:, at, :].rearrange("p a f -> p (a f)"))
                    tile_walk(l, 0, True)
                    with v.Fori(1, T) as t:
                        tile_walk(l, t, False)
                    q = v.snap((l + 1) * T)
                    post_stats(q)
                    post_norm(q)
                    post_silu(q, T - 1)
                v.drain()
                with v.Fori(0, T) as t:
                    v.tensor_copy(hc[:], H[:, bass.ds(t, 1), :].rearrange("p a f -> p (a f)")).then_inc(m_h, 1)
                    v.wait_ge(m_e, t + 1)
                    v.tensor_scalar(em[:], em[:], 1.0, None, ALU.add)
                    v.drain()
                    v.reciprocal(em[:], em[:])
                    v.drain()
                    v.tensor_tensor(zm[:], em[:], ps_w[0][:, 0:HID], ALU.mult)
                    v.drain()
                    v.bn_stats(stats[:], zm[:])
                    v.drain()
                    v.bn_aggr(mv[:], stats[:])
                    v.drain()
                    v.tensor_scalar(mv[:, 1:2], mv[:, 1:2], EPS, None, ALU.add).then_inc(m_v, 1)
                    v.wait_ge(m_r, t + 1)
                    v.tensor_scalar(zm[:], zm[:], mv[:, 0:1], root[:, 0:1], ALU.subtract, ALU.mult)
                    v.drain()
                    v.tensor_tensor(zm[:], zm[:], g2[:], ALU.mult)
                    v.drain()
                    v.tensor_tensor(zm[:], zm[:], be2[:], ALU.add).then_inc(m_z, 1)
                    v.wait_ge(m_o, t + 1)
                    x = XS[:, bass.ds(t, 1), :].rearrange("p a f -> p (a f)")
                    v.tensor_tensor(x, x, ps_o[:, 0:D], ALU.add)
                    v.drain()
                layernorm(v, XS[:], H[:], mean[:], var[:], f_var, 1, 1)
                v.wait_ge(f_root, 1)
                v.tensor_tensor(XS[:], XS[:], bc(var[:], 2, D), ALU.mult)



def flat(ap):
    return ap.rearrange("p a f -> p (a f)")


def stage_sheaf(g, XS, sdego):
    nc = g.nc
    I = g.ins
    M = 2 * S
    GROUPS = -(-T // S)
    OT = GROUPS * S
    ORDER = (0, 1, 3, 2)
    PORDER = (0, 1, 3, 5, 2, 4)
    E4 = S * DD
    with ExitStack() as c:
        lists = Lists(g, "sheaf", c, g.t_tab, TW)
        own = g.sb("own_rows", [P, OT, TW], F32, c)
        own8 = g.sb("own_repeated", [P, 2, S, HH], F32, c)
        agg = g.sb("agg", [P, OT, D], F32, c)
        w1n = g.sb("sheaf_w1_rows", [D, DD], F32, c)
        w1r = g.sb("sheaf_w1", [D, DD], F32, c)
        w2r = g.sb("sheaf_w2", [D, HH], F32, c)
        K = g.sb("sheaf_k", [D, D], F32, c)
        m1n = g.sb("mlp1_rows", [HH, 2, DD, HH], F32, c)
        m1 = g.sb("mlp1_ordered", [HH, 2, DD, HH], F32, c)
        PQ = g.sb("pq", [D + 1, 2 * HH], F32, c)
        m2n = g.sb("mlp2_columns", [P, NPAR], F32, c)
        same = g.sb("same_edge", [P, S], F32, c)
        BD = g.sb("mlp2_blocks", [P, S, NPAR], F32, c)
        mb2n = g.sb("mlp2_b_rows", [P, NPAR], F32, c)
        mb2 = g.sb("mlp2_b", [P, NPAR], F32, c)
        eps = g.sb("epsilons", [P, DD], F32, c)
        coef = g.sb("coefficients", [P, DD], F32, c)
        xt = [g.sb(f"x3_turned{b}", [D, CHUNK * P], F32, c) for b in range(2)]
        xft = [g.sb(f"xf_turned{b}", [D + 1, CHUNK * P], F32, c) for b in range(2)]
        zrow = g.sb("zero_rows", [NP - N, TW], F32, c)
        zh = g.sb("zero_half", [P, 512], F16, c)
        pq = g.sb("block_pq", [P, 2, S, HH], F32, c)
        xj = g.sb("block_x", [P, 2, S, D], F32, c)
        dj = g.sb("block_dis", [P, 2, S], F32, c)
        hT = g.sb("hidden_turned", [P, 2 * P], F32, c)
        Z = g.sb("columns", [P, M * 2, 2, DD], F32, c)
        negs = g.sb("products5", [P, M, 2], F32, c)
        us = g.sb("sums", [P, M, 2], F32, c)
        tp0 = g.sb("products0", [P, M, 2], F32, c)
        pr = g.sb("column_products", [P, M * 2, 2, DD], F32, c)
        inv = g.sb("inverse_norm", [P, M * 2], F32, c)
        cc = g.sb("projection", [P, M * 2], F32, c)
        Wv = g.sb("projected", [P, M * 2, DD], F32, c)
        nn = g.sb("norms", [P, M * 2, 2], F32, c)
        U = g.sb("orthonormal", [P, M * 2, 2, DD], F32, c)
        mm4 = g.sb("map_products", [P, DD, S, DD, DD], F32, c)
        maps = g.sb("maps", [P, DD, S, DD], F32, c)
        wts = g.sb("edge_weights", [P, S], F32, c)
        pm = g.sb("message_products", [P, E4 * D], F32, c)
        part = g.sb("message_sum", [P, D], F32, c)
        rem = g.sb("sheaf_left", [P, 1], F32, c)
        mask = g.sb("sheaf_mask", [P, S], F32, c)
        dis = g.sb("dis", [P, T], F32, c)
        mean = g.sb("sheaf_mean", [P, T], F32, c)
        var = g.sb("sheaf_var", [P, T], F32, c)
        el = g.sb("elu", [P, T, D], F32, c)
        ps_a = [g.ps(f"sheaf_a{b}", [P, 512], F32, c) for b in range(2)]
        ps_b = [g.ps(f"sheaf_b{b}", [P, 512], F32, c) for b in range(2)]
        ps_h = g.ps("sheaf_hidden", [P, 512], F32, c)
        ps_p = g.ps("sheaf_params", [P, 512], F32, c)
        ps_m = g.ps("sheaf_messages", [P, 512], F32, c)
        loaded = g.sem("sheaf_weights")
        z_set = g.sem("sheaf_zero_set")
        z_out = g.sem("sheaf_zero_out")
        same_set = g.sem("sheaf_same_set")
        ordered = g.sem("sheaf_weights_ordered")
        deg_ready = g.sem("sheaf_degrees")
        dis_ready = g.sem("sheaf_dis")
        w_turned = g.sem("sheaf_w_turned")
        w_moved = g.sem("sheaf_w_moved")
        x_turned = g.sem("sheaf_x_turned")
        x_copied = g.sem("sheaf_x_copied")
        f_done = g.sem("sheaf_xf_turned")
        f_copied = g.sem("sheaf_xf_copied")
        rows_done = g.sem("sheaf_rows")
        rows_read = g.sem("sheaf_rows_read")
        table_ready = g.sem("sheaf_own_ready")
        scattered = g.sem("sheaf_table_out")
        loop_in = g.sem("sheaf_loops_copied")
        hid_ready = g.sem("sheaf_hidden_ready")
        relu_ready = g.sem("sheaf_relu_ready")
        par_ready = g.sem("sheaf_params_ready")
        par_read = g.sem("sheaf_params_read")
        nn_ready = g.sem("sheaf_norms")
        rs_ready = g.sem("sheaf_roots")
        edges_done = g.sem("sheaf_edges_done")
        msg_done = g.sem("sheaf_messages_added")
        tile_sum = g.sem("sheaf_tile_sum")
        tile_read = g.sem("sheaf_tile_read")
        e_in = g.sem("sheaf_exp_in")
        e_out = g.sem("sheaf_exp_out")
        f_var = g.sem("final_var")
        f_root = g.sem("final_root")
        final = g.sem("final_ready")
        stored = g.sem("final_stored")
        LOADS = 2 * DD + S + 5

        with nc.Block() as block:

            @block.sync
            def _(sp):
                def load(to, frm):
                    sp.dma_start(to, frm).then_inc(loaded, 16)

                def row(ap):
                    return ap.rearrange("(a b) -> a b", a=1)

                for d in range(DD):
                    load(w1n[d * HH:(d + 1) * HH, :], I["L3_gnn_W1"][d:d + 1, :].broadcast_to([HH, DD]))
                    load(w2r[d * HH:(d + 1) * HH, :], I["L3_gnn_W2"])
                load(m1n[:].rearrange("o a d h -> o (a d h)"), I["L3_gnn_mlp1_w"])
                load(PQ[D:D + 1, 0:HH], row(I["L3_gnn_mlp1_b"]))
                with nc.allow_non_contiguous_dma(reason="96 numbers, once for each slot"):
                    for s in range(S):
                        load(m2n[s * HH:(s + 1) * HH, :], I["L3_gnn_mlp2_w"].rearrange("n h -> h n"))
                load(mb2n[:], row(I["L3_gnn_mlp2_b"]).broadcast_to([P, NPAR]))
                load(eps[:], row(I["L3_gnn_epsilons"]).broadcast_to([P, DD]))
                sp.wait_ge(z_set, 1)
                load(PQ[D:D + 1, HH:2 * HH], zrow[0:1, 0:HH])
                sp.dma_start(g.t_tab[N:NP, :], zrow[:]).then_inc(z_out, 16)
                k = lists.counter(sp, "sheaf_sp")
                lists.sp_walk(sp, k)

            @block.gpsimd
            def _(pool):
                k = lists.counter(pool, "sheaf_pool")
                nc.gpsimd.memset(same[:], 1.0)
                pool.drain()
                nc.gpsimd.affine_select(out=same[:], in_=same[:], compare_op=ALU.is_ge, fill=0.0, base=0,
                                        pattern=[[-HH, S]], channel_multiplier=1)
                pool.drain()
                nc.gpsimd.affine_select(out=same[:], in_=same[:], compare_op=ALU.is_ge, fill=0.0, base=HH - 1,
                                        pattern=[[HH, S]], channel_multiplier=-1).then_inc(same_set, 1)
                pool.wait_ge(z_out, 16)
                pool.wait_ge(table_ready, 1)
                for t in range(T):
                    nc.gpsimd.indirect_dma_start(
                        out=g.t_tab, out_offset=bass.IndirectOffsetOnAxis(ap=g.sorted[:, t, 2:3], axis=0),
                        in_=own[:, t, :], in_offset=None, bounds_check=N - 1, oob_is_err=False
                    ).then_inc(scattered, 16)
                pool.wait_ge(scattered, 16 * T)
                lists.pool_walk(pool, k)
                pool.wait_ge(final, 1)
                for t in range(T):
                    nc.gpsimd.indirect_dma_start(
                        out=g.out, out_offset=bass.IndirectOffsetOnAxis(ap=g.sorted[:, t, 2:3], axis=0),
                        in_=XS[:, t, :], in_offset=None, bounds_check=N - 1, oob_is_err=False
                    ).then_inc(stored, 16)
                pool.wait_ge(stored, 16 * T)

            @block.tensor
            def _(pe):
                pe.wait_ge(loaded, 16 * LOADS)
                pe.wait_ge(ordered, 1)
                for i in range(2):
                    nc.tensor.transpose(ps_a[i][0:D, 0:HH], m1[:, i].rearrange("o d h -> o (d h)"),
                                        g.ident[0:HH, 0:HH]).then_inc(w_turned, 1)
                pe.wait_ge(w_moved, 2)
                for ch, (t0, n) in enumerate(CHUNKS):
                    b = ch % 2
                    for j in range(n):
                        tr = nc.tensor.transpose(ps_a[b][0:D, j * P:(j + 1) * P], XS[:, t0 + j, :], g.ident[:])
                    tr.then_inc(x_turned, 1)
                    pe.wait_ge(x_copied, ch + 1)
                    nc.tensor.matmul(ps_a[b][0:D, 0:n * P], K[:], xt[b][:, 0:n * P], start=True, stop=True).then_inc(f_done, 1)
                    pe.wait_ge(f_copied, ch + 1)
                    if ch >= 2:
                        pe.wait_ge(rows_read, ch - 1)
                    for j in range(n):
                        at = slice(j * P, (j + 1) * P)
                        nc.tensor.matmul(ps_b[b][:, j * P:j * P + D], xt[b][:, at], K[:], start=True, stop=True)
                        mm = nc.tensor.matmul(ps_b[b][:, j * P + D:j * P + D + 2 * HH], xft[b][:, at], PQ[:],
                                              start=True, stop=True)
                    mm.then_inc(rows_done, 1)

                def params(i, ve, ue):
                    for h, two in enumerate((ve, ue)):
                        for a, x in enumerate(two):
                            mm = nc.tensor.matmul(ps_h[:, h * P:(h + 1) * P], x, g.ident[:], start=(a == 0), stop=(a == 1))
                    mm.then_inc(hid_ready, 1)
                    pe.wait_ge(relu_ready, i + 1)
                    pe.wait_ge(par_read, i)
                    for h in range(2):
                        mm = nc.tensor.matmul(ps_p[:, h * S * NPAR:(h + 1) * S * NPAR], hT[:, h * P:(h + 1) * P],
                                              BD[:].rearrange("p s n -> p (s n)"), start=True, stop=True)
                    mm.then_inc(par_ready, 1)

                def messages(i):
                    pe.wait_ge(edges_done, i)
                    for q in range(E4 * D // 512):
                        mm = nc.tensor.matmul(ps_m[:], g.ident[:], pm[:, q * 512:(q + 1) * 512], start=False, stop=False,
                                              skip_group_check=True)
                    mm.then_inc(msg_done, 1)

                def clear():
                    nc.tensor.matmul(ps_m[:], zh[:, 0:P], zh[:], start=True, stop=False, skip_group_check=True)

                def close():
                    nc.tensor.matmul(ps_m[:], zh[:, 0:P], zh[:], start=False, stop=True,
                                     skip_group_check=True).then_inc(tile_sum, 1)

                pe.wait_ge(table_ready, 1)
                both = tuple(pq[:, h].rearrange("p s h -> p (s h)") for h in range(2))
                flat8 = tuple(own8[:, h].rearrange("p s h -> p (s h)") for h in range(2))
                for i in range(GROUPS):
                    pe.wait_ge(loop_in, i + 1)
                    params(i, both, both)
                k = lists.counter(pe, "sheaf_pe")

                def edge_block():
                    i = pe.snap(k) + GROUPS
                    for h in range(2):
                        pe.wait_ge(lists.free[h], pe.snap(k) + 1)
                    params(i, (both[1], flat8[0]), (both[0], flat8[1]))
                    return i

                def tile(t, first):
                    n = lists.count(pe, t)
                    i = edge_block()
                    if not first:
                        messages(i)
                        close()
                        pe.wait_ge(tile_read, t)
                    clear()
                    pe.reg_add(k, k, 1)
                    with pe.Fori(1, n) as _j:
                        messages(edge_block())
                        pe.reg_add(k, k, 1)

                tile(0, True)
                with pe.Fori(1, T) as t:
                    tile(t, False)
                messages(pe.snap(k) + GROUPS)
                close()

            @block.scalar
            def _(act):
                for i in range(2):
                    act.wait_ge(w_turned, i + 1)
                    act.activation(PQ[0:D, i * HH:(i + 1) * HH], ps_a[i][0:D, 0:HH], ACT.Copy).then_inc(w_moved, 1)
                act.wait_ge(deg_ready, 1)
                root_inverse(act, dis[:], dis_ready)
                act.activation(coef[:], eps[:], ACT.Exp, scale=2.0).then_inc(dis_ready, 1)
                for ch, (t0, n) in enumerate(CHUNKS):
                    b = ch % 2
                    act.wait_ge(x_turned, ch + 1)
                    if ch >= 2:
                        act.wait_ge(rows_done, ch - 1)
                    act.activation(xt[b][:, 0:n * P], ps_a[b][0:D, 0:n * P], ACT.Copy).then_inc(x_copied, 1)
                    act.wait_ge(f_done, ch + 1)
                    act.activation(xft[b][0:D, 0:n * P], ps_a[b][0:D, 0:n * P], ACT.Copy).then_inc(f_copied, 1)

                def relu(i):
                    act.wait_ge(hid_ready, i + 1)
                    act.activation(hT[:], ps_h[:, 0:2 * P], ACT.Relu).then_inc(relu_ready, 1)

                def roots(i):
                    act.wait_ge(nn_ready, i + 1)
                    act.activation(nn[:], nn[:], ACT.Ln)
                    act.drain()
                    act.activation(nn[:], nn[:], ACT.Exp, scale=-0.5).then_inc(rs_ready, 1)

                act.wait_ge(table_ready, 1)
                for i in range(GROUPS):
                    if i:
                        act.wait_ge(par_ready, i)
                    act.activation(pq[:], own[:, i * S:(i + 1) * S, D:D + 2 * HH].rearrange("p s (c h) -> p c s h", c=2),
                                   ACT.Copy).then_inc(loop_in, 1)
                    relu(i)
                    roots(i)
                act.wait_ge(par_ready, GROUPS)
                k = lists.counter(act, "sheaf_act")
                with act.Fori(0, T) as t:
                    n = lists.count(act, t)
                    act.activation(own8[:], bc(own[:, bass.ds(t, 1), D:D + 2 * HH].rearrange("p a (c h) -> p (a c) h", c=2), 2, S),
                                   ACT.Copy)
                    with act.Fori(0, n) as _j:
                        kk = act.snap(k)
                        b = act.snap(kk % 2, min_val=0, max_val=1)
                        act.wait_ge(edges_done, kk + GROUPS - 1)
                        for h in range(2):
                            act.wait_ge(lists.half[h], (kk + 1) * (16 * HS))
                            at = slice(h * HS, (h + 1) * HS)
                            rows = lists.rows[:, at, :]
                            act.activation(pq[:, :, at, :], rows[:, :, D:D + 2 * HH].rearrange("p s (c h) -> p c s h", c=2),
                                           ACT.Copy)
                            act.activation(dj[:, bass.ds(b, 1), at].rearrange("p a s -> p (a s)"), rows[:, :, TW - 1], ACT.Copy)
                            act.activation(xj[:, bass.ds(b, 1), at, :].rearrange("p a s f -> p (a s) f"), rows[:, :, 0:D],
                                           ACT.Copy).then_inc(lists.free[h], 1)
                        relu(kk + GROUPS)
                        roots(kk + GROUPS)
                        act.reg_add(k, k, 1)
                act.wait_ge(e_in, 1)
                act.activation(el[:], el[:], ACT.Exp).then_inc(e_out, 1)
                act.wait_ge(f_var, 1)
                root_inverse(act, var[:], f_root)

            @block.vector
            def _(v):
                def tt(to, a, b, op):
                    return v.tensor_tensor(to, a, b, op)

                z8 = Z[:].rearrange("p (m q) v k -> p m (q v k)", q=2)

                v.memset(zrow[:], 0.0).then_inc(z_set, 1)
                v.memset(zh[:], 0.0)
                v.memset(xft[0][D:D + 1, :], 1.0)
                v.memset(xft[1][D:D + 1, :], 1.0)
                v.memset(own[:, T:OT, :], 0.0)
                v.memset(Z[:], 0.0)
                v.drain()
                for i in (0, 5, 11, 14):
                    v.memset(z8[:, :, i], 1.0)
                v.tensor_scalar(dis[:], sdego[:], 1.0, None, ALU.add).then_inc(deg_ready, 1)
                v.wait_ge(loaded, 16 * LOADS)
                for i, o in enumerate(ORDER):
                    v.tensor_copy(w1r[:, i:i + 1], w1n[:, o:o + 1])
                    v.tensor_copy(m1[:, :, i, :], m1n[:, :, o, :])
                v.wait_ge(same_set, 1)
                for i, o in enumerate(PORDER):
                    v.tensor_scalar(BD[:, :, i], same[:], m2n[:, o:o + 1], None, ALU.mult)
                    v.tensor_copy(mb2[:, i:i + 1], mb2n[:, o:o + 1])
                v.drain()
                tt(K[:].rearrange("p (k f) -> p k f", k=DD), bc(w1r[:], 2, HH), bc(w2r[:], 1, DD), ALU.mult).then_inc(ordered, 1)
                v.wait_ge(dis_ready, 2)
                v.tensor_scalar(coef[:], coef[:], 1.0, None, ALU.add)
                v.drain()
                v.reciprocal(coef[:], coef[:])
                v.drain()
                v.tensor_scalar(coef[:], coef[:], -2.0, 3.0, ALU.mult, ALU.add)
                for ch, (t0, n) in enumerate(CHUNKS):
                    v.wait_ge(rows_done, ch + 1)
                    frm = ps_b[ch % 2][:, 0:n * P].rearrange("p (t f) -> p t f", f=P)
                    v.tensor_copy(own[:, t0:t0 + n, 0:TW - 1], frm[:, :, 0:TW - 1]).then_inc(rows_read, 1)
                v.tensor_copy(own[:, 0:T, TW - 1], dis[:])
                v.drain()
                v.nop().then_inc(table_ready, 1)

                par = ps_p[:, 0:M * NPAR].rearrange("p (m n) -> p m n", n=NPAR)
                u4 = U[:].rearrange("p (m q) v k -> p m (q v) k", q=2)

                def edge_maps(i, between=None):
                    v.wait_ge(par_ready, i + 1)
                    tt(z8[:, :, 1:4], par[:, :, 0:3], bc(mb2[:, 0:3], 1, M), ALU.add)
                    tt(z8[:, :, 6:8], par[:, :, 4:6], bc(mb2[:, 4:6], 1, M), ALU.add)
                    v.scalar_tensor_tensor(z8[:, :, 10:14:3], par[:, :, 3:5], -1.0, bc(mb2[:, 3:5], 1, M),
                                           ALU.mult, ALU.subtract)
                    tt(us[:, :, 1], par[:, :, 1], mb2[:, 1:2].broadcast_to([P, M]), ALU.add).then_inc(par_read, 1)
                    v.drain()
                    tt(negs[:, :, 0], z8[:, :, 10], z8[:, :, 13], ALU.mult)
                    tt(negs[:, :, 1], z8[:, :, 10], z8[:, :, 2], ALU.mult)
                    v.drain()
                    tt(z8[:, :, 9], negs[:, :, 0], z8[:, :, 7], ALU.subtract)
                    tt(us[:, :, 0], negs[:, :, 1], z8[:, :, 3], ALU.add)
                    v.drain()
                    tt(tp0[:], z8[:, :, 9:14:4], z8[:, :, 1:2].broadcast_to([P, M, 2]), ALU.mult)
                    v.drain()
                    v.scalar_tensor_tensor(z8[:, :, 8:13:4], tp0[:], -1.0, us[:], ALU.mult, ALU.subtract)
                    v.drain()
                    tt(pr[:], Z[:], bc(Z[:, :, 0, :], 2, 2), ALU.mult)
                    v.drain()
                    v.tensor_reduce(nn[:].rearrange("p m v -> p (m v)"), pr[:].rearrange("p m v k -> p (m v) k"), AX, ALU.add)
                    v.drain()
                    v.reciprocal(inv[:], nn[:, :, 0])
                    v.drain()
                    tt(cc[:], nn[:, :, 1], inv[:], ALU.mult)
                    v.drain()
                    tt(pr[:, :, 0, :], bc(cc[:], 2, DD), Z[:, :, 0, :], ALU.mult)
                    v.drain()
                    tt(Wv[:], Z[:, :, 1, :], pr[:, :, 0, :], ALU.subtract)
                    v.drain()
                    tt(pr[:, :, 1, :], Wv[:], Wv[:], ALU.mult)
                    v.drain()
                    v.tensor_reduce(nn[:, :, 1], pr[:, :, 1, :], AX, ALU.add).then_inc(nn_ready, 1)
                    if between:
                        between()
                    v.wait_ge(rs_ready, i + 1)
                    n4 = nn[:, 0:2 * S, :].rearrange("p (s q) v -> p s (q v)", q=2)
                    tt(n4, n4, bc(wts[:], 2, DD), ALU.mult)
                    v.drain()
                    tt(U[:, :, 0, :], Z[:, :, 0, :], bc(nn[:, :, 0], 2, DD), ALU.mult)
                    tt(U[:, :, 1, :], Wv[:], bc(nn[:, :, 1], 2, DD), ALU.mult)
                    v.drain()
                    for a in range(DD):
                        tt(mm4[:, a], bc(u4[:, 0:S, a, :], 2, DD), u4[:, S:M], ALU.mult)
                    v.drain()
                    v.tensor_reduce(maps[:].rearrange("p a s b -> p (a s b)"),
                                    mm4[:].rearrange("p a s b k -> p (a s b) k"), AX, ALU.add)
                    v.drain()

                pm4 = pm[:].rearrange("p (s d b) -> p s d b", s=S, b=DD)
                for i in range(GROUPS):
                    v.tensor_copy(wts[:], own[:, i * S:(i + 1) * S, TW - 1])
                    v.drain()
                    edge_maps(i)
                    for s in range(S):
                        x = own[:, i * S + s, 0:D].rearrange("p (b h) -> p h b", b=DD)
                        tt(pm4[:, s].rearrange("p (a h) b -> p a h b", a=DD),
                           bc(maps[:, :, s, :], 2, HH), bc(x, 1, DD), ALU.mult)
                    v.drain()
                    v.tensor_reduce(agg[:, i * S:(i + 1) * S, :].rearrange("p s d -> p (s d)"),
                                    pm[:].rearrange("p (e b) -> p e b", b=DD), AX, ALU.add).then_inc(edges_done, 1)
                    v.drain()

                k = lists.counter(v, "sheaf_v")

                def take_sums(t):
                    v.wait_ge(tile_sum, t)
                    v.tensor_reduce(part[:], ps_m[:].rearrange("p (e d) -> p d e", d=D), AX, ALU.add).then_inc(tile_read, 1)
                    v.drain()
                    to = agg[:, bass.ds(t - 1, 1), :].rearrange("p a f -> p (a f)")
                    tt(to, to, part[:], ALU.add)

                def edge_block(between):
                    kk = v.snap(k)
                    b = v.snap(kk % 2, min_val=0, max_val=1)
                    v.tensor_scalar(rem[:], rem[:], float(-S), None, ALU.add)
                    v.drain()
                    v.tensor_scalar(mask[:], g.slot[:, 0:S], rem[:, 0:1], None, ALU.is_lt)
                    for h in range(2):
                        v.wait_ge(lists.free[h], kk + 1)
                    v.tensor_copy(wts[:], dj[:, bass.ds(b, 1), :].rearrange("p a s -> p (a s)"))
                    v.drain()
                    tt(wts[:], wts[:], mask[:], ALU.mult)
                    edge_maps(kk + GROUPS, between)
                    v.wait_ge(msg_done, kk)
                    tt(pm[:].rearrange("p (e a h) -> p e a h", e=E4, a=DD),
                       bc(maps[:].rearrange("p a s b -> p (s b) a"), 3, HH),
                       bc(xj[:, bass.ds(b, 1), :, :].rearrange("p a s (b h) -> p (a s b) h", b=DD), 2, DD),
                       ALU.mult).then_inc(edges_done, 1)
                    v.reg_add(k, k, 1)

                def tile(t, first):
                    n = lists.count(v, t)
                    v.tensor_scalar(rem[:], g.sdeg[:, bass.ds(t, 1)], float(S), None, ALU.add)
                    v.drain()
                    edge_block(None if first else lambda: take_sums(t))
                    with v.Fori(1, n) as _j:
                        edge_block(None)

                tile(0, True)
                with v.Fori(1, T) as t:
                    tile(t, False)
                take_sums(T)
                v.drain()
                a = agg[:, 0:T, :]
                tt(a, a, bc(dis[:], 2, D), ALU.mult)
                v.drain()
                v.tensor_scalar(el[:], a, 0.0, None, ALU.min).then_inc(e_in, 1)
                for d in range(DD):
                    at = slice(d * HH, (d + 1) * HH)
                    v.tensor_scalar(XS[:, :, at], XS[:, :, at], coef[:, d:d + 1], None, ALU.mult)
                v.drain()
                v.tensor_scalar(a, a, 0.0, -1.0, ALU.max, ALU.add)
                v.wait_ge(e_out, 1)
                v.drain()
                tt(a, a, el[:], ALU.add)
                v.drain()
                for i, o in enumerate(ORDER):
                    x = XS[:, :, o * HH:(o + 1) * HH]
                    tt(x, x, agg[:, 0:T, i * HH:(i + 1) * HH], ALU.subtract)
                v.drain()
                layernorm(v, XS[:], el[:], mean[:], var[:], f_var, 1, 1)
                v.wait_ge(f_root, 1)
                tt(XS[:], XS[:], bc(var[:], 2, D), ALU.mult).then_inc(final, 1)


def build(nc, ins, out, upto=99):
    with ExitStack() as ctx:
        g = Program(nc, ctx, ins, out)
        stage_graph(g)
        if upto < 2:
            return g
        stage_lists(g)
        if upto < 3:
            return g
        with ExitStack() as c:
            A = g.sb("adjacency", [P, T, NP], F16, c)
            stage_adjacency(g, A, c)
            if upto < 4:
                return g
            X = g.sb("x", [P, T, D], F32, c)
            stage_appnp(g, A, X, c)
            if upto < 5:
                return g
            stage_turn(g, A)
            stage_lightgcn(g, A, X)
        if upto < 6:
            return g
        XS = g.sb("x_sorted", [P, T, D], F32)
        sdego = g.sb("dego_sorted", [P, T], F32)
        stage_sage(g, XS, sdego)
        if upto < 7:
            return g
        stage_sheaf(g, XS, sdego)
        return g


def kernel(**inputs):
    import concourse.bacc as bacc
    from concourse.bass_utils import run_bass_kernel_spmd

    nc = bacc.Bacc("TRN2", target_bir_lowering=False, num_devices=1)
    arrays, aps = {}, {}
    for name, value in inputs.items():
        a = np.ascontiguousarray(value)
        arrays["in_" + name] = a
        aps[name] = nc.dram_tensor("in_" + name, a.shape, mybir.dt.from_np(a.dtype), kind="ExternalInput").ap()
    out = nc.dram_tensor("out", [N, D], F32, kind="ExternalOutput").ap()
    build(nc, aps, out)
    result = run_bass_kernel_spmd(nc, [arrays], core_ids=[0])
    return result.results[0]["out"]
```

```python
from contextlib import ExitStack

import numpy as np

import concourse.bass as bass
from concourse import mybir

F32 = mybir.dt.float32
F16 = mybir.dt.float16
I32 = mybir.dt.int32
ALU = mybir.AluOpType
ACT = mybir.ActivationFunctionType
AX = mybir.AxisListType.X

P = 128
N = 3125
E = 103125
D = 64
T = -(-N // P)
NP = T * P
TAIL = N - (T - 1) * P
EC = -(-E // P)
DUMMY = NP - 1
NOHI = 63
HC = 13
HSTEPS = EC // HC
W = 64
S = 8
HS = S // 2
TT = T + T % 2
PAIRS = TT // 2
GN = 16
GSTEPS = P // GN
STEPS = PAIRS * GSTEPS
CAP = 4000
KEY = 4096
MINBLK = 3
WB = W // S
BLOCKS = WB * (E // W + 1 + sum(E // (P * t) // W + 1 for t in range(1, T)))
CHUNK = 4
CHUNKS = [(c, min(CHUNK, T - c)) for c in range(0, T, CHUNK)]
NC = len(CHUNKS)
LOSCALE = 2048.0
ROUNDS = 10
ALPHA = 0.1
HOPS = 3
LAYERS = 5
HID = 4 * D
EPS = 1e-5
BIG = 3.0e38
DD, HH = 4, 16
NPAR = DD * (DD - 1) // 2
TW = D + 2 * HH
assert EC == HC * HSTEPS and W % S == 0 and DD * HH == D


def bc(ap, axis, n):
    x = ap.unsqueeze(axis)
    shape = list(x.shape)
    shape[axis] = n
    return x.broadcast_to(shape)


HELD = []


class Program:

    def __init__(self, nc, ctx, ins, out):
        self.nc, self.ctx, self.ins, self.out = nc, ctx, ins, out

        def dram(name, shape, dt):
            return nc.dram_tensor(name, shape, dt, kind="Internal").ap()

        HELD[:] = [self.sem("held")]
        self.src_pad = dram("src_pad", [E + P], I32)
        self.key_row = dram("key_row", [NP], F32)
        self.perm_tab = dram("perm_tab", [NP, 4], I32)
        self.ids_dram = dram("ids_blocks", [BLOCKS * P * S], I32)
        self.x2_dram = dram("x2_rows", [NP, D + 1], F32)
        self.h_tab = dram("h_tab", [NP, D], F32)
        self.t_tab = dram("t_tab", [NP, TW], F32)

        sb = self.sb
        self.norm_var = self.sem("norm_variances")
        self.norm_root = self.sem("norm_roots")
        self.ident = sb("ident", [P, P], F32)
        self.identh = sb("identh", [P, P], F16)
        self.comb = sb("comb", [P, D], F32)
        self.codes = sb("codes", [P, P, GN], F16)
        self.slot = sb("slot", [P, W], F32)
        self.deg = sb("deg", [P, T], F32)
        self.start = sb("start", [P, T], F32)
        self.sorted = sb("sorted_tab", [P, T, 4], I32)
        self.sdeg = sb("sdeg", [P, T], F32)
        self.nblk = sb("nblk", [1, T + 1], I32)
        self.npair = sb("npair", [1, 1], I32)
        self.nwin = sb("nwin", [1, T], I32)
        self.nlast = sb("nlast", [1, T], I32)
        self.nempty = sb("nempty", [1, T], I32)
        self.nsign = [sb(f"nsign{h}", [1, T], I32) for h in range(2)]
        self.nwall = sb("nwall", [1, 1], I32)
        self.dego = sb("dego", [P, T], F32)
        self.win_starts = self.sem("window_starts")
        self.win_landed = self.sem("windows_landed")

    def windows(self, c):
        self.cur = self.sb("cur_start", [P, TT], F32, c)
        self.left = self.sb("cur_left", [P, TT], F32, c)
        self.first = self.sb("cur_start_i", [P, TT], I32, c)
        self.win = self.sb("node_windows", [P, TT, W], I32, c)

    def sb(self, name, shape, dt, ctx=None):
        return (ctx or self.ctx).enter_context(self.nc.sbuf_tensor(name, shape, dt))

    def ps(self, name, shape, dt, ctx):
        return ctx.enter_context(self.nc.psum_tensor(name, shape, dt))

    def sem(self, name):
        return self.ctx.enter_context(self.nc.semaphore(name))


def hold(eng, sem, value):
    eng.wait_ge(sem, value)
    eng.sem_inc(HELD[0], 1)


def one_hots(v, lo_out, hi_out, codes, lo, hi, n):
    v.tensor_tensor(lo_out, codes[:, 0:P, 0:n], bc(lo, 1, P), ALU.is_equal)
    return v.tensor_tensor(hi_out, codes[:, 0:T, 0:n], bc(hi, 1, T), ALU.is_equal)


def stage_graph(g, A):
    nc = g.nc
    src, dst = g.ins["src"], g.ins["dst"]
    with ExitStack() as c:
        dst_sb = g.sb("dst_sb", [P, EC], I32, c)
        lo = g.sb("dst_lo", [P, EC], I32, c)
        hi = g.sb("dst_hi", [P, EC], I32, c)
        lo16 = g.sb("dst_lo16", [P, EC], F16, c)
        hi16 = g.sb("dst_hi16", [P, EC], F16, c)
        oh_lo = g.sb("oh_lo", [P, 2, P, HC], F16, c)
        oh_hi = g.sb("oh_hi", [P, 2, T, HC], F16, c)
        zh = g.sb("zh", [P, P], F16, c)
        tri = g.sb("tri", [P, P], F32, c)
        ones = g.sb("ones", [P, P], F32, c)
        zt = g.sb("zt", [P, T], F32, c)
        incl = g.sb("incl", [P, T], F32, c)
        excl = g.sb("excl", [P, T], F32, c)
        nid = g.sb("nid", [P, T], F32, c)
        nkey = g.sb("nkey", [P, T], F32, c)
        key = g.sb("key", [P, T], F32, c)
        keys = g.sb("keys", [P, NP], F32, c)
        gt = A[:, 0:2, :]
        rank = g.sb("rank", [P, T], F32, c)
        ranki = g.sb("ranki", [P, T], I32, c)
        tab = g.sb("tab", [P, T, 4], I32, c)
        zsrc = g.sb("zsrc", [1, P], I32, c)
        tmax = g.sb("tmax", [T, 1], F32, c)
        allmax = g.sb("allmax", [1, T], F32, c)
        maxi = g.sb("maxi", [1, T], I32, c)
        one = g.sb("one", [1, 1], F32, c)
        onei = g.sb("onei", [1, 1], I32, c)
        hist = g.ps("hist", [P, 512], F32, c)
        pre = g.ps("pre", [P, 512], F32, c)
        mt = g.ps("mt", [P, 512], F32, c)
        mt2 = g.ps("mt2", [P, 512], F32, c)
        fills = g.sem("fills_set")
        loaded = g.sem("dst_loaded")
        const = g.sem("graph_constants")
        coded = g.sem("dst_coded")
        counted = g.sem("dst_counted")
        hist_done = g.sem("histogram_done")
        deg_done = g.sem("degrees_copied")
        pre_done = g.sem("prefix_done")
        key_done = g.sem("keys_computed")
        key_out = g.sem("keys_stored")
        key_in = g.sem("keys_loaded")
        ranked = g.sem("nodes_ranked")
        scattered = g.sem("rows_scattered")
        tab_in = g.sem("sorted_loaded")
        sdeg_done = g.sem("sorted_degrees")
        max_t = g.sem("degrees_transposed")
        max_d = g.sem("tile_maxima")
        max_r = g.sem("maxima_row")
        pad_out = g.sem("src_pad_stored")
        counts = g.sem("block_counts")

        with nc.Block() as block:

            @block.sync
            def _(sp):
                full = (P - 1) * EC
                sp.wait_ge(fills, 1)
                sp.dma_start(dst_sb[0:P - 1, :], dst[0:full].rearrange("(p j) -> p j", j=EC)).then_inc(loaded, 16)
                sp.dma_start(dst_sb[P - 1:P, 0:E - full], dst[full:E].rearrange("(p j) -> p j", p=1)).then_inc(loaded, 16)
                sp.dma_start(g.src_pad[0:E].rearrange("(a b) -> a b", a=125), src.rearrange("(a b) -> a b", a=125)).then_inc(pad_out, 16)
                sp.wait_ge(fills, 2)
                sp.dma_start(g.src_pad[E:E + P].rearrange("(a b) -> a b", a=1), zsrc[:]).then_inc(pad_out, 16)
                hold(sp, key_done, 1)
                with nc.allow_non_contiguous_dma(reason="keys in order of nodes, once"):
                    sp.dma_start(g.key_row.rearrange("(t p) -> p t", p=P), key[:]).then_inc(key_out, 16)
                sp.wait_ge(key_out, 16)
                sp.dma_start(keys[:], g.key_row.rearrange("(a n) -> a n", a=1).broadcast_to([P, NP])).then_inc(key_in, 16)
                sp.wait_ge(scattered, 16 * T)
                sp.dma_start(g.sorted[:], g.perm_tab.rearrange("(t p) c -> p t c", p=P)).then_inc(tab_in, 16)
                sp.wait_ge(pad_out, 32)

            @block.gpsimd
            def _(pool):
                nc.gpsimd.memset(dst_sb[:], NOHI * P).then_inc(fills, 1)
                nc.gpsimd.memset(zsrc[:], 0).then_inc(fills, 1)
                nc.gpsimd.iota(g.codes[:], [[1, P], [0, GN]], channel_multiplier=0, allow_small_or_imprecise_dtypes=True)
                nc.gpsimd.iota(g.slot[:], [[1, W]], channel_multiplier=0, allow_small_or_imprecise_dtypes=True)
                nc.gpsimd.iota(nid[:], [[P, T]], channel_multiplier=1, allow_small_or_imprecise_dtypes=True)
                nc.gpsimd.memset(tab[:], 0)
                nc.gpsimd.memset(g.ident[:], 0.0)
                nc.gpsimd.memset(g.comb[:], 0.0)
                nc.gpsimd.memset(tri[:], 1.0)
                pool.drain()
                nc.gpsimd.affine_select(out=g.ident[:], in_=g.ident[:], compare_op=ALU.not_equal, fill=1.0, base=0,
                                        pattern=[[-1, P]], channel_multiplier=1)
                nc.gpsimd.affine_select(out=tri[:], in_=tri[:], compare_op=ALU.is_gt, fill=0.0, base=0,
                                        pattern=[[1, P]], channel_multiplier=-1)
                nc.gpsimd.affine_select(out=g.comb[:], in_=g.comb[:], compare_op=ALU.not_equal, fill=1.0, base=0,
                                        pattern=[[-1, D]], channel_multiplier=1)
                pool.drain()
                nc.gpsimd.affine_select(out=g.comb[:], in_=g.comb[:], compare_op=ALU.not_equal, fill=1.0 / LOSCALE,
                                        base=-D, pattern=[[-1, D]], channel_multiplier=1)
                nc.gpsimd.tensor_copy(g.identh[:], g.ident[:]).then_inc(const, 1)
                pool.wait_ge(g.win_starts, 1)
                pool.wait_ge(pad_out, 32)
                src_rows = g.src_pad.rearrange("(a e) -> a e", a=1)
                for t in range(T):
                    nc.gpsimd.indirect_dma_start(
                        out=g.win[:, t, :], out_offset=None, in_=src_rows,
                        in_offset=bass.IndirectOffsetOnAxis(ap=g.first[:, t:t + 1], axis=1)).then_inc(g.win_landed, 16)
                pool.wait_ge(ranked, 1)
                for t in range(T):
                    nc.gpsimd.indirect_dma_start(
                        out=g.perm_tab, out_offset=bass.IndirectOffsetOnAxis(ap=ranki[:, t:t + 1], axis=0),
                        in_=tab[:, t, :], in_offset=None).then_inc(scattered, 16)
                pool.wait_ge(scattered, 16 * T)

            @block.vector
            def _(v):
                v.memset(zh[:], 0.0)
                v.memset(ones[:], 1.0)
                v.memset(one[:], 1.0)
                v.memset(zt[:], 0.0)
                v.memset(g.cur[:], 0.0)
                v.memset(g.left[:], 0.0)
                v.memset(g.win[:, T:TT, :], 0)
                v.wait_ge(const, 1)
                v.wait_ge(loaded, 32)
                v.tensor_scalar(lo[:], dst_sb[:], P - 1, None, ALU.bitwise_and)
                v.tensor_scalar(hi[:], dst_sb[:], 7, None, ALU.logical_shift_right)
                v.drain()
                v.tensor_copy(lo16[:], lo[:])
                v.tensor_copy(hi16[:], hi[:])
                v.drain()
                with v.Fori(0, HSTEPS // 2) as i:
                    for b in range(2):
                        v.wait_ge(counted, 2 * i + b)
                        at = bass.ds((2 * i + b) * HC, HC)
                        one_hots(v, oh_lo[:, b], oh_hi[:, b], g.codes, lo16[:, at], hi16[:, at], HC).then_inc(coded, 1)
                v.wait_ge(hist_done, 1)
                v.tensor_copy(g.deg[:], hist[:, 0:T])
                v.drain()
                v.tensor_tensor_scan(incl[:], g.deg[:], zt[:], 0.0, ALU.add, ALU.add)
                v.drain()
                v.tensor_tensor(excl[:], incl[:], g.deg[:], ALU.subtract).then_inc(deg_done, 1)
                v.tensor_scalar(nkey[:], nid[:], -1.0, KEY - 1.0, ALU.mult, ALU.add)
                v.tensor_scalar(key[:], g.deg[:], float(CAP), float(KEY), ALU.min, ALU.mult)
                v.drain()
                v.tensor_tensor(key[:], key[:], nkey[:], ALU.add).then_inc(key_done, 1)
                v.wait_ge(pre_done, 1)
                v.tensor_copy(g.start[:], pre[:, 0:T])
                v.drain()
                v.tensor_copy(g.cur[:, 0:T], g.start[:])
                v.tensor_copy(g.left[:, 0:T], g.deg[:])
                v.drain()
                v.tensor_scalar(g.first[:], g.cur[:], float(E), None, ALU.min).then_inc(g.win_starts, 1)
                v.tensor_copy(tab[:, :, 0], g.start[:])
                v.tensor_copy(tab[:, :, 1], g.deg[:])
                v.tensor_copy(tab[:, :, 2], nid[:])
                v.wait_ge(key_in, 16)
                for t in range(T):
                    v.tensor_scalar(gt[:, t % 2, :], keys[:], key[:, t:t + 1], 0.0, ALU.is_gt, ALU.add,
                                    accum_out=rank[:, t:t + 1])
                    if t % 2:
                        v.drain()
                v.drain()
                v.tensor_copy(ranki[:], rank[:]).then_inc(ranked, 1)
                v.wait_ge(tab_in, 16)
                v.tensor_copy(g.sdeg[:], g.sorted[:, :, 1]).then_inc(sdeg_done, 1)
                v.wait_ge(max_t, 1)
                v.tensor_reduce(tmax[:], mt[0:T, 0:P], AX, ALU.max).then_inc(max_d, 1)
                v.wait_ge(max_r, 1)
                v.tensor_copy(allmax[:], mt2[0:1, 0:T])
                v.drain()
                v.tensor_reduce(one[:], allmax[:], AX, ALU.max)
                v.tensor_copy(maxi[:], allmax[:])
                v.drain()
                v.tensor_copy(onei[:], one[:])
                nb = g.nblk[:, 0:T]
                v.memset(g.nblk[:, T:T + 1], MINBLK)
                v.tensor_scalar(nb, maxi[:], float(S - 1), None, ALU.add)
                v.drain()
                v.tensor_scalar(nb, nb, 3, None, ALU.logical_shift_right)
                v.drain()
                v.tensor_scalar(nb, nb, float(MINBLK), None, ALU.max)
                v.tensor_scalar(onei[:], onei[:], float(W - 1), None, ALU.add)
                v.drain()
                v.tensor_reduce(one[:], nb, AX, ALU.add)
                v.tensor_scalar(g.nlast[:], nb, -float(S), float(S), ALU.mult, ALU.add)
                v.drain()
                v.tensor_tensor(g.nlast[:], g.nlast[:], maxi[:], ALU.add)
                v.drain()
                v.tensor_scalar(g.nlast[:], g.nlast[:], 0.0, None, ALU.max)
                v.tensor_scalar(g.npair[:], one[:], 1.0, None, ALU.add)
                v.drain()
                v.tensor_scalar(g.npair[:], g.npair[:], 1, None, ALU.logical_shift_right)
                v.drain()
                v.tensor_scalar(g.nempty[:], g.nlast[:], -1.0, float(S), ALU.mult, ALU.add)
                for h in range(2):
                    v.tensor_scalar(g.nsign[h][:], g.nlast[:], -float(h * HS), 0.0, ALU.add, ALU.max)
                v.drain()
                for h in range(2):
                    v.tensor_scalar(g.nsign[h][:], g.nsign[h][:], float(HS), 16.0, ALU.min, ALU.mult)
                v.tensor_scalar(g.nwin[:], nb, float(WB - 1), None, ALU.add)
                v.tensor_scalar(g.nwall[:], onei[:], 6, None, ALU.logical_shift_right)
                v.drain()
                v.tensor_scalar(g.nwin[:], g.nwin[:], 3, None, ALU.logical_shift_right)
                v.tensor_scalar(g.nwall[:], g.nwall[:], 1.0, None, ALU.max).then_inc(counts, 1)

            @block.tensor
            def _(pe):
                pe.wait_ge(coded, 1)
                nc.tensor.matmul(hist[:, 0:T], zh[:], oh_hi[:, 0, :, 0], start=True, stop=False,
                                 skip_group_check=True).then_inc(counted, 1)
                with pe.Fori(0, HSTEPS // 2) as i:
                    for b in range(2):
                        pe.wait_ge(coded, 2 * i + b + 1)
                        for j in range(HC):
                            mm = nc.tensor.matmul(hist[:, 0:T], oh_lo[:, b, :, j], oh_hi[:, b, :, j],
                                                  start=False, stop=False, skip_group_check=True)
                        mm.then_inc(counted, 1)
                nc.tensor.matmul(hist[:, 0:T], zh[:], oh_hi[:, 0, :, 0], start=False, stop=True,
                                 skip_group_check=True).then_inc(hist_done, 1)
                pe.wait_ge(deg_done, 1)
                nc.tensor.matmul(pre[:, 0:T], tri[:], g.deg[:], start=True, stop=False)
                nc.tensor.matmul(pre[:, 0:T], ones[:], excl[:], start=False, stop=True).then_inc(pre_done, 1)
                pe.wait_ge(sdeg_done, 1)
                nc.tensor.transpose(mt[0:T, 0:P], g.sdeg[:], g.ident[:]).then_inc(max_t, 1)
                pe.wait_ge(max_d, 1)
                nc.tensor.transpose(mt2[0:1, 0:T], tmax[:], g.ident[0:T, 0:T]).then_inc(max_r, 1)


def lists_programs(g, c, winf, mask):
    nc = g.nc
    first = g.sb("win_start", [P, T], I32, c)
    win = g.sb("win_ids", [P, T, W], I32, c)
    cur = g.sb("x_start", [P, 1], F32, c)
    rem = g.sb("x_left", [P, 1], F32, c)
    curi = g.sb("x_start_i", [P, 1], I32, c)
    xwin = g.sb("xwin", [P, W], I32, c)
    xmask = g.sb("xmask", [P, W], F32, c)
    starts = g.sem("list_starts")
    landed = g.sem("list_windows")
    masked = g.sem("list_masked")
    stored = g.sem("list_stored")
    x_idx = g.sem("overflow_start")
    x_landed = g.sem("overflow_window")
    x_masked = g.sem("overflow_masked")
    x_stored = g.sem("overflow_stored")
    src_rows = g.src_pad.rearrange("(a e) -> a e", a=1)

    def blocks_at(block0):
        return g.ids_dram[bass.ds(block0 * (P * S), W * P)].rearrange("(b p s) -> p b s", p=P, s=S)

    def begin(v):
        v.tensor_scalar(first[:], g.sorted[:, :, 0], float(E), None, ALU.min).then_inc(starts, 1)

    def end(v):
        v.tensor_tensor(mask, bc(g.slot[:], 1, T), bc(g.sdeg[:], 2, W), ALU.is_lt)
        v.wait_ge(landed, 16 * T)
        v.tensor_scalar(winf, win[:], float(-DUMMY), None, ALU.add)
        v.drain()
        v.tensor_tensor(winf, winf, mask, ALU.mult)
        v.drain()
        v.tensor_scalar(win[:], winf, float(DUMMY), None, ALU.add).then_inc(masked, 1)
        k = v.alloc_register("v_over")
        v.reg_mov(k, 0)
        with v.Fori(0, T) as t:
            n = v.value_load(g.nwin[0:1, bass.ds(t, 1)], min_val=1, max_val=BLOCKS)
            with v.If(n > 1):
                v.tensor_copy(cur[:], g.sorted[:, bass.ds(t, 1), 0])
                v.tensor_copy(rem[:], g.sdeg[:, bass.ds(t, 1)])
                v.drain()
                with v.Fori(1, n) as _w:
                    done = v.snap(k)
                    v.tensor_scalar(cur[:], cur[:], float(W), float(E), ALU.add, ALU.min)
                    v.tensor_scalar(rem[:], rem[:], float(-W), None, ALU.add)
                    v.drain()
                    v.tensor_copy(curi[:], cur[:]).then_inc(x_idx, 1)
                    v.tensor_scalar(xmask[:], g.slot[:], rem[:, 0:1], None, ALU.is_lt)
                    v.wait_ge(x_landed, (done + 1) * 16)
                    v.tensor_scalar(winf[:, 0, :], xwin[:], float(-DUMMY), None, ALU.add)
                    v.drain()
                    v.tensor_tensor(winf[:, 0, :], winf[:, 0, :], xmask[:], ALU.mult)
                    v.drain()
                    v.tensor_scalar(xwin[:], winf[:, 0, :], float(DUMMY), None, ALU.add).then_inc(x_masked, 1)
                    v.wait_ge(x_stored, (done + 1) * 16)
                    v.reg_add(k, k, 1)

    def gathers(pool):
        pool.wait_ge(starts, 1)
        for t in range(T):
            nc.gpsimd.indirect_dma_start(
                out=win[:, t, :], out_offset=None, in_=src_rows,
                in_offset=bass.IndirectOffsetOnAxis(ap=first[:, t:t + 1], axis=1)).then_inc(landed, 16)
        k = pool.alloc_register("p_over")
        pool.reg_mov(k, 0)
        with pool.Fori(0, T) as t:
            n = pool.value_load(g.nwin[0:1, bass.ds(t, 1)], min_val=1, max_val=BLOCKS)
            with pool.If(n > 1):
                with pool.Fori(1, n) as _w:
                    done = pool.snap(k)
                    hold(pool, x_idx, done + 1)
                    nc.gpsimd.indirect_dma_start(
                        out=xwin[:], out_offset=None, in_=src_rows,
                        in_offset=bass.IndirectOffsetOnAxis(ap=curi[:], axis=1)).then_inc(x_landed, 16)
                    hold(pool, x_landed, (done + 1) * 16)
                    pool.reg_add(k, k, 1)

    def stores(sp):
        k = sp.alloc_register("s_over")
        at = sp.alloc_register("s_block")
        sp.reg_mov(k, 0)
        sp.reg_mov(at, 0)
        sp.wait_ge(masked, 1)
        with sp.Fori(0, T) as t:
            n = sp.value_load(g.nwin[0:1, bass.ds(t, 1)], min_val=1, max_val=BLOCKS)
            base = sp.snap(at, min_val=0, max_val=BLOCKS - WB)
            sp.dma_start(blocks_at(base), win[:, bass.ds(t, 1), :].rearrange("p a (b s) -> p (a b) s", s=S)
                         ).then_inc(stored, 16)
            with sp.If(n > 1):
                with sp.Fori(1, n) as _w:
                    done = sp.snap(k)
                    sp.reg_add(at, at, WB)
                    here = sp.snap(at, min_val=WB, max_val=BLOCKS - WB)
                    hold(sp, x_masked, done + 1)
                    sp.dma_start(blocks_at(here), xwin[:].rearrange("p (b s) -> p b s", s=S)
                                 ).then_inc(x_stored, 16)
                    sp.reg_add(k, k, 1)
            sp.reg_add(at, at, WB)
        sp.wait_ge(stored, 16 * T)
        hold(sp, x_stored, sp.snap(k) * 16)

    return begin, end, gathers, stores


def stage_adjacency(g, A, c):
    nc = g.nc
    none = float(NOHI * P)
    with ExitStack() as c:
        cur, rem, first, win = g.cur, g.left, g.first, g.win
        winf = g.sb("a_winf", [P, TT, W], F32, c)
        hi = win[:].rearrange("p t w -> p (t w)")
        lo = g.sb("a_lo", [P, PAIRS * P], I32, c)[:]
        lo16 = g.sb("a_lo16", [P, PAIRS * P], F16, c)
        hi16 = g.sb("a_hi16", [P, PAIRS * P], F16, c)
        oh_lo = g.sb("a_oh_lo", [P, 2, P, GN], F16, c)
        oh_hi = g.sb("a_oh_hi", [P, 2, T, GN], F16, c)
        begin_lists, end_lists, gather_lists, store_lists = lists_programs(
            g, c, winf[:, 0:T, :], lo16[:, 0:T * W].rearrange("p (t w) -> p t w", w=W))
        turned = [g.ps(f"a_turned{b}", [P, 512], F32, c) for b in range(2)]
        cols = [[g.ps(f"a_cols{b}{h}", [P, 512], F32, c) for h in range(2)] for b in range(2)]
        starts, landed = g.win_starts, g.win_landed
        masked = g.sem("adj_masked")
        turn_done = g.sem("adj_turned")
        turn_read = g.sem("adj_turned_read")
        coded = g.sem("adj_coded")
        used = g.sem("adj_multiplied")
        moved = g.sem("adj_moved")
        filled = g.sem("adj_filled")
        SPLIT = 15
        src_rows = g.src_pad.rearrange("(a e) -> a e", a=1)

        def columns(b, h, u, gi):
            frm = cols[b][h][:, 0:GN * T].rearrange("q (p h) -> q h p", h=T)
            return A[:, :, bass.ds(u * (2 * P) + h * P + gi * GN, GN)], frm

        def steps(eng, w, do):
            with eng.Fori(0, PAIRS - 1) as u:
                for gi in range(GSTEPS):
                    do(w * STEPS + u * GSTEPS + gi, u, gi, 2)
            for gi in range(GSTEPS):
                do(w * STEPS + (PAIRS - 1) * GSTEPS + gi, PAIRS - 1, gi, 2 if TT == T else 1)

        def overflow(eng, body):
            n = eng.value_load(g.nwall[0:1, 0:1], min_val=1, max_val=E // W + 1)
            with eng.If(n > 1):
                with eng.Fori(1, n) as w:
                    body(w)

        with nc.Block() as block:

            @block.vector
            def _(v):
                def windows(w, first_pass):
                    if not first_pass:
                        v.tensor_scalar(cur[:], cur[:], float(W), float(E), ALU.add, ALU.min)
                        v.tensor_scalar(rem[:], rem[:], float(-W), None, ALU.add)
                        v.drain()
                        v.tensor_copy(first[:], cur[:]).then_inc(starts, 1)
                    v.wait_ge(turn_read, w * PAIRS)
                    v.wait_ge(landed, (w + 1) * (16 * T))
                    v.tensor_scalar(winf[:], win[:], -none, None, ALU.add)
                    v.drain()
                    v.tensor_tensor(win[:], bc(g.slot[:], 1, TT), bc(rem[:], 2, W), ALU.is_lt)
                    v.drain()
                    v.tensor_tensor(winf[:], winf[:], win[:], ALU.mult)
                    v.drain()
                    v.tensor_scalar(winf[:], winf[:], none, None, ALU.add).then_inc(masked, 1)
                    for u in range(PAIRS):
                        v.wait_ge(turn_done, w * PAIRS + u + 1)
                        v.tensor_copy(lo[:, u * P:(u + 1) * P], turned[u % 2][:, 0:P]).then_inc(turn_read, 1)
                    v.drain()
                    v.tensor_scalar(hi, lo, 7, None, ALU.logical_shift_right)
                    v.drain()
                    v.tensor_scalar(lo, lo, P - 1, None, ALU.bitwise_and)
                    v.tensor_copy(hi16[:], hi)
                    v.drain()
                    v.tensor_copy(lo16[:], lo)
                    v.drain()

                def code(k, u, gi, halves):
                    v.wait_ge(used, k)
                    at = bass.ds(u * P + gi * GN, GN)
                    one_hots(v, oh_lo[:, gi % 2], oh_hi[:, gi % 2], g.codes, lo16[:, at], hi16[:, at], GN).then_inc(coded, 1)

                def add(k, u, gi, halves):
                    code(k, u, gi, halves)
                    v.wait_ge(used, k + 2)
                    for h in range(halves):
                        to, frm = columns(gi % 2, h, u, gi)
                        last = v.tensor_tensor(to, to, frm, ALU.add)
                    last.then_inc(moved, 1)

                begin_lists(v)
                windows(0, True)
                steps(v, 0, code)
                v.wait_ge(moved, STEPS + 1)

                def more(w):
                    windows(w, False)
                    steps(v, w, add)

                overflow(v, more)
                v.drain()
                v.nop().then_inc(filled, 1)
                end_lists(v)
                for t in range(SPLIT):
                    v.tensor_scalar(A[:, t, :], A[:, t, :], 1.0, 0.0, ALU.mult, ALU.add, accum_out=g.dego[:, t:t + 1])
                v.drain()

            @block.sync
            def _(sp):
                store_lists(sp)

            @block.gpsimd
            def _(pool):
                def gather(w):
                    hold(pool, starts, w + 1)
                    hold(pool, landed, w * (16 * T))
                    for t in range(T):
                        nc.gpsimd.indirect_dma_start(
                            out=win[:, t, :], out_offset=None, in_=src_rows,
                            in_offset=bass.IndirectOffsetOnAxis(ap=first[:, t:t + 1], axis=1)).then_inc(landed, 16)

                overflow(pool, gather)
                gather_lists(pool)

            @block.scalar
            def _(act):
                act.preload_act_table_set("natural_log_exp_and_others")
                act.nop().then_inc(moved, 1)

                def move(k, u, gi, halves):
                    act.wait_ge(used, k + 2)
                    for h in range(halves):
                        to, frm = columns(gi % 2, h, u, gi)
                        last = nc.scalar.activation(to, frm, ACT.Copy)
                    last.then_inc(moved, 1)

                steps(act, 0, move)
                act.wait_ge(filled, 1)
                for t in range(SPLIT, T):
                    act.activation(A[:, t, :], A[:, t, :], ACT.Copy, accum_out=g.dego[:, t:t + 1])
                act.drain()

            @block.tensor
            def _(pe):
                def passes(w, first_pass):
                    pe.wait_ge(masked, w + 1)
                    for u in range(PAIRS):
                        if not first_pass or u >= 2:
                            pe.wait_ge(turn_read, w * PAIRS + u - 1)
                        tr = nc.tensor.transpose(turned[u % 2][:, 0:P],
                                                 winf[:, 2 * u:2 * u + 2, :].rearrange("p a b -> p (a b)"), g.ident[:])
                        tr.then_inc(turn_done, 1)
                    if first_pass:
                        pe.nop().then_inc(used, 1)

                    def multiply(k, u, gi, halves):
                        pe.wait_ge(coded, k + 1)
                        pe.wait_ge(moved, k)
                        b = gi % 2
                        for h in range(halves):
                            at = slice(h * W, (h + 1) * W)
                            for p in range(GN):
                                mm = nc.tensor.matmul(cols[b][h][:, p * T:(p + 1) * T], oh_lo[at, b, :, p],
                                                      oh_hi[at, b, :, p], start=True, stop=True)
                        mm.then_inc(used, 1)

                    steps(pe, w, multiply)

                passes(0, True)
                overflow(pe, lambda w: passes(w, False))



def layernorm(v, x, sq, m, var, out_var):
    v.tensor_reduce(m, x, AX, ALU.add)
    v.drain()
    v.tensor_scalar(m, m, -1.0 / D, None, ALU.mult)
    v.drain()
    v.tensor_tensor(x, x, bc(m, 2, D), ALU.add)
    v.drain()
    v.tensor_tensor(sq, x, x, ALU.mult)
    v.drain()
    v.tensor_reduce(var, sq, AX, ALU.add)
    v.drain()
    v.tensor_scalar(var, var, 1.0 / D, EPS, ALU.mult, ALU.add).then_inc(out_var, 1)


def root_inverse(act, x, inc):
    act.activation(x, x, ACT.Ln)
    act.drain()
    act.activation(x, x, ACT.Exp, scale=-0.5).then_inc(inc, 1)


class Spread:

    def __init__(self, g, name, c, A, x):
        self.g, self.A, self.x = g, A, x
        self.split = [g.sb(f"{name}_split{b}", [P, T, 2 * D], F16, c) for b in range(2)]
        self.copy = [g.sb(f"{name}_copy{b}", [P, CHUNK * P], F32, c) for b in range(2)]
        self.new = [g.sb(f"{name}_new{b}", [P, CHUNK, D], F32, c) for b in range(2)]
        self.rest = [g.sb(f"{name}_rest{b}", [P, CHUNK, D], F32, c) for b in range(2)]
        self.wide = [g.ps(f"{name}_wide{b}", [P, CHUNK * P], F32, c) for b in range(2)]
        self.turned = [g.ps(f"{name}_nodes{b}", [P, CHUNK * P], F32, c) for b in range(2)]
        self.product = g.sem(f"{name}_product")
        self.copied = g.sem(f"{name}_copied")
        self.nodes = g.sem(f"{name}_nodes_ready")
        self.made = g.sem(f"{name}_made")
        self.high = g.sem(f"{name}_high")
        self.low = g.sem(f"{name}_rest_ready")
        self.ready = g.sem(f"{name}_split_ready")

    def pe_turn(self, pe, r, c):
        t0, n = CHUNKS[c]
        k = r * NC + c
        pe.wait_ge(self.copied, k + 1)
        pe.wait_ge(self.made, NC + (k if c == 0 else k - 1))
        for j in range(n):
            mm = self.g.nc.tensor.matmul(self.turned[c % 2][:, j * D:(j + 1) * D],
                                         self.copy[c % 2][:, j * P:(j + 1) * P], self.g.comb[:],
                                         start=True, stop=True)
        mm.then_inc(self.nodes, 1)

    def pe_round(self, pe, r, b):
        for c, (t0, n) in enumerate(CHUNKS):
            k = r * NC + c
            pe.wait_ge(self.copied, k if c == 0 else k - 1)
            for s in range(T):
                if c == 0 and s % CHUNK == 0:
                    pe.wait_ge(self.ready, k + s // CHUNK + 1)
                if c > 0 and s == T // 2:
                    self.pe_turn(pe, r, c - 1)
                mm = self.g.nc.tensor.matmul(self.wide[c % 2][:, 0:n * P], self.split[b][:, s, :],
                                             self.A[:, s, t0 * P:(t0 + n) * P], start=(s == 0), stop=(s == T - 1))
            mm.then_inc(self.product, 1)
        self.pe_turn(pe, r, NC - 1)

    def act_split(self, act, j, c, b):
        t0, n = CHUNKS[c]
        act.wait_ge(self.made, j + 1)
        act.activation(self.split[b][:, t0:t0 + n, 0:D], self.new[c % 2][:, 0:n, :], ACT.Copy).then_inc(self.high, 1)
        act.wait_ge(self.low, j + 1)
        act.activation(self.split[b][:, t0:t0 + n, D:2 * D], self.rest[c % 2][:, 0:n, :], ACT.Copy,
                       scale=LOSCALE).then_inc(self.ready, 1)

    def act_round(self, act, r, b, last=False):
        for c, (t0, n) in enumerate(CHUNKS):
            k = r * NC + c
            act.wait_ge(self.product, k + 1)
            act.wait_ge(self.nodes, k if c == 0 else k - 1)
            act.activation(self.copy[c % 2][:, 0:n * P], self.wide[c % 2][:, 0:n * P], ACT.Copy).then_inc(self.copied, 1)
            if not last:
                self.act_split(act, NC + k, c, 1 - b)

    def v_split(self, v, j, c, b):
        t0, n = CHUNKS[c]
        v.wait_ge(self.high, j + 1)
        v.tensor_tensor(self.rest[c % 2][:, 0:n, :], self.new[c % 2][:, 0:n, :], self.split[b][:, t0:t0 + n, 0:D],
                        ALU.subtract).then_inc(self.low, 1)

    def v_round(self, v, r, b, make, last=False):
        for c, (t0, n) in enumerate(CHUNKS):
            k = r * NC + c
            v.wait_ge(self.nodes, k + 1)
            if not last:
                v.wait_ge(self.ready, NC + (k if c == 0 else k - 1))
            frm = self.turned[c % 2][:, 0:n * D].rearrange("p (t f) -> p t f", f=D)
            make(t0, n, frm, self.new[c % 2][:, 0:n, :])
            if not last:
                self.v_split(v, NC + k, c, 1 - b)


def stage_appnp(g, A, X, c):
    nc = g.nc
    with ExitStack() as c:
        sp_ = Spread(g, "appnp", c, A, X)
        H0 = g.sb("h0", [P, T, D], F32, c)
        wb = g.sb("w_b", [D + 1, D], F32, c)
        xt = [g.sb(f"x_turned{b}", [D + 1, CHUNK * P], F32, c) for b in range(2)]
        dl = g.sb("norm_in", [P, 2, T], F32, c)
        on = g.sb("norm_on", [P, 2, T], F32, c)
        c1 = g.sb("c_agg", [P, T], F32, c)
        cl = g.sb("c_agg_last", [P, T], F32, c)
        c2 = g.sb("c_h0", [P, T], F32, c)
        mean = g.sb("ln_mean", [P, T], F32, c)
        var = g.sb("ln_var", [P, T], F32, c)
        loaded = g.sem("appnp_loaded")
        padded = g.sem("appnp_padded")
        degs = g.sem("appnp_degrees")
        roots = g.sem("appnp_norms")
        x_turned = g.sem("appnp_x_turned")
        x_copied = g.sem("appnp_x_copied")
        h0_done = g.sem("appnp_h0")
        h0_read = g.sem("appnp_h0_read")
        full = (T - 1) * P

        with nc.Block() as block:

            @block.sync
            def _(sp):
                x = g.ins["x"]
                sp.dma_start(X[:, 0:T - 1, :], x[0:full].rearrange("(t p) f -> p t f", p=P)).then_inc(loaded, 16)
                sp.dma_start(wb[0:D, :], g.ins["L0_gnn_W"]).then_inc(loaded, 16)
                sp.dma_start(wb[D:D + 1, :], g.ins["L0_gnn_b"].rearrange("(a b) -> a b", a=1)).then_inc(loaded, 16)
                sp.wait_ge(padded, 1)
                sp.dma_start(X[0:TAIL, T - 1, :], x[full:N]).then_inc(loaded, 16)

            @block.gpsimd
            def _(pool):
                nc.gpsimd.memset(X[:, T - 1, :], 0.0).then_inc(padded, 1)

            @block.tensor
            def _(pe):
                pe.wait_ge(loaded, 64)
                pe.wait_ge(degs, 1)
                for ch, (t0, n) in enumerate(CHUNKS):
                    b = ch % 2
                    if ch >= 2:
                        pe.wait_ge(x_copied, ch - 1)
                    for j in range(n):
                        tr = nc.tensor.transpose(sp_.wide[b][0:D, j * P:(j + 1) * P], X[:, t0 + j, :], g.ident[:])
                    tr.then_inc(x_turned, 1)
                    pe.wait_ge(x_copied, ch + 1)
                    if ch >= 2:
                        pe.wait_ge(h0_read, ch - 1)
                    for j in range(n):
                        mm = nc.tensor.matmul(sp_.turned[b][:, j * D:(j + 1) * D], xt[b][:, j * P:(j + 1) * P], wb[:],
                                              start=True, stop=True)
                    mm.then_inc(h0_done, 1)
                with pe.Fori(0, ROUNDS // 2) as i:
                    sp_.pe_round(pe, i * 2, 0)
                    sp_.pe_round(pe, i * 2 + 1, 1)

            @block.scalar
            def _(act):
                act.preload_act_table_set("natural_log_exp_and_others")
                act.wait_ge(degs, 1)
                root_inverse(act, dl[:], roots)
                for ch, (t0, n) in enumerate(CHUNKS):
                    b = ch % 2
                    act.wait_ge(x_turned, ch + 1)
                    if ch >= 2:
                        act.wait_ge(h0_done, ch - 1)
                    act.activation(xt[b][0:D, 0:n * P], sp_.wide[b][0:D, 0:n * P], ACT.Copy).then_inc(x_copied, 1)
                for ch in range(NC):
                    sp_.act_split(act, ch, ch, 0)
                with act.Fori(0, ROUNDS // 2 - 1) as i:
                    sp_.act_round(act, i * 2, 0)
                    sp_.act_round(act, i * 2 + 1, 1)
                sp_.act_round(act, ROUNDS - 2, 0)
                sp_.act_round(act, ROUNDS - 1, 1, last=True)
                act.wait_ge(g.norm_var, 1)
                root_inverse(act, var[:], g.norm_root)

            @block.vector
            def _(v):
                v.memset(xt[0][D:D + 1, :], 1.0)
                v.memset(xt[1][D:D + 1, :], 1.0)
                v.tensor_scalar(dl[:, 0, :], g.dego[:], 1.0, None, ALU.max)
                v.tensor_scalar(dl[:, 1, :], g.deg[:], 1.0, None, ALU.max).then_inc(degs, 1)
                v.tensor_scalar(on[:, 0, :], g.dego[:], 0.0, None, ALU.is_gt)
                v.tensor_scalar(on[:, 1, :], g.deg[:], 0.0, None, ALU.is_gt)
                v.drain()
                v.wait_ge(roots, 1)
                v.tensor_tensor(dl[:], dl[:], on[:], ALU.mult)
                v.drain()
                ns, nd = dl[:, 0, :], dl[:, 1, :]
                v.tensor_scalar(cl[:], nd, 1.0 - ALPHA, None, ALU.mult)
                v.tensor_scalar(c2[:], ns, ALPHA, None, ALU.mult)
                v.drain()
                v.tensor_tensor(c1[:], cl[:], ns, ALU.mult)
                for ch, (t0, n) in enumerate(CHUNKS):
                    v.wait_ge(h0_done, ch + 1)
                    v.tensor_copy(H0[:, t0:t0 + n, :],
                                  sp_.turned[ch % 2][:, 0:n * D].rearrange("p (t f) -> p t f", f=D)).then_inc(h0_read, 1)
                v.drain()
                for ch, (t0, n) in enumerate(CHUNKS):
                    if ch >= 2:
                        v.wait_ge(sp_.ready, ch - 1)
                    v.tensor_tensor(sp_.new[ch % 2][:, 0:n, :], H0[:, t0:t0 + n, :], bc(ns[:, t0:t0 + n], 2, D),
                                    ALU.mult).then_inc(sp_.made, 1)
                    sp_.v_split(v, ch, ch, 0)

                def make(t0, n, frm, to):
                    rest = sp_.rest[(t0 // CHUNK) % 2][:, 0:n, :]
                    v.tensor_tensor(to, frm, bc(c1[:, t0:t0 + n], 2, D), ALU.mult)
                    v.tensor_tensor(rest, H0[:, t0:t0 + n, :], bc(c2[:, t0:t0 + n], 2, D), ALU.mult)
                    v.drain()
                    v.tensor_tensor(to, to, rest, ALU.add).then_inc(sp_.made, 1)

                def make_last(t0, n, frm, to):
                    x = X[:, t0:t0 + n, :]
                    v.tensor_tensor(to, frm, bc(cl[:, t0:t0 + n], 2, D), ALU.mult)
                    v.scalar_tensor_tensor(x, H0[:, t0:t0 + n, :], ALPHA, x, ALU.mult, ALU.add)
                    v.drain()
                    v.tensor_tensor(x, x, to, ALU.add).then_inc(sp_.made, 1)

                with v.Fori(0, ROUNDS // 2 - 1) as i:
                    sp_.v_round(v, i * 2, 0, make)
                    sp_.v_round(v, i * 2 + 1, 1, make)
                sp_.v_round(v, ROUNDS - 2, 0, make)
                v.wait_ge(sp_.ready, NC * ROUNDS)
                sp_.v_round(v, ROUNDS - 1, 1, make_last, last=True)
                v.drain()
                layernorm(v, X[:], H0[:], mean[:], var[:], g.norm_var)
                v.wait_ge(g.norm_root, 1)
                v.tensor_tensor(X[:], X[:], bc(var[:], 2, D), ALU.mult)


def stage_turn(g, A):
    nc = g.nc
    BANK = 8
    groups = [(s, t0, min(BANK, T - t0)) for s in range(T) for t0 in range(s + 1, T, BANK)]
    with ExitStack() as c:
        up = [g.ps(f"turn_up{b}", [P, BANK, P], F16, c) for b in range(2)]
        down = [g.ps(f"turn_down{b}", [P, BANK, P], F16, c) for b in range(2)]
        done = g.sem("turn_done")
        up_moved = g.sem("turn_up_moved")
        down_moved = g.sem("turn_down_moved")
        diagonal = [(t0, min(BANK, T - t0)) for t0 in range(0, T, BANK)]

        with nc.Block() as block:

            @block.tensor
            def _(pe):
                for k, (s, t0, n) in enumerate(groups):
                    if k >= 2:
                        pe.wait_ge(up_moved, k - 1)
                        pe.wait_ge(down_moved, k - 1)
                    for j in range(n):
                        t = t0 + j
                        nc.tensor.transpose(up[k % 2][:, j, :], A[:, s, t * P:(t + 1) * P], g.identh[:])
                        tr = nc.tensor.transpose(down[k % 2][:, j, :], A[:, t, s * P:(s + 1) * P], g.identh[:])
                    tr.then_inc(done, 1)
                for i, (t0, n) in enumerate(diagonal):
                    k = len(groups) + i
                    pe.wait_ge(up_moved, k - 1)
                    for j in range(n):
                        t = t0 + j
                        tr = nc.tensor.transpose(up[k % 2][:, j, :], A[:, t, t * P:(t + 1) * P], g.identh[:])
                    tr.then_inc(done, 1)

            @block.scalar
            def _(act):
                act.preload_act_table_set("natural_log_exp_and_others")
                for k, (s, t0, n) in enumerate(groups):
                    act.wait_ge(done, k + 1)
                    act.activation(A[:, t0:t0 + n, s * P:(s + 1) * P], up[k % 2][:, 0:n, :], ACT.Copy).then_inc(up_moved, 1)
                for i, (t0, n) in enumerate(diagonal):
                    k = len(groups) + i
                    act.wait_ge(done, k + 1)
                    for j in range(n):
                        t = t0 + j
                        last = act.activation(A[:, t, t * P:(t + 1) * P], up[k % 2][:, j, :], ACT.Copy)
                    last.then_inc(up_moved, 1)

            @block.vector
            def _(v):
                for k, (s, t0, n) in enumerate(groups):
                    v.wait_ge(done, k + 1)
                    v.tensor_copy(A[:, s, t0 * P:(t0 + n) * P].rearrange("p (t q) -> p t q", q=P),
                                  down[k % 2][:, 0:n, :]).then_inc(down_moved, 1)


def stage_lightgcn(g, A, X):
    nc = g.nc
    with ExitStack() as c:
        sp_ = Spread(g, "light", c, A, X)
        acc = g.sb("light_sum", [P, T, D], F32, c)
        dl = g.sb("light_norm", [P, T], F32, c)
        on = g.sb("light_on", [P, T], F32, c)
        mean = g.sb("light_mean", [P, T], F32, c)
        var = g.sb("light_var", [P, T], F32, c)
        degs = g.sem("light_degrees")
        roots = g.sem("light_norms")
        x_done = g.sem("light_x")
        x_out = g.sem("light_x_stored")

        with nc.Block() as block:

            @block.tensor
            def _(pe):
                with pe.Fori(0, (HOPS - 1) // 2) as i:
                    sp_.pe_round(pe, i * 2, 0)
                    sp_.pe_round(pe, i * 2 + 1, 1)
                sp_.pe_round(pe, HOPS - 1, 0)

            @block.scalar
            def _(act):
                act.preload_act_table_set("natural_log_exp_and_others")
                act.wait_ge(degs, 1)
                root_inverse(act, dl[:], roots)
                for ch in range(NC):
                    sp_.act_split(act, ch, ch, 0)
                with act.Fori(0, (HOPS - 1) // 2) as i:
                    sp_.act_round(act, i * 2, 0)
                    sp_.act_round(act, i * 2 + 1, 1)
                sp_.act_round(act, HOPS - 1, 0, last=True)
                act.wait_ge(g.norm_var, 2)
                root_inverse(act, var[:], g.norm_root)

            @block.vector
            def _(v):
                v.tensor_scalar(dl[:], g.dego[:], 1.0, None, ALU.max).then_inc(degs, 1)
                v.tensor_scalar(on[:], g.dego[:], 0.0, None, ALU.is_gt)
                v.tensor_copy(acc[:], X[:])
                v.drain()
                v.wait_ge(roots, 1)
                v.tensor_tensor(dl[:], dl[:], dl[:], ALU.mult)
                v.drain()
                v.tensor_tensor(dl[:], dl[:], on[:], ALU.mult)
                v.drain()
                for ch, (t0, n) in enumerate(CHUNKS):
                    if ch >= 2:
                        v.wait_ge(sp_.ready, ch - 1)
                    v.tensor_copy(sp_.new[ch % 2][:, 0:n, :], X[:, t0:t0 + n, :]).then_inc(sp_.made, 1)
                    sp_.v_split(v, ch, ch, 0)

                def make(t0, n, frm, to):
                    a = acc[:, t0:t0 + n, :]
                    v.tensor_tensor(to, frm, bc(dl[:, t0:t0 + n], 2, D), ALU.mult).then_inc(sp_.made, 1)
                    v.drain()
                    v.tensor_tensor(a, a, to, ALU.add)

                with v.Fori(0, (HOPS - 1) // 2) as i:
                    sp_.v_round(v, i * 2, 0, make)
                    sp_.v_round(v, i * 2 + 1, 1, make)
                v.wait_ge(sp_.ready, NC * HOPS)
                sp_.v_round(v, HOPS - 1, 0, make, last=True)
                v.drain()
                v.scalar_tensor_tensor(X[:], acc[:], 1.0 / (HOPS + 1), X[:], ALU.mult, ALU.add)
                v.drain()
                layernorm(v, X[:], acc[:], mean[:], var[:], g.norm_var)
                v.wait_ge(g.norm_root, 2)
                v.tensor_tensor(X[:], X[:], bc(var[:], 2, D), ALU.mult).then_inc(x_done, 1)

            @block.sync
            def _(sp):
                rows = g.x2_dram.rearrange("(t p) f -> p t f", p=P)
                with nc.allow_non_contiguous_dma(reason="one degree beside each row, once"):
                    sp.dma_start(rows[:, :, D:D + 1], g.dego[:].unsqueeze(2)).then_inc(x_out, 16)
                hold(sp, x_done, 1)
                sp.dma_start(rows[:, :, 0:D], X[:]).then_inc(x_out, 16)
                sp.wait_ge(x_out, 32)



class Lists:

    def __init__(self, g, name, c, table, width, empty):
        self.g, self.table, self.width, self.empty = g, table, width, empty
        self.body, self.last = Lists.Part(), Lists.Part()
        for kind, part in (("body", self.body), ("last", self.last)):
            part.ids = [g.sb(f"{name}_{kind}_ids{h}", [P, HS], I32, c) for h in range(2)]
            part.rows = g.sb(f"{name}_{kind}_rows", [P, S, width], F32, c)
            part.landed = [g.sem(f"{name}_{kind}_ids_landed{h}") for h in range(2)]
            part.half = [g.sem(f"{name}_{kind}_rows{h}") for h in range(2)]
            part.free = [g.sem(f"{name}_{kind}_free{h}") for h in range(2)]
        self.emptied = g.sem(f"{name}_emptied")

    class Part:
        pass

    class Place:

        def __init__(self, eng, name):
            self.body, self.tiles, self.half0, self.half1, self.empties = regs = [
                eng.alloc_register(f"{name}_{what}") for what in ("blocks", "tiles", "half0", "half1", "empties")]
            self.halves = (self.half0, self.half1)
            for r in regs:
                eng.reg_mov(r, 0)

    def count(self, eng, t):
        return eng.value_load(self.g.nblk[0:1, bass.ds(t, 1)], min_val=MINBLK, max_val=BLOCKS)

    def wait_body(self, eng, at, h):
        eng.wait_ge(self.body.half[h], eng.snap(at.body) * (16 * HS) + 16 * HS)

    def enter_last(self, eng, at, t):
        g = self.g
        for h in range(2):
            eng.reg_add(at.halves[h], at.halves[h],
                        eng.value_load(g.nsign[h][0:1, bass.ds(t, 1)], min_val=0, max_val=16 * HS))
        eng.reg_add(at.empties, at.empties, eng.value_load(g.nempty[0:1, bass.ds(t, 1)], min_val=0, max_val=S))
        eng.wait_ge(self.emptied, eng.snap(at.empties))

    def wait_last(self, eng, at, h):
        eng.wait_ge(self.last.half[h], eng.snap(at.halves[h]))

    def sp_walk(self, sp, at):
        g = self.g
        window = sp.alloc_register(f"window_{self.body.rows.name}")
        here = sp.alloc_register(f"here_{self.body.rows.name}")
        sp.reg_mov(window, 0)

        def ids():
            block = sp.snap(here, min_val=0, max_val=BLOCKS - 1)
            return g.ids_dram[bass.ds(block * (P * S), P * S)].rearrange("(p s) -> p s", s=S)

        with sp.Fori(0, T) as t:
            n = self.count(sp, t)
            wins = sp.value_load(g.nwin[0:1, bass.ds(t, 1)], min_val=1, max_val=BLOCKS)
            sp.reg_mov(here, window)
            with sp.Fori(1, n) as _j:
                frm = ids()
                for h in range(2):
                    hold(sp, self.body.half[h], sp.snap(at.body) * (16 * HS))
                    sp.dma_start(self.body.ids[h][:], frm[:, h * HS:(h + 1) * HS]).then_inc(self.body.landed[h], 16)
                sp.reg_add(at.body, at.body, 1)
                sp.reg_add(here, here, 1)
            frm = ids()
            for h in range(2):
                hold(sp, self.last.landed[h], sp.snap(at.tiles) * 16)
                hold(sp, self.last.half[h], sp.snap(at.halves[h]))
                sp.dma_start(self.last.ids[h][:], frm[:, h * HS:(h + 1) * HS]).then_inc(self.last.landed[h], 16)
                sp.reg_add(at.halves[h], at.halves[h],
                           sp.value_load(g.nsign[h][0:1, bass.ds(t, 1)], min_val=0, max_val=16 * HS))
            sp.reg_add(at.tiles, at.tiles, 1)
            sp.reg_add(window, window, wins * WB)
        sp.free_register(window)
        sp.free_register(here)

    def pool_walk(self, pool, at):
        g = self.g

        def gather(part, h, s):
            g.nc.gpsimd.indirect_dma_start(
                out=part.rows[:, h * HS + s, :], out_offset=None, in_=self.table,
                in_offset=bass.IndirectOffsetOnAxis(ap=part.ids[h][:, s:s + 1], axis=0)).then_inc(part.half[h], 16)

        with pool.Fori(0, T) as t:
            n = self.count(pool, t)
            used = pool.value_load(g.nlast[0:1, bass.ds(t, 1)], min_val=0, max_val=S)
            with pool.Fori(1, n) as _j:
                done = pool.snap(at.body)
                for h in range(2):
                    hold(pool, self.body.free[h], done)
                    hold(pool, self.body.landed[h], (done + 1) * 16)
                    for s in range(HS):
                        gather(self.body, h, s)
                pool.reg_add(at.body, at.body, 1)
            done = pool.snap(at.tiles)
            for h in range(2):
                hold(pool, self.last.free[h], done)
                hold(pool, self.last.landed[h], (done + 1) * 16)
                for s in range(HS):
                    with pool.If(used > h * HS + s):
                        gather(self.last, h, s)
                    with pool.Else():
                        g.nc.gpsimd.memset(self.last.rows[:, h * HS + s, :], self.empty).then_inc(self.emptied, 1)
            pool.reg_add(at.tiles, at.tiles, 1)


def stage_sage(g, XS, sdego):
    nc = g.nc
    I = g.ins
    with ExitStack() as c:
        H = g.sb("h", [P, T, D], F32, c)
        x2 = g.sb("x2_sorted", [P, T, D + 1], F32, c)
        lists = Lists(g, "sage", c, g.h_tab, D, -BIG)
        wl_n = g.sb("wl_rows", [D, LAYERS, 2 * D], F32, c)
        wr_n = g.sb("wr_rows", [D, LAYERS, D], F32, c)
        ad_n = g.sb("adapter_rows", [D, D], F32, c)
        w1_n = g.sb("w1_rows", [P, HID // P, D], F32, c)
        w2_n = g.sb("w2_rows", [D, HID], F32, c)
        WL = g.sb("wl", [2 * D, LAYERS, D], F32, c)
        WR = g.sb("wr", [D + 1, LAYERS, 2 * D], F32, c)
        adb = g.sb("adapter_b", [D + 1, D], F32, c)
        lng = g.sb("ln_g", [P, LAYERS, D], F32, c)
        wl = g.sb("wl_now", [2 * D, D], F32, c)
        wr = g.sb("wr_now", [D + 1, 2 * D], F32, c)
        gain = g.sb("gain_now", [P, D], F32, c)
        W1 = g.sb("w1", [D + 1, HID], F32, c)
        W2 = g.sb("w2", [P, HID // P, D], F32, c)
        b2 = g.sb("b2", [1, D], F32, c)
        ones = g.sb("sage_ones", [1, P], F32, c)
        g2 = g.sb("mlp_g", [P, HID // P], F32, c)
        be2 = g.sb("mlp_be", [P, HID // P], F32, c)
        W2g = g.sb("w2_with_gain", [P, HID // P, D], F32, c)
        b2g = g.sb("b2_with_beta", [1, D], F32, c)
        neg = g.sb("neg_big", [NP - N, D], F32, c)
        valid = g.sb("valid", [P, T], F32, c)
        rdeg = g.sb("rdeg", [P, T], F32, c)
        rem = g.sb("left", [P, 1], F32, c)
        mask = g.sb("row_mask", [P, S], F32, c)
        masked = g.sb("masked_rows", [P, S, D], F32, c)
        top = [g.sb(f"half_max{h}", [P, D], F32, c) for h in range(2)]
        sums = g.sb("block_sum", [P, D], F32, c)
        acc_max = g.sb("acc_max", [P, D], F32, c)
        acc_sum = g.sb("acc_sum", [P, D], F32, c)
        cat = g.sb("cat", [P, 3 * D], F32, c)
        catT = g.sb("cat_turned", [P, P], F32, c)
        hT = g.sb("h_turned", [D + 1, P], F32, c)
        stats = g.sb("bn_stats", [P, 6], F32, c)
        mv = g.sb("mean_var", [P, 2], F32, c)
        root = g.sb("root", [P, 1], F32, c)
        y = g.sb("y", [P, D], F32, c)
        z = g.sb("z", [P, D], F32, c)
        e = g.sb("e", [P, D], F32, c)
        hT2 = g.sb("mlp_h_turned", [D + 1, 2, 2 * P], F32, c)
        em = g.sb("mlp_e", [P, 2, 2 * HID], F32, c)
        zm = g.sb("mlp_z", [P, 2, 2 * HID], F32, c)
        zT = g.sb("mlp_z_turned", [P, 2 * HID], F32, c)
        mst = g.sb("mlp_bn_stats", [P, 2, 6], F32, c)
        mmv = g.sb("mlp_mean_var", [P, 2, 2, 2], F32, c)
        mean = g.sb("sage_mean", [P, T], F32, c)
        var = g.sb("sage_var", [P, T], F32, c)
        ps_t = g.ps("sage_turned", [P, 512], F32, c)
        ps_o = g.ps("sage_out", [P, 512], F32, c)
        ps_z = g.ps("mlp_z_turning", [P, 512], F32, c)
        ps_y = [g.ps(f"mlp_out{b}", [P, 512], F32, c) for b in range(2)]
        ps_w = [g.ps(f"sage_w{b}", [P, 512], F32, c) for b in range(2)]
        loaded = g.sem("sage_weights")
        neg_set = g.sem("sage_neg_set")
        neg_out = g.sem("sage_neg_out")
        x_in = g.sem("sage_x_gathered")
        w_turned = g.sem("sage_w_turned")
        w_moved = g.sem("sage_w_moved")
        prepared = g.sem("sage_prepared")
        scattered = g.sem("sage_scattered")
        cat_ready = g.sem("sage_cat")
        turned = g.sem("sage_cat_turned")
        copied = g.sem("sage_cat_copied")
        out_ready = g.sem("sage_conv")
        var_ready = g.sem("sage_var_ready")
        root_ready = g.sem("sage_root")
        z_ready = g.sem("sage_z")
        e_ready = g.sem("sage_e")
        h_ready = g.sem("sage_h")
        m_b = g.sem("mlp_bias")
        m_g = g.sem("mlp_gained")
        m_t = g.sem("mlp_h_turned")
        m_c = g.sem("mlp_h_copied")
        m_1 = g.sem("mlp_hidden")
        m_e = g.sem("mlp_exp")
        m_v = g.sem("mlp_var")
        m_r = g.sem("mlp_root")
        m_z = g.sem("mlp_normed")
        m_zt = g.sem("mlp_z_turned_ready")
        m_zc = g.sem("mlp_z_copied")
        m_o = g.sem("mlp_out")
        LOADS = 13
        PAIRS = [(t, min(2, T - t)) for t in range(0, T, 2)]
        STEPS = len(PAIRS)
        turns = [(wl_n[:, l, :], WL[:, l, :], D, 2 * D) for l in range(LAYERS)]
        turns += [(wr_n[:, l, :], WR[0:D, l, 0:D], D, D) for l in range(LAYERS)]
        turns += [(ad_n[:], WR[0:D, 0, D:2 * D], D, D)]
        turns += [(w1_n[:, i, :], W1[0:D, i * P:(i + 1) * P], P, D) for i in range(HID // P)]
        turns += [(w2_n[:, i * P:(i + 1) * P], W2[:, i, :], D, P) for i in range(HID // P)]

        with nc.Block() as block:

            @block.sync
            def _(sp):
                def load(to, frm):
                    sp.dma_start(to, frm).then_inc(loaded, 16)

                def row(ap):
                    return ap.rearrange("(a b) -> a b", a=1)

                load(wl_n[:], I["L2_gnn_conv_wl"].rearrange("l o i -> o l i"))
                load(wr_n[:], I["L2_gnn_conv_wr"].rearrange("l o i -> o l i"))
                load(ad_n[:], I["L2_gnn_adapter_w"])
                load(w1_n[:], I["L2_gnn_mlp_w1"].rearrange("(a p) i -> p a i", p=P))
                load(w2_n[:], I["L2_gnn_mlp_w2"])
                load(W1[D:D + 1, :], row(I["L2_gnn_mlp_b1"]))
                load(b2[:], row(I["L2_gnn_mlp_b2"]))
                with nc.allow_non_contiguous_dma(reason="two vectors to partitions, once"):
                    load(g2[:], I["L2_gnn_mlp_ln_g"].rearrange("(a p) -> p a", p=P))
                    load(be2[:], I["L2_gnn_mlp_ln_b"].rearrange("(a p) -> p a", p=P))
                load(adb[D:D + 1, :], row(I["L2_gnn_adapter_b"]))
                load(lng[:], I["L2_gnn_ln_g"].unsqueeze(0).broadcast_to([P, LAYERS, D]))
                load(WR[D:D + 1, :, 0:D], I["L2_gnn_conv_bl"].unsqueeze(0))
                load(WR[D:D + 1, :, D:2 * D], I["L2_gnn_ln_b"].unsqueeze(0))
                sp.wait_ge(neg_set, 1)
                sp.dma_start(g.h_tab[N:NP, :], neg[:]).then_inc(neg_out, 16)
                at = Lists.Place(sp, "sage_sp")
                with sp.Fori(0, LAYERS) as _l:
                    lists.sp_walk(sp, at)

            @block.gpsimd
            def _(pool):
                for t in range(T):
                    nc.gpsimd.indirect_dma_start(
                        out=x2[:, t, :], out_offset=None, in_=g.x2_dram,
                        in_offset=bass.IndirectOffsetOnAxis(ap=g.sorted[:, t, 2:3], axis=0)).then_inc(x_in, 16)
                at = Lists.Place(pool, "sage_pool")
                pool.wait_ge(neg_out, 16)
                with pool.Fori(0, LAYERS) as l:
                    pool.wait_ge(prepared, 1)
                    hold(pool, h_ready, l * T)
                    for h in range(2):
                        hold(pool, lists.body.free[h], pool.snap(at.body))
                        hold(pool, lists.last.free[h], l * T)
                    for t in range(T):
                        nc.gpsimd.indirect_dma_start(
                            out=g.h_tab, out_offset=bass.IndirectOffsetOnAxis(ap=g.sorted[:, t, 2:3], axis=0),
                            in_=H[:, t, :], in_offset=None, bounds_check=N - 1, oob_is_err=False
                        ).then_inc(scattered, 16)
                    hold(pool, scattered, (l + 1) * (16 * T))
                    lists.pool_walk(pool, at)

            @block.tensor
            def _(pe):
                pe.wait_ge(loaded, 16 * LOADS)
                for i, (frm, _to, rows, cols) in enumerate(turns):
                    if i >= 2:
                        pe.wait_ge(w_moved, i - 1)
                    nc.tensor.transpose(ps_w[i % 2][0:cols, 0:rows], frm, g.ident[0:rows, 0:rows]).then_inc(w_turned, 1)
                with pe.Fori(0, LAYERS) as l:
                    with pe.Fori(0, T) as t:
                        q = pe.snap(l * T + t)
                        pe.wait_ge(cat_ready, q + 1)
                        nc.tensor.transpose(ps_t[:, 0:P], cat[:, 0:2 * D], g.ident[:])
                        nc.tensor.transpose(ps_t[0:D, P:2 * P], cat[:, 2 * D:3 * D], g.ident[:]).then_inc(turned, 1)
                        pe.wait_ge(copied, q + 1)
                        pe.wait_ge(z_ready, q)
                        nc.tensor.matmul(ps_o[:, 0:2 * D], hT[:], wr[:], start=True, stop=False, skip_group_check=True)
                        nc.tensor.matmul(ps_o[:, 0:D], catT[:], wl[:], start=False, stop=True,
                                         skip_group_check=True).then_inc(out_ready, 1)
                for i in range(HID // P):
                    nc.tensor.matmul(ps_z[0:1, 0:D], be2[:, i:i + 1], W2[:, i, :], start=(i == 0), stop=False)
                nc.tensor.matmul(ps_z[0:1, 0:D], ones[0:1, 0:1], b2[:], start=False, stop=True).then_inc(m_b, 1)

                def hidden(i):
                    t0, n = PAIRS[i]
                    b = i % 2
                    for j in range(n):
                        tr = nc.tensor.transpose(ps_t[0:D, (2 * b + j) * P:(2 * b + j + 1) * P], H[:, t0 + j, :], g.ident[:])
                    tr.then_inc(m_t, 1)
                    pe.wait_ge(m_c, i + 1)
                    if i >= 2:
                        pe.wait_ge(m_v, i - 1)
                    for j in range(n):
                        mm = nc.tensor.matmul(ps_w[b][:, j * HID:(j + 1) * HID], hT2[:, b, j * P:(j + 1) * P], W1[:],
                                              start=True, stop=True)
                    mm.then_inc(m_1, 1)

                def output(i):
                    n = PAIRS[i][1]
                    b = i % 2
                    pe.wait_ge(m_z, i + 1)
                    for j in range(n * HID // P):
                        tr = nc.tensor.transpose(ps_z[:, j * P:(j + 1) * P], zm[:, b, j * P:(j + 1) * P], g.ident[:])
                    tr.then_inc(m_zt, 1)
                    pe.wait_ge(m_zc, i + 1)
                    for j in range(n):
                        to = ps_y[b][:, j * D:(j + 1) * D]
                        for a in range(HID // P):
                            at = j * HID + a * P
                            nc.tensor.matmul(to, zT[:, at:at + P], W2g[:, a, :], start=(a == 0), stop=False)
                        mm = nc.tensor.matmul(to, ones[:], b2g[:], start=False, stop=True)
                    mm.then_inc(m_o, 1)

                pe.wait_ge(h_ready, LAYERS * T)
                pe.wait_ge(m_g, 2)
                hidden(0)
                for i in range(STEPS + 1):
                    if i + 1 < STEPS:
                        hidden(i + 1)
                    if i:
                        output(i - 1)

            @block.scalar
            def _(act):
                act.preload_act_table_set("natural_log_exp_and_others")
                for i, (_frm, to, rows, cols) in enumerate(turns):
                    act.wait_ge(w_turned, i + 1)
                    act.activation(to, ps_w[i % 2][0:cols, 0:rows], ACT.Copy).then_inc(w_moved, 1)

                def conv(q):
                    act.wait_ge(turned, q + 1)
                    act.activation(catT[:], ps_t[:, 0:P], ACT.Copy)
                    act.activation(hT[0:D, :], ps_t[0:D, P:2 * P], ACT.Copy).then_inc(copied, 1)

                def post(q):
                    act.wait_ge(var_ready, q + 1)
                    act.activation(root[:], mv[:, 1:2], ACT.Ln)
                    act.drain()
                    act.activation(root[:], root[:], ACT.Exp, scale=-0.5).then_inc(root_ready, 1)
                    act.wait_ge(z_ready, q + 1)
                    act.activation(e[:], z[:], ACT.Exp, scale=-1.0).then_inc(e_ready, 1)

                with act.Fori(0, LAYERS) as l:
                    with act.Fori(0, T) as t:
                        q = act.snap(l * T + t)
                        conv(q)
                        post(q)
                act.wait_ge(m_b, 1)
                act.activation(b2g[:], ps_z[0:1, 0:D], ACT.Copy).then_inc(m_g, 1)

                def mlp_silu(i):
                    w = PAIRS[i][1]
                    b = i % 2
                    act.wait_ge(m_t, i + 1)
                    act.activation(hT2[0:D, b, 0:w * P], ps_t[0:D, 2 * b * P:(2 * b + w) * P], ACT.Copy).then_inc(m_c, 1)
                    act.wait_ge(m_1, i + 1)
                    act.activation(em[:, b, 0:w * HID], ps_w[b][:, 0:w * HID], ACT.Exp, scale=-1.0).then_inc(m_e, 1)

                mlp_silu(0)
                for i in range(STEPS + 1):
                    if i + 1 < STEPS:
                        mlp_silu(i + 1)
                    if i < STEPS:
                        act.wait_ge(m_v, i + 1)
                        root_inverse(act, mmv[:, i % 2, 0:PAIRS[i][1], 1], m_r)
                    if i:
                        w = PAIRS[i - 1][1]
                        act.wait_ge(m_zt, i)
                        act.activation(zT[:, 0:w * HID], ps_z[:, 0:w * HID], ACT.Copy).then_inc(m_zc, 1)
                act.wait_ge(g.norm_var, 3)
                root_inverse(act, var[:], g.norm_root)

            @block.vector
            def _(v):
                v.memset(neg[:], -BIG).then_inc(neg_set, 1)
                v.memset(ones[:], 1.0)
                v.memset(hT[D:D + 1, :], 1.0)
                v.memset(hT2[D:D + 1, :, :], 1.0)
                v.tensor_scalar(valid[:], g.sdeg[:], 0.0, None, ALU.is_gt)
                v.tensor_scalar(rdeg[:], g.sdeg[:], 1.0, None, ALU.max)
                v.drain()
                v.reciprocal(rdeg[:], rdeg[:])
                v.wait_ge(loaded, 16 * LOADS)
                for l in range(1, LAYERS):
                    v.tensor_copy(WR[0:D, l, D:2 * D], g.ident[0:D, 0:D])
                v.tensor_tensor(WR[D:D + 1, 0, D:2 * D], WR[D:D + 1, 0, D:2 * D], adb[D:D + 1, :], ALU.add)
                v.wait_ge(w_moved, len(turns))
                for i in range(HID // P):
                    gained = v.tensor_scalar(W2g[:, i, :], W2[:, i, :], g2[:, i:i + 1], None, ALU.mult)
                gained.then_inc(m_g, 1)
                v.wait_ge(x_in, 16 * T)
                v.tensor_copy(XS[:], x2[:, :, 0:D])
                v.tensor_copy(sdego[:], x2[:, :, D])
                v.tensor_copy(H[:], x2[:, :, 0:D]).then_inc(prepared, 1)
                at = Lists.Place(v, "sage_v")

                def take(part, h):
                    if part is lists.body:
                        lists.wait_body(v, at, h)
                    else:
                        lists.wait_last(v, at, h)
                    rows = part.rows[:, h * HS:(h + 1) * HS, :]
                    v.tensor_reduce(top[h][:], rows.rearrange("p s f -> p f s"), AX, ALU.max)
                    v.tensor_tensor(masked[:, h * HS:(h + 1) * HS, :], rows, bc(mask[:, h * HS:(h + 1) * HS], 2, D),
                                    ALU.mult).then_inc(part.free[h], 1)

                def post_stats(q):
                    v.wait_ge(out_ready, q)
                    v.bn_stats(stats[:], ps_o[:, 0:D])
                    v.drain()
                    v.bn_aggr(mv[:], stats[:])
                    v.drain()
                    v.tensor_scalar(mv[:, 1:2], mv[:, 1:2], EPS, None, ALU.add).then_inc(var_ready, 1)

                def post_norm(q):
                    v.wait_ge(root_ready, q)
                    v.tensor_scalar(y[:], ps_o[:, 0:D], mv[:, 0:1], root[:, 0:1], ALU.subtract, ALU.mult)
                    v.drain()
                    v.tensor_tensor(y[:], y[:], gain[:], ALU.mult)
                    v.drain()
                    v.tensor_tensor(z[:], y[:], ps_o[:, D:2 * D], ALU.add).then_inc(z_ready, 1)

                def post_silu(q, t):
                    v.wait_ge(e_ready, q)
                    v.tensor_scalar(e[:], e[:], 1.0, None, ALU.add)
                    v.drain()
                    v.reciprocal(e[:], e[:])
                    v.drain()
                    v.tensor_tensor(H[:, bass.ds(t, 1), :].rearrange("p a f -> p (a f)"), z[:], e[:],
                                    ALU.mult).then_inc(h_ready, 1)

                def more(part):
                    v.tensor_scalar(rem[:], rem[:], float(-S), None, ALU.add)
                    v.drain()
                    v.tensor_scalar(mask[:], g.slot[:, 0:S], rem[:, 0:1], None, ALU.is_lt)
                    v.drain()
                    take(part, 0)
                    take(part, 1)
                    v.drain()
                    v.tensor_reduce(sums[:], masked[:].rearrange("p s f -> p f s"), AX, ALU.add)
                    v.tensor_tensor(acc_max[:], acc_max[:], top[0][:], ALU.max)
                    v.drain()
                    v.tensor_tensor(acc_max[:], acc_max[:], top[1][:], ALU.max)
                    v.tensor_tensor(acc_sum[:], acc_sum[:], sums[:], ALU.add)

                def tile_walk(l, t, first):
                    q = v.snap(l * T + t)
                    n = lists.count(v, t)
                    v.tensor_copy(rem[:], g.sdeg[:, bass.ds(t, 1)])
                    v.drain()
                    v.tensor_scalar(mask[:], g.slot[:, 0:S], rem[:, 0:1], None, ALU.is_lt)
                    v.drain()
                    take(lists.body, 0)
                    if not first:
                        post_stats(q)
                    take(lists.body, 1)
                    if not first:
                        post_norm(q)
                    v.drain()
                    v.tensor_tensor(acc_max[:], top[0][:], top[1][:], ALU.max)
                    v.tensor_reduce(acc_sum[:], masked[:].rearrange("p s f -> p f s"), AX, ALU.add)
                    v.reg_add(at.body, at.body, 1)
                    with v.Fori(2, n) as _j:
                        more(lists.body)
                        v.reg_add(at.body, at.body, 1)
                    lists.enter_last(v, at, t)
                    more(lists.last)
                    if not first:
                        post_silu(q, t - 1)
                    v.drain()
                    v.wait_ge(turned, q)
                    v.tensor_scalar(cat[:, 0:D], acc_max[:], valid[:, bass.ds(t, 1)], None, ALU.mult)
                    v.tensor_scalar(cat[:, D:2 * D], acc_sum[:], rdeg[:, bass.ds(t, 1)], None, ALU.mult)
                    v.tensor_copy(cat[:, 2 * D:3 * D], H[:, bass.ds(t, 1), :].rearrange("p a f -> p (a f)")
                                  ).then_inc(cat_ready, 1)

                with v.Fori(0, LAYERS) as l:
                    v.drain()
                    now = bass.ds(l, 1)
                    v.tensor_copy(wl[:], WL[:, now, :].rearrange("p a f -> p (a f)"))
                    v.tensor_copy(wr[:], WR[:, now, :].rearrange("p a f -> p (a f)"))
                    v.tensor_copy(gain[:], lng[:, now, :].rearrange("p a f -> p (a f)"))
                    tile_walk(l, 0, True)
                    with v.Fori(1, T) as t:
                        tile_walk(l, t, False)
                    q = v.snap((l + 1) * T)
                    post_stats(q)
                    post_norm(q)
                    post_silu(q, T - 1)

                def mlp_hidden(i):
                    w = PAIRS[i][1]
                    b = i % 2
                    e_now, z_now = em[:, b, 0:w * HID], zm[:, b, 0:w * HID]
                    v.wait_ge(m_e, i + 1)
                    v.tensor_scalar(e_now, e_now, 1.0, None, ALU.add)
                    v.drain()
                    v.reciprocal(e_now, e_now)
                    v.drain()
                    if i >= 2:
                        v.wait_ge(m_zt, i - 1)
                    v.tensor_tensor(z_now, e_now, ps_w[b][:, 0:w * HID], ALU.mult)
                    v.drain()
                    for j in range(w):
                        v.bn_stats(mst[:, j, :], zm[:, b, j * HID:(j + 1) * HID])
                    v.drain()
                    for j in range(w):
                        v.bn_aggr(mmv[:, b, j, :], mst[:, j, :])
                    v.drain()
                    at = mmv[:, b, 0:w, 1]
                    v.tensor_scalar(at, at, EPS, None, ALU.add).then_inc(m_v, 1)

                def mlp_norm(i):
                    w = PAIRS[i][1]
                    b = i % 2
                    v.wait_ge(m_r, i + 1)
                    for j in range(w):
                        z_now = zm[:, b, j * HID:(j + 1) * HID]
                        ts = v.tensor_scalar(z_now, z_now, mmv[:, b, j, 0:1], mmv[:, b, j, 1:2], ALU.subtract, ALU.mult)
                    ts.then_inc(m_z, 1)

                def mlp_out(i):
                    t0, w = PAIRS[i]
                    b = i % 2
                    v.wait_ge(m_o, i + 1)
                    x = XS[:, t0:t0 + w, :]
                    v.tensor_tensor(x, x, ps_y[b][:, 0:w * D].rearrange("p (t f) -> p t f", f=D), ALU.add)

                for i in range(STEPS + 2):
                    if i < STEPS:
                        mlp_hidden(i)
                    if 1 <= i <= STEPS:
                        mlp_norm(i - 1)
                    if i >= 2:
                        mlp_out(i - 2)
                v.drain()
                layernorm(v, XS[:], H[:], mean[:], var[:], g.norm_var)
                v.wait_ge(g.norm_root, 3)
                v.tensor_tensor(XS[:], XS[:], bc(var[:], 2, D), ALU.mult)



def counter(eng, name):
    k = eng.alloc_register(f"{name}_all_blocks")
    eng.reg_mov(k, 0)
    return k


def stage_sheaf(g, XS, sdego):
    nc = g.nc
    I = g.ins
    S2 = 2 * S
    M = 2 * S2
    STEPS0 = -(-T // S2)
    GROUPS = 2 * STEPS0
    LAG = 6
    XBUF = 8
    OT = GROUPS * S
    ORDER = (0, 1, 3, 2)
    PORDER = (0, 1, 3, 5, 2, 4)
    E4 = S * DD
    with ExitStack() as c:
        lists = Lists(g, "sheaf", c, g.t_tab, TW, 0.0)
        own = g.sb("own_rows", [P, OT, TW], F32, c)
        own8 = g.sb("own_repeated", [P, 2, S, HH], F32, c)
        agg = g.sb("agg", [P, OT, D], F32, c)
        w1n = g.sb("sheaf_w1_rows", [D, DD], F32, c)
        w1r = g.sb("sheaf_w1", [D, DD], F32, c)
        w2r = g.sb("sheaf_w2", [D, HH], F32, c)
        K = g.sb("sheaf_k", [D, D], F32, c)
        m1n = g.sb("mlp1_rows", [HH, 2, DD, HH], F32, c)
        m1 = g.sb("mlp1_ordered", [HH, 2, DD, HH], F32, c)
        PQ = g.sb("pq", [D + 1, 2 * HH], F32, c)
        m2n = g.sb("mlp2_columns", [P, NPAR], F32, c)
        same = g.sb("same_edge", [P, S], F32, c)
        BD = g.sb("mlp2_blocks", [P, S, NPAR], F32, c)
        mb2n = g.sb("mlp2_b_row", [1, NPAR], F32, c)
        mb2 = g.sb("mlp2_b", [1, S2, NPAR], F32, c)
        one = g.sb("sheaf_ones", [1, P], F32, c)
        eps = g.sb("epsilons", [P, DD], F32, c)
        coef = g.sb("coefficients", [P, DD], F32, c)
        xt = [g.sb(f"x3_turned{b}", [D, CHUNK * P], F32, c) for b in range(2)]
        xft = [g.sb(f"xf_turned{b}", [D + 1, CHUNK * P], F32, c) for b in range(2)]
        zrow = g.sb("zero_rows", [NP - N, TW], F32, c)
        zh = g.sb("zero_half", [P, 512], F16, c)
        pq = g.sb("block_pq", [P, 2, S, HH], F32, c)
        xj = g.sb("block_x", [P, XBUF, S, D], F32, c)
        hT = g.sb("hidden_turned", [P, 2 * P], F32, c)
        Z = g.sb("columns", [P, 4, 2, S, 2, 2, DD], F32, c)
        by5 = g.sb("products5", [P, M, 2], F32, c)
        by0 = g.sb("products0", [P, M, 2], F32, c)
        pr = g.sb("column_products", [P, M * 2, 2, DD], F32, c)
        inv = g.sb("inverse_norm", [P, M * 2], F32, c)
        cc = g.sb("projection", [P, M * 2], F32, c)
        Wv = g.sb("projected", [P, 4, M, DD], F32, c)
        nn = g.sb("norms", [P, 4, M, 2], F32, c)
        U = g.sb("orthonormal", [P, M * 2, 2, DD], F32, c)
        mm4 = g.sb("map_products", [P, DD, S2, DD, DD], F32, c)
        maps = g.sb("maps", [P, DD, S2, DD], F32, c)
        pm = g.sb("message_products", [P, 4, E4 * D], F32, c)
        sums = g.sb("tile_sums", [P, T, 512], F32, c)
        dis = g.sb("dis", [P, T], F32, c)
        mean = g.sb("sheaf_mean", [P, T], F32, c)
        var = g.sb("sheaf_var", [P, T], F32, c)
        el = g.sb("elu", [P, T, D], F32, c)
        ps_a = [g.ps(f"sheaf_a{b}", [P, 512], F32, c) for b in range(2)]
        ps_b = [g.ps(f"sheaf_b{b}", [P, 512], F32, c) for b in range(2)]
        ps_h = g.ps("sheaf_hidden", [P, 512], F32, c)
        ps_p = g.ps("sheaf_params", [P, 512], F32, c)
        ps_m = g.ps("sheaf_messages", [P, 512], F32, c)
        loaded = g.sem("sheaf_weights")
        z_set = g.sem("sheaf_zero_set")
        z_out = g.sem("sheaf_zero_out")
        same_set = g.sem("sheaf_same_set")
        ordered = g.sem("sheaf_weights_ordered")
        deg_ready = g.sem("sheaf_degrees")
        dis_ready = g.sem("sheaf_dis")
        w_turned = g.sem("sheaf_w_turned")
        w_moved = g.sem("sheaf_w_moved")
        x_turned = g.sem("sheaf_x_turned")
        x_copied = g.sem("sheaf_x_copied")
        f_done = g.sem("sheaf_xf_turned")
        f_copied = g.sem("sheaf_xf_copied")
        rows_done = g.sem("sheaf_rows")
        rows_read = g.sem("sheaf_rows_read")
        table_ready = g.sem("sheaf_own_ready")
        scattered = g.sem("sheaf_table_out")
        copied = g.sem("sheaf_rows_copied")
        hid_ready = g.sem("sheaf_hidden_ready")
        relu_ready = g.sem("sheaf_relu_ready")
        par_ready = g.sem("sheaf_params_ready")
        col_ready = g.sem("sheaf_columns_ready")
        col_read = g.sem("sheaf_columns_read")
        nn_ready = g.sem("sheaf_norms")
        rs_ready = g.sem("sheaf_roots")
        edges_done = g.sem("sheaf_edges_done")
        msg_done = g.sem("sheaf_messages_added")
        tile_sum = g.sem("sheaf_tile_sum")
        tile_read = g.sem("sheaf_tile_read")
        e_in = g.sem("sheaf_exp_in")
        e_out = g.sem("sheaf_exp_out")
        final = g.sem("final_ready")
        stored = g.sem("final_stored")
        LOADS = 2 * DD + S + 5
        par = ps_p[:, 0:S2 * NPAR].rearrange("p (u s n) -> p u s n", s=S, n=NPAR)

        class MessageTile:

            def __init__(self, eng, name):
                self.eng = eng
                self.tile, self.left = (eng.alloc_register(f"{name}_{what}") for what in ("message_tile", "message_left"))
                eng.reg_mov(self.tile, 0)
                eng.reg_mov(self.left, eng.value_load(g.nblk[0:1, 0:1], min_val=MINBLK, max_val=BLOCKS))

            def step(self, close):
                eng = self.eng
                eng.reg_add(self.left, self.left, -1)
                with eng.If(eng.snap(self.left) < 1):
                    close(eng.snap(self.tile, min_val=0, max_val=T - 1))
                    eng.reg_add(self.tile, self.tile, 1)
                    eng.reg_mov(self.left, eng.value_load(
                        g.nblk[0:1, bass.ds(eng.snap(self.tile, min_val=0, max_val=T), 1)], min_val=MINBLK, max_val=BLOCKS))
                eng.sem_inc(HELD[0], 1)

        with nc.Block() as block:

            @block.sync
            def _(sp):
                def load(to, frm):
                    sp.dma_start(to, frm).then_inc(loaded, 16)

                def row(ap):
                    return ap.rearrange("(a b) -> a b", a=1)

                for d in range(DD):
                    load(w1n[d * HH:(d + 1) * HH, :], I["L3_gnn_W1"][d:d + 1, :].broadcast_to([HH, DD]))
                    load(w2r[d * HH:(d + 1) * HH, :], I["L3_gnn_W2"])
                load(m1n[:].rearrange("o a d h -> o (a d h)"), I["L3_gnn_mlp1_w"])
                load(PQ[D:D + 1, 0:HH], row(I["L3_gnn_mlp1_b"]))
                with nc.allow_non_contiguous_dma(reason="96 numbers, once for each slot"):
                    for s in range(S):
                        load(m2n[s * HH:(s + 1) * HH, :], I["L3_gnn_mlp2_w"].rearrange("n h -> h n"))
                load(mb2n[:], row(I["L3_gnn_mlp2_b"]))
                load(eps[:], row(I["L3_gnn_epsilons"]).broadcast_to([P, DD]))
                sp.wait_ge(z_set, 1)
                load(PQ[D:D + 1, HH:2 * HH], zrow[0:1, 0:HH])
                sp.dma_start(g.t_tab[N:NP, :], zrow[:]).then_inc(z_out, 16)
                lists.sp_walk(sp, Lists.Place(sp, "sheaf_sp"))

            @block.gpsimd
            def _(pool):
                nc.gpsimd.memset(same[:], 1.0)
                pool.drain()
                nc.gpsimd.affine_select(out=same[:], in_=same[:], compare_op=ALU.is_ge, fill=0.0, base=0,
                                        pattern=[[-HH, S]], channel_multiplier=1)
                pool.drain()
                nc.gpsimd.affine_select(out=same[:], in_=same[:], compare_op=ALU.is_ge, fill=0.0, base=HH - 1,
                                        pattern=[[HH, S]], channel_multiplier=-1).then_inc(same_set, 1)
                pool.wait_ge(z_out, 16)
                pool.wait_ge(table_ready, 1)
                for t in range(T):
                    nc.gpsimd.indirect_dma_start(
                        out=g.t_tab, out_offset=bass.IndirectOffsetOnAxis(ap=g.sorted[:, t, 2:3], axis=0),
                        in_=own[:, t, :], in_offset=None, bounds_check=N - 1, oob_is_err=False
                    ).then_inc(scattered, 16)
                pool.wait_ge(scattered, 16 * T)
                lists.pool_walk(pool, Lists.Place(pool, "sheaf_pool"))
                pool.wait_ge(final, 1)
                for t in range(T):
                    nc.gpsimd.indirect_dma_start(
                        out=g.out, out_offset=bass.IndirectOffsetOnAxis(ap=g.sorted[:, t, 2:3], axis=0),
                        in_=XS[:, t, :], in_offset=None, bounds_check=N - 1, oob_is_err=False
                    ).then_inc(stored, 16)
                pool.wait_ge(stored, 16 * T)

            @block.tensor
            def _(pe):
                pe.wait_ge(loaded, 16 * LOADS)
                pe.wait_ge(ordered, 1)
                for i in range(2):
                    nc.tensor.transpose(ps_a[i][0:D, 0:HH], m1[:, i].rearrange("o d h -> o (d h)"),
                                        g.ident[0:HH, 0:HH]).then_inc(w_turned, 1)
                pe.wait_ge(w_moved, 2)
                for ch, (t0, n) in enumerate(CHUNKS):
                    b = ch % 2
                    for j in range(n):
                        tr = nc.tensor.transpose(ps_a[b][0:D, j * P:(j + 1) * P], XS[:, t0 + j, :], g.ident[:])
                    tr.then_inc(x_turned, 1)
                    pe.wait_ge(x_copied, ch + 1)
                    nc.tensor.matmul(ps_a[b][0:D, 0:n * P], K[:], xt[b][:, 0:n * P], start=True, stop=True).then_inc(f_done, 1)
                    pe.wait_ge(f_copied, ch + 1)
                    if ch >= 2:
                        pe.wait_ge(rows_read, ch - 1)
                    for j in range(n):
                        at = slice(j * P, (j + 1) * P)
                        nc.tensor.matmul(ps_b[b][:, j * P:j * P + D], xt[b][:, at], K[:], start=True, stop=True)
                        mm = nc.tensor.matmul(ps_b[b][:, j * P + D:j * P + D + 2 * HH], xft[b][:, at], PQ[:],
                                              start=True, stop=True)
                    mm.then_inc(rows_done, 1)

                def params(i, ve, ue):
                    for h, two in enumerate((ve, ue)):
                        for a, x in enumerate(two):
                            mm = nc.tensor.matmul(ps_h[:, h * P:(h + 1) * P], x, g.ident[:], start=(a == 0), stop=(a == 1))
                    mm.then_inc(hid_ready, 1)
                    pe.wait_ge(relu_ready, i + 1)
                    pe.wait_ge(col_ready, i)
                    nc.tensor.matmul(ps_p[:, 0:S2 * NPAR], one[:], mb2[:].rearrange("p m n -> p (m n)"), start=True,
                                     stop=False, skip_group_check=True)
                    for h in range(2):
                        mm = nc.tensor.matmul(ps_p[:, h * S * NPAR:(h + 1) * S * NPAR], hT[:, h * P:(h + 1) * P],
                                              BD[:].rearrange("p s n -> p (s n)"), start=False, stop=(h == 1),
                                              skip_group_check=True)
                    mm.then_inc(par_ready, 1)

                def messages(kk):
                    pe.wait_ge(edges_done, kk + (XBUF - LAG + 1))
                    b = bass.ds(pe.snap((kk + (-LAG) % 4) % 4, min_val=0, max_val=3), 1)
                    for q in range(E4 * D // 512):
                        mm = nc.tensor.matmul(ps_m[:], g.ident[:], pm[:, b, q * 512:(q + 1) * 512].rearrange("p a e -> p (a e)"),
                                              start=False, stop=False, skip_group_check=True)
                    mm.then_inc(msg_done, 1)
                    now.step(close)

                def clear():
                    return nc.tensor.matmul(ps_m[:], zh[:, 0:P], zh[:], start=True, stop=False, skip_group_check=True)

                def close(t):
                    nc.tensor.matmul(ps_m[:], zh[:, 0:P], zh[:], start=False, stop=True,
                                     skip_group_check=True).then_inc(tile_sum, 1)
                    pe.wait_ge(tile_read, t + 1)
                    clear()

                pe.wait_ge(table_ready, 1)
                both = tuple(pq[:, h].rearrange("p s h -> p (s h)") for h in range(2))
                flat8 = tuple(own8[:, h].rearrange("p s h -> p (s h)") for h in range(2))
                for i in range(GROUPS):
                    pe.wait_ge(copied, i + 1)
                    params(i, both, both)
                k = counter(pe, "sheaf_pe")
                now = MessageTile(pe, "sheaf_pe")
                clear().then_inc(msg_done, 4)
                with pe.Fori(0, T) as t:
                    with pe.Fori(0, lists.count(pe, t)) as _j:
                        kk = pe.snap(k)
                        pe.wait_ge(copied, kk + (GROUPS + 1))
                        params(kk + GROUPS, (both[1], flat8[0]), (both[0], flat8[1]))
                        with pe.If(kk > LAG - 1):
                            messages(kk)
                        pe.reg_add(k, k, 1)
                with pe.Fori(0, LAG) as _j:
                    messages(pe.snap(k))
                    pe.reg_add(k, k, 1)

            @block.scalar
            def _(act):
                act.preload_act_table_set("natural_log_exp_and_others")
                for i in range(2):
                    act.wait_ge(w_turned, i + 1)
                    act.activation(PQ[0:D, i * HH:(i + 1) * HH], ps_a[i][0:D, 0:HH], ACT.Copy).then_inc(w_moved, 1)
                act.wait_ge(deg_ready, 1)
                root_inverse(act, dis[:], dis_ready)
                act.activation(coef[:], eps[:], ACT.Exp, scale=2.0).then_inc(dis_ready, 1)
                for ch, (t0, n) in enumerate(CHUNKS):
                    b = ch % 2
                    act.wait_ge(x_turned, ch + 1)
                    if ch >= 2:
                        act.wait_ge(rows_done, ch - 1)
                    act.activation(xt[b][:, 0:n * P], ps_a[b][0:D, 0:n * P], ACT.Copy).then_inc(x_copied, 1)
                    act.wait_ge(f_done, ch + 1)
                    act.activation(xft[b][0:D, 0:n * P], ps_a[b][0:D, 0:n * P], ACT.Copy).then_inc(f_copied, 1)

                def relu(i):
                    act.wait_ge(hid_ready, i + 1)
                    act.activation(hT[:], ps_h[:, 0:2 * P], ACT.Relu).then_inc(relu_ready, 1)

                def columns(i, step, blk):
                    act.wait_ge(par_ready, i + 1)
                    to = Z[:, step, blk].rearrange("p u y s q v k -> p u (y s) (q v k)")
                    act.activation(to[:, :, :, 1:4], par[:, :, :, 0:3], ACT.Copy)
                    act.activation(to[:, :, :, 6:8], par[:, :, :, 4:6], ACT.Copy)
                    act.activation(to[:, :, :, 10:14:3], par[:, :, :, 3:5], ACT.Copy, scale=-1.0).then_inc(col_ready, 1)

                def roots(blocks, step):
                    act.wait_ge(nn_ready, blocks)
                    to = nn[:, step].rearrange("p a m v -> p (a m v)")
                    act.activation(to, to, ACT.Ln)
                    act.drain()
                    act.activation(to, to, ACT.Exp, scale=-0.5).then_inc(rs_ready, 2)

                act.wait_ge(table_ready, 1)
                for i in range(GROUPS):
                    at0 = 2 * (i // 2 % 2)
                    act.activation(pq[:], own[:, i * S:(i + 1) * S, D:D + 2 * HH].rearrange("p s (c h) -> p c s h", c=2),
                                   ACT.Copy).then_inc(copied, 1)
                    relu(i)
                    columns(i, slice(at0, at0 + 2), slice(i % 2, i % 2 + 1))
                    if i % 2:
                        roots(i + 1, slice(at0, at0 + 2))
                k = counter(act, "sheaf_act")
                at = Lists.Place(act, "sheaf_act")
                now = MessageTile(act, "sheaf_act")

                def read_sums(t):
                    act.wait_ge(tile_sum, t + 1)
                    act.activation(sums[:, bass.ds(t, 1), :].rearrange("p a e -> p (a e)"), ps_m[:], ACT.Copy).then_inc(tile_read, 1)

                def edge_block(first, part):
                    kk = act.snap(k)
                    odd = act.snap(kk % 2, min_val=0, max_val=1)
                    step = bass.ds(act.snap(kk % 4 // 2 * 2, min_val=0, max_val=2), 2)
                    xb = bass.ds(act.snap(kk % XBUF, min_val=0, max_val=XBUF - 1), 1)
                    act.wait_ge(edges_done, kk + 1)
                    for h in range(2):
                        if part is lists.body:
                            lists.wait_body(act, at, h)
                        else:
                            lists.wait_last(act, at, h)
                        slots = slice(h * HS, (h + 1) * HS)
                        rows = part.rows[:, slots, :]
                        act.activation(pq[:, :, slots, :], rows[:, :, D:D + 2 * HH].rearrange("p s (c h) -> p c s h", c=2),
                                       ACT.Copy)
                        act.activation(xj[:, xb, slots, :].rearrange("p a s f -> p (a s) f"), rows[:, :, 0:D],
                                       ACT.Copy).then_inc(part.free[h], 1)
                    act.drain()
                    act.sem_inc(copied, 1)
                    if not first:
                        with act.If(kk > LAG):
                            now.step(read_sums)
                    relu(kk + GROUPS)
                    if not first:
                        with act.If(odd < 1):
                            roots(kk + GROUPS, bass.ds(act.snap((kk + 2) % 4 // 2 * 2, min_val=0, max_val=2), 2))
                    act.wait_ge(col_read, kk + 1)
                    columns(kk + GROUPS, step, bass.ds(odd, 1))
                    act.reg_add(k, k, 1)

                def tile(t, first):
                    n = lists.count(act, t)
                    act.activation(own8[:], bc(own[:, bass.ds(t, 1), D:D + 2 * HH].rearrange("p a (c h) -> p (a c) h", c=2), 2, S),
                                   ACT.Copy)
                    edge_block(first, lists.body)
                    act.reg_add(at.body, at.body, 1)
                    with act.Fori(2, n) as _j:
                        edge_block(False, lists.body)
                        act.reg_add(at.body, at.body, 1)
                    lists.enter_last(act, at, t)
                    edge_block(False, lists.last)

                tile(0, True)
                with act.Fori(1, T) as t:
                    tile(t, False)
                act.drain()
                act.sem_inc(copied, 1)
                act.sem_inc(col_ready, 1)
                kk = act.snap(k)
                kk = act.snap(kk + kk % 2)
                roots(kk + GROUPS, bass.ds(act.snap((kk + 2) % 4 // 2 * 2, min_val=0, max_val=2), 2))
                with act.Fori(0, LAG + 1) as _j:
                    now.step(read_sums)
                act.wait_ge(e_in, 1)
                act.activation(el[:], el[:], ACT.Exp).then_inc(e_out, 1)
                act.wait_ge(g.norm_var, 4)
                root_inverse(act, var[:], g.norm_root)

            @block.vector
            def _(v):
                def tt(to, a, b, op):
                    return v.tensor_tensor(to, a, b, op)

                v.memset(zrow[:], 0.0).then_inc(z_set, 1)
                v.memset(zh[:], 0.0)
                v.memset(xj[:], 0.0)
                v.memset(one[:], 1.0)
                v.memset(xft[0][D:D + 1, :], 1.0)
                v.memset(xft[1][D:D + 1, :], 1.0)
                v.memset(own[:, T:OT, :], 0.0)
                v.memset(Z[:], 0.0)
                v.drain()
                for i in (0, 5, 11, 14):
                    v.memset(Z[:].rearrange("p a y s q v k -> p (a y s) (q v k)")[:, :, i], 1.0)
                v.tensor_scalar(dis[:], sdego[:], 1.0, None, ALU.add).then_inc(deg_ready, 1)
                v.wait_ge(loaded, 16 * LOADS)
                for i, o in enumerate(ORDER):
                    v.tensor_copy(w1r[:, i:i + 1], w1n[:, o:o + 1])
                    v.tensor_copy(m1[:, :, i, :], m1n[:, :, o, :])
                v.wait_ge(same_set, 1)
                for i, o in enumerate(PORDER):
                    v.tensor_scalar(BD[:, :, i], same[:], m2n[:, o:o + 1], None, ALU.mult)
                    v.tensor_copy(mb2[:, :, i], mb2n[:, o:o + 1].broadcast_to([1, S2]))
                v.drain()
                tt(K[:].rearrange("p (k f) -> p k f", k=DD), bc(w1r[:], 2, HH), bc(w2r[:], 1, DD), ALU.mult).then_inc(ordered, 1)
                v.wait_ge(dis_ready, 2)
                v.tensor_scalar(coef[:], coef[:], 1.0, None, ALU.add)
                v.drain()
                v.reciprocal(coef[:], coef[:])
                v.drain()
                v.tensor_scalar(coef[:], coef[:], -2.0, 3.0, ALU.mult, ALU.add)
                for ch, (t0, n) in enumerate(CHUNKS):
                    v.wait_ge(rows_done, ch + 1)
                    frm = ps_b[ch % 2][:, 0:n * P].rearrange("p (t f) -> p t f", f=P)
                    tt(own[:, t0:t0 + n, 0:D], frm[:, :, 0:D], bc(dis[:, t0:t0 + n], 2, D), ALU.mult)
                    v.tensor_copy(own[:, t0:t0 + n, D:TW], frm[:, :, D:TW]).then_inc(rows_read, 1)
                v.drain()
                v.nop().then_inc(table_ready, 1)

                def pairs(blocks, b):
                    z = Z[:, b].rearrange("p a y s q v k -> p (a y s q) v k")
                    z8 = Z[:, b].rearrange("p a y s q v k -> p (a y s) (q v k)")
                    w = Wv[:, b].rearrange("p a m k -> p (a m) k")
                    norm = nn[:, b].rearrange("p a m v -> p (a m) v")
                    v.wait_ge(col_ready, blocks)
                    tt(by5[:, :, 0], z8[:, :, 10], z8[:, :, 13], ALU.mult)
                    tt(by5[:, :, 1], z8[:, :, 10], z8[:, :, 2], ALU.mult)
                    v.drain()
                    tt(z8[:, :, 9], by5[:, :, 0], z8[:, :, 7], ALU.subtract)
                    tt(by5[:, :, 1], by5[:, :, 1], z8[:, :, 3], ALU.add)
                    v.drain()
                    tt(by0[:], z8[:, :, 9:14:4], z8[:, :, 1:2].broadcast_to([P, M, 2]), ALU.mult)
                    v.drain()
                    v.scalar_tensor_tensor(z8[:, :, 8], by0[:, :, 0], -1.0, by5[:, :, 1], ALU.mult, ALU.subtract)
                    v.scalar_tensor_tensor(z8[:, :, 12], by0[:, :, 1], -1.0, z8[:, :, 2], ALU.mult, ALU.subtract)
                    v.drain()
                    tt(pr[:], z, bc(z[:, :, 0, :], 2, 2), ALU.mult)
                    v.drain()
                    v.tensor_reduce(norm, pr[:], AX, ALU.add)
                    v.drain()
                    v.reciprocal(inv[:], norm[:, :, 0])
                    v.drain()
                    tt(cc[:], norm[:, :, 1], inv[:], ALU.mult)
                    v.drain()
                    tt(pr[:, :, 0, :], bc(cc[:], 2, DD), z[:, :, 0, :], ALU.mult)
                    v.drain()
                    tt(w, z[:, :, 1, :], pr[:, :, 0, :], ALU.subtract)
                    v.drain()
                    tt(pr[:, :, 1, :], w, w, ALU.mult)
                    v.drain()
                    v.tensor_reduce(norm[:, :, 1], pr[:, :, 1, :], AX, ALU.add).then_inc(nn_ready, 2)

                def edge_maps(blocks, b):
                    z = Z[:, b].rearrange("p a y s q v k -> p (a y s q) v k")
                    w = Wv[:, b].rearrange("p a m k -> p (a m) k")
                    norm = nn[:, b].rearrange("p a m v -> p (a m) v")
                    v.wait_ge(rs_ready, blocks)
                    tt(U[:, :, 0, :], z[:, :, 0, :], bc(norm[:, :, 0], 2, DD), ALU.mult).then_inc(col_read, 2)
                    tt(U[:, :, 1, :], w, bc(norm[:, :, 1], 2, DD), ALU.mult)
                    v.drain()
                    for a in range(DD):
                        tt(mm4[:, a], bc(u4[:, 0:S2, a, :], 2, DD), u4[:, S2:M], ALU.mult)
                    v.drain()
                    v.tensor_reduce(maps[:].rearrange("p a s b -> p (a s b)"),
                                    mm4[:].rearrange("p a s b k -> p (a s b) k"), AX, ALU.add)
                    v.drain()

                u4 = U[:].rearrange("p (m q) v k -> p m (q v) k", q=2)

                pm4 = pm[:, 0:2].rearrange("p c (e b) -> p (c e) b", b=DD)
                for i in range(STEPS0):
                    b = slice(2 * (i % 2), 2 * (i % 2) + 2)
                    pairs(2 * i + 2, b)
                    edge_maps(2 * i + 2, b)
                    for s in range(S2):
                        x = own[:, i * S2 + s, 0:D].rearrange("p (b h) -> p h b", b=DD)
                        tt(pm4[:, s * D:(s + 1) * D, :].rearrange("p (a h) b -> p a h b", a=DD),
                           bc(maps[:, :, s, :], 2, HH), bc(x, 1, DD), ALU.mult)
                    v.drain()
                    v.tensor_reduce(agg[:, i * S2:(i + 1) * S2, :].rearrange("p s d -> p (s d)"), pm4, AX, ALU.add)
                    v.drain()
                v.sem_inc(edges_done, XBUF)

                def begin_step(j):
                    pairs(j * 2 + (GROUPS + 2), bass.ds(v.snap(j % 2 * 2, min_val=0, max_val=2), 2))

                def end_step(j):
                    two = bass.ds(v.snap(j % 2 * 2, min_val=0, max_val=2), 2)
                    x2 = bass.ds(v.snap(j % (XBUF // 2) * 2, min_val=0, max_val=XBUF - 2), 2)
                    edge_maps(j * 2 + (GROUPS + 2), two)
                    v.wait_ge(copied, j * 2 + (GROUPS + 2))
                    v.wait_ge(msg_done, j * 2 + 2)
                    tt(pm[:, two].rearrange("p c (e a h) -> p (c e) a h", e=E4, a=DD),
                       bc(maps[:].rearrange("p a s b -> p (s b) a"), 3, HH),
                       bc(xj[:, x2].rearrange("p a s (b h) -> p (a s b) h", b=DD), 2, DD),
                       ALU.mult).then_inc(edges_done, 2)

                steps = v.value_load(g.npair[0:1, 0:1], min_val=2, max_val=BLOCKS)
                done = v.alloc_register("sheaf_v_steps")
                v.reg_mov(done, 0)
                begin_step(v.snap(done))
                with v.Fori(1, steps) as j:
                    begin_step(v.snap(j))
                    end_step(v.snap(done))
                    v.reg_add(done, done, 1)
                end_step(v.snap(done))
                for t0, t1 in ((0, T - 3), (T - 3, T)):
                    v.wait_ge(tile_read, t1)
                    v.tensor_reduce(el[:, t0:t1, :], sums[:, t0:t1, :].rearrange("p t (e d) -> p t d e", d=D), AX, ALU.add)
                v.drain()
                tt(agg[:, 0:T, :], agg[:, 0:T, :], el[:], ALU.add)
                v.drain()
                a = agg[:, 0:T, :]
                tt(a, a, bc(dis[:], 2, D), ALU.mult)
                v.drain()
                v.tensor_scalar(el[:], a, 0.0, None, ALU.min).then_inc(e_in, 1)
                for d in range(DD):
                    at = slice(d * HH, (d + 1) * HH)
                    v.tensor_scalar(XS[:, :, at], XS[:, :, at], coef[:, d:d + 1], None, ALU.mult)
                v.drain()
                v.tensor_scalar(a, a, 0.0, -1.0, ALU.max, ALU.add)
                v.wait_ge(e_out, 1)
                v.drain()
                tt(a, a, el[:], ALU.add)
                v.drain()
                for i, o in enumerate(ORDER):
                    x = XS[:, :, o * HH:(o + 1) * HH]
                    tt(x, x, agg[:, 0:T, i * HH:(i + 1) * HH], ALU.subtract)
                v.drain()
                layernorm(v, XS[:], el[:], mean[:], var[:], g.norm_var)
                v.wait_ge(g.norm_root, 4)
                tt(XS[:], XS[:], bc(var[:], 2, D), ALU.mult).then_inc(final, 1)


def build(nc, ins, out):
    with ExitStack() as ctx:
        g = Program(nc, ctx, ins, out)
        with ExitStack() as c:
            A = g.sb("adjacency", [P, T, NP], F16, c)
            with ExitStack() as c_windows:
                g.windows(c_windows)
                stage_graph(g, A)
                stage_adjacency(g, A, c)
            X = g.sb("x", [P, T, D], F32, c)
            stage_appnp(g, A, X, c)
            stage_turn(g, A)
            stage_lightgcn(g, A, X)
        XS = g.sb("x_sorted", [P, T, D], F32)
        sdego = g.sb("dego_sorted", [P, T], F32)
        stage_sage(g, XS, sdego)
        stage_sheaf(g, XS, sdego)
        return g


def kernel(**inputs):
    import concourse.bacc as bacc
    from concourse.bass_utils import run_bass_kernel_spmd

    nc = bacc.Bacc("TRN2", target_bir_lowering=False, num_devices=1)
    arrays, aps = {}, {}
    for name, value in inputs.items():
        a = np.ascontiguousarray(value)
        arrays["in_" + name] = a
        aps[name] = nc.dram_tensor("in_" + name, a.shape, mybir.dt.from_np(a.dtype), kind="ExternalInput").ap()
    out = nc.dram_tensor("out", [N, D], F32, kind="ExternalOutput").ap()
    build(nc, aps, out)
    result = run_bass_kernel_spmd(nc, [arrays], core_ids=[0])
    return result.results[0]["out"]
```
